# Optimizing a Trainium2 kernel written in Bass

```python
import numpy as np
import jax
import jax.numpy as jnp

def _softmax(x, axis=-1):
    return jax.nn.softmax(x, axis=axis)

def _gelu(x):
    return jax.nn.gelu(x, approximate=True)

def _silu(x):
    return jax.nn.silu(x)

def _sigmoid(x):
    return jax.nn.sigmoid(x)

def _layernorm(x, axis=-1, eps=1e-05):
    m = jnp.mean(x, axis=axis, keepdims=True)
    v = jnp.var(x, axis=axis, keepdims=True)
    return (x - m) / jnp.sqrt(v + eps)

def _scatter_add(tgt, idx, src, axis=0):
    return tgt.at[idx].add(src)

def _segment_sum(src, seg, n):
    return jax.ops.segment_sum(src, seg, n)
kernel_name = 'mk_xattn_ffn_d4_seqx_r8_076374'

def setup_inputs(seed: int=0):
    np.random.seed(seed)
    _w = jnp.asarray

    def _rec_inputs():
        import jax
        import jax.numpy as jnp
        _rk = jax.random.key(seed)
        x = 7.22e-05 + 1 * jax.random.normal(jax.random.fold_in(_rk, 1), (4, 512, 128), jnp.float32)
        _lenS = 512 - jax.random.randint(jax.random.fold_in(_rk, 7), (4,), 0, max(1, 512 // 4) + 1, jnp.int32)
        _lenS2 = 32 - jax.random.randint(jax.random.fold_in(_rk, 8), (4,), 0, max(1, 32 // 4) + 1, jnp.int32)
        _ctx_1024P = jax.random.normal(jax.random.fold_in(_rk, 11), (4, 16, 128), jnp.float32)
        _ctx_1024c = jax.random.dirichlet(jax.random.fold_in(_rk, 511), 0.3 * jnp.ones((16,), jnp.float32), (4, 32))
        _ctx_1024t = jnp.einsum('bsk,bkd->bsd', _ctx_1024c, _ctx_1024P)
        _ctx_1024t = _ctx_1024t * jax.lax.rsqrt(jnp.mean(jnp.square(_ctx_1024t)) + 1e-12) * 0.953939
        ctx_1024 = 2.81802e-05 + 1.00001 * (_ctx_1024t + 0.3 * jax.random.normal(jax.random.fold_in(_rk, 611), (4, 32, 128), jnp.float32))
        _validS = jnp.arange(512)[None, :] < _lenS[:, None]
        _validS2 = jnp.arange(32)[None, :] < _lenS2[:, None]
        _causal = jnp.tril(jnp.ones((512, 512), dtype=bool))
        mask_BxSxS2_bf1 = jnp.ones((4, 512, 32), dtype=bool)
        mask_BxS2_bf1 = jnp.ones((4, 32), dtype=bool)
        mask_BxS2_ff1 = jnp.where(jnp.ones((4, 32), dtype=bool), 1.0, 0.0).astype(jnp.float32)
        return (x, ctx_1024, mask_BxSxS2_bf1, mask_BxS2_bf1, mask_BxS2_ff1)
    x, ctx_1024, mask_BxSxS2_bf1, mask_BxS2_bf1, mask_BxS2_ff1 = _rec_inputs()

    def _L0_xattn_setup():
        import jax, jax.numpy as jnp
        import numpy as np
        B, NT, NM, C, H, FF = (8, 128, 256, 128, 8, 512)

        def _ln(x, g, b):
            m = x.mean(-1, keepdims=True)
            v = jnp.mean((x - m) ** 2, axis=-1, keepdims=True)
            return (x - m) / jnp.sqrt(v + 1e-05) * g + b
        key = jax.random.key(seed)
        ks = jax.random.split(key, 8)
        w = lambda k, shape, s=0.02: jax.random.normal(k, shape, dtype=jnp.float32) * s
        return {'tgt': jax.random.normal(ks[0], (B, NT, C), dtype=jnp.float32), 'memory': jax.random.normal(ks[1], (B, NM, C), dtype=jnp.float32), 'qkv_w': w(ks[2], (3 * C, C)), 'qkv_b': jnp.zeros((3 * C,), jnp.float32), 'sa_out_w': w(ks[3], (C, C)), 'sa_out_b': jnp.zeros((C,), jnp.float32), 'in_proj_w': w(ks[4], (3 * C, C)), 'in_proj_b': jnp.zeros((3 * C,), jnp.float32), 'mha_out_w': w(ks[5], (C, C)), 'mha_out_b': jnp.zeros((C,), jnp.float32), 'lin1_w': w(ks[6], (FF, C)), 'lin1_b': jnp.zeros((FF,), jnp.float32), 'lin2_w': w(ks[7], (C, FF)), 'lin2_b': jnp.zeros((C,), jnp.float32), 'ln1_g': jnp.ones((C,), jnp.float32), 'ln1_b': jnp.zeros((C,), jnp.float32), 'ln2_g': jnp.ones((C,), jnp.float32), 'ln2_b': jnp.zeros((C,), jnp.float32), 'ln3_g': jnp.ones((C,), jnp.float32), 'ln3_b': jnp.zeros((C,), jnp.float32)}
    _L0_xattn_all = _L0_xattn_setup()
    _L0_xattn_in = {k: v for k, v in _L0_xattn_all.items() if k in ('qkv_w', 'qkv_b', 'sa_out_w', 'sa_out_b', 'in_proj_w', 'in_proj_b', 'mha_out_w', 'mha_out_b', 'lin1_w', 'lin1_b', 'lin2_w', 'lin2_b', 'ln1_g', 'ln1_b', 'ln2_g', 'ln2_b', 'ln3_g', 'ln3_b')}
    del _L0_xattn_all

    def _L0_ffn_setup():
        import jax, jax.numpy as jnp
        import numpy as np
        D_MODEL = 128
        EXPERT_DIM = 512
        N_EXPERTS = 8
        CAP_FACTOR = 0.5
        key = jax.random.key(seed)
        ks = jax.random.split(key, 7)
        inp = {'input': jax.random.normal(ks[0], (4, 512, D_MODEL), dtype=jnp.float32), 'w_switch': jax.random.normal(ks[1], (D_MODEL, N_EXPERTS), dtype=jnp.float32) * 0.02, 'b_switch': jnp.zeros((N_EXPERTS,), jnp.float32), 'w1': jax.random.normal(ks[2], (N_EXPERTS, D_MODEL, EXPERT_DIM), dtype=jnp.float32) * 0.02, 'b1': jnp.zeros((N_EXPERTS, EXPERT_DIM), jnp.float32), 'w2': jax.random.normal(ks[3], (N_EXPERTS, EXPERT_DIM, D_MODEL), dtype=jnp.float32) * 0.02, 'b2': jnp.zeros((N_EXPERTS, D_MODEL), jnp.float32)}
        return inp
    _L0_ffn_all = _L0_ffn_setup()
    _L0_ffn_in = {k: v for k, v in _L0_ffn_all.items() if k in ('w_switch', 'b_switch', 'w1', 'b1', 'w2', 'b2')}
    del _L0_ffn_all

    def _L1_xattn_setup():
        import jax, jax.numpy as jnp
        import numpy as np
        DIM = 128
        HEAD_DIM = 64
        NUM_HEADS = DIM // HEAD_DIM
        SCALE = HEAD_DIM ** (-0.5)
        key = jax.random.key(seed)
        k_x, k_ctx, k_wq, k_wkv, k_wo = jax.random.split(key, 5)
        B, N, M = (2, 256, 256)
        x = jax.random.normal(k_x, (B, N, DIM), dtype=jnp.float32)
        context = jax.random.normal(k_ctx, (B, M, DIM), dtype=jnp.float32)
        mask = jnp.ones((B, N, M), dtype=bool)
        s = DIM ** (-0.5)
        Wq = jax.random.normal(k_wq, (DIM, DIM), dtype=jnp.float32) * s
        Wkv = jax.random.normal(k_wkv, (DIM, 2 * DIM), dtype=jnp.float32) * s
        Wo = jax.random.normal(k_wo, (DIM, DIM), dtype=jnp.float32) * s
        return {'x': x, 'context': context, 'mask': mask, 'Wq': Wq, 'Wkv': Wkv, 'Wo': Wo}
    _L1_xattn_all = _L1_xattn_setup()
    _L1_xattn_in = {k: v for k, v in _L1_xattn_all.items() if k in ('Wq', 'Wkv', 'Wo')}
    del _L1_xattn_all

    def _L1_ffn_setup():
        import jax, jax.numpy as jnp
        import numpy as np
        B, L, D = (4, 256, 128)
        H = 16
        E = 16
        NS = 16
        S = NS // E
        F = 512
        EPS = 1e-05

        def _layernorm(x, g, b):
            mu = jnp.mean(x, axis=-1, keepdims=True)
            var = jnp.mean(jnp.square(x - mu), axis=-1, keepdims=True)
            return (x - mu) * jax.lax.rsqrt(var + EPS) * g + b

        def _mha(q, k, v, Wq, bq, Wk, bk, Wv, bv, Wo, bo):
            Bq, Lq, Dm = q.shape
            dh = Dm // H
            qh = (q @ Wq + bq).reshape(Bq, Lq, H, dh)
            kh = (k @ Wk + bk).reshape(Bq, -1, H, dh)
            vh = (v @ Wv + bv).reshape(Bq, -1, H, dh)
            scores = jnp.einsum('bqhd,bkhd->bhqk', qh, kh) / jnp.asarray(np.sqrt(dh), q.dtype)
            attn = jax.nn.softmax(scores, axis=-1)
            out = jnp.einsum('bhqk,bkhd->bqhd', attn, vh).reshape(Bq, Lq, Dm)
            return out @ Wo + bo
        key = jax.random.key(seed)
        ks = jax.random.split(key, 32)
        s = 0.02
        d = {}
        d['x'] = jax.random.normal(ks[0], (B, L, D), jnp.float32)
        d['slot_query'] = jax.random.normal(ks[1], (1, NS, D), jnp.float32) * 0.01
        for i, nm in enumerate(['d_Wq', 'd_Wk', 'd_Wv', 'd_Wo']):
            d[nm] = jax.random.normal(ks[2 + i], (D, D), jnp.float32) * s
        for nm in ['d_bq', 'd_bk', 'd_bv', 'd_bo']:
            d[nm] = jnp.zeros((D,), jnp.float32)
        for i, nm in enumerate(['c_Wq', 'c_Wk', 'c_Wv', 'c_Wo']):
            d[nm] = jax.random.normal(ks[6 + i], (D, D), jnp.float32) * s
        for nm in ['c_bq', 'c_bk', 'c_bv', 'c_bo']:
            d[nm] = jnp.zeros((D,), jnp.float32)
        d['e_ln_g'] = jnp.ones((E, D), jnp.float32)
        d['e_ln_b'] = jnp.zeros((E, D), jnp.float32)
        d['e_W1'] = jax.random.normal(ks[10], (E, D, F), jnp.float32) * s
        d['e_b1'] = jnp.zeros((E, F), jnp.float32)
        d['e_Wg'] = jax.random.normal(ks[11], (E, D, F), jnp.float32) * s
        d['e_bg'] = jnp.zeros((E, F), jnp.float32)
        d['e_W2'] = jax.random.normal(ks[12], (E, F, D), jnp.float32) * s
        d['e_b2'] = jnp.zeros((E, D), jnp.float32)
        return d
    _L1_ffn_all = _L1_ffn_setup()
    _L1_ffn_in = {k: v for k, v in _L1_ffn_all.items() if k in ('slot_query', 'd_Wq', 'd_Wk', 'd_Wv', 'd_Wo', 'd_bq', 'd_bk', 'd_bv', 'd_bo', 'c_Wq', 'c_Wk', 'c_Wv', 'c_Wo', 'c_bq', 'c_bk', 'c_bv', 'c_bo', 'e_ln_g', 'e_ln_b', 'e_W1', 'e_b1', 'e_Wg', 'e_bg', 'e_W2', 'e_b2')}
    del _L1_ffn_all

    def _L2_xattn_setup():
        import jax, jax.numpy as jnp
        import numpy as np
        PROJ_DIM = 64
        D_MODEL = 128
        key = jax.random.key(seed)
        ks = jax.random.split(key, 8)
        B, Q, K = (16, 256, 256)
        q = jax.random.normal(ks[0], (B, Q, D_MODEL), dtype=jnp.float32)
        k = jax.random.normal(ks[1], (B, K, D_MODEL), dtype=jnp.float32)
        v = jax.random.normal(ks[2], (B, K, D_MODEL), dtype=jnp.float32)
        mask = jnp.ones((B, K), dtype=bool)
        s = 1.0 / np.sqrt(D_MODEL)
        Wq = jax.random.normal(ks[3], (PROJ_DIM, D_MODEL), dtype=jnp.float32) * s
        Wk = jax.random.normal(ks[4], (PROJ_DIM, D_MODEL), dtype=jnp.float32) * s
        Wv = jax.random.normal(ks[5], (PROJ_DIM, D_MODEL), dtype=jnp.float32) * s
        Wout = jax.random.normal(ks[6], (D_MODEL, PROJ_DIM), dtype=jnp.float32) / np.sqrt(PROJ_DIM)
        return {'q': q, 'k': k, 'v': v, 'mask': mask, 'Wq': Wq, 'Wk': Wk, 'Wv': Wv, 'Wout': Wout}
    _L2_xattn_all = _L2_xattn_setup()
    _L2_xattn_in = {k: v for k, v in _L2_xattn_all.items() if k in ('Wq', 'Wk', 'Wv', 'Wout')}
    del _L2_xattn_all

    def _L2_ffn_setup():
        import jax, jax.numpy as jnp
        import numpy as np
        N_EXP = 8
        TOP_K = 2
        CAP_FACTOR = 1.25
        NEG_INF = -1000000000.0

        def _moe_forward(x, w_g, c_fc, c_proj):
            B, T, D = x.shape
            N = B * T
            xf = x.reshape(N, D)
            logits = xf @ w_g
            topv, topi = jax.lax.top_k(logits, TOP_K)
            full = jnp.full_like(logits, NEG_INF)
            full = full.at[jnp.arange(N)[:, None], topi].set(topv)
            probs = jax.nn.softmax(full, axis=-1)
            capacity = int(TOP_K * CAP_FACTOR * N / N_EXP)
            capacity += capacity % 2
            mask = jax.nn.one_hot(jnp.swapaxes(topi, 0, 1), N_EXP, dtype=jnp.int32)
            rank = jnp.cumsum(mask.reshape(TOP_K * N, N_EXP), axis=0).reshape(TOP_K, N, N_EXP) - 1
            mask = mask * (rank < capacity)
            rank_sel = jnp.sum(mask * rank, axis=-1)
            wts = jnp.sum(mask * probs[None], axis=-1)
            cb = jnp.zeros((N, N_EXP, capacity), x.dtype)
            tok = jnp.arange(N)
            for k in range(TOP_K):
                cb = cb.at[tok, topi[:, k], rank_sel[k]].add(wts[k])
            sec_mask = (cb != 0).astype(x.dtype)
            exp_batches = jnp.einsum('nec,nd->ecd', sec_mask, xf)
            h = jax.nn.gelu(jnp.einsum('ecd,edh->ech', exp_batches, c_fc), approximate=False)
            exp_out = jnp.einsum('ech,ehd->ecd', h, c_proj)
            out = jnp.einsum('nec,ecd->nd', cb, exp_out)
            return out.reshape(B, T, D)
        key = jax.random.key(seed)
        k1, k2, k3, k4 = jax.random.split(key, 4)
        B, T, D = (4, 64, 128)
        H = 4 * D
        x = jax.random.normal(k1, (B, T, D), jnp.float32)
        w_g = jax.random.normal(k2, (D, N_EXP), jnp.float32) * 0.02
        c_fc = jax.random.normal(k3, (N_EXP, D, H), jnp.float32) * 0.02
        c_proj = jax.random.normal(k4, (N_EXP, H, D), jnp.float32) * 0.02
        return {'x': x, 'w_g': w_g, 'c_fc': c_fc, 'c_proj': c_proj}
    _L2_ffn_all = _L2_ffn_setup()
    _L2_ffn_in = {k: v for k, v in _L2_ffn_all.items() if k in ('w_g', 'c_fc', 'c_proj')}
    del _L2_ffn_all

    def _L3_xattn_setup():
        import jax, jax.numpy as jnp
        import numpy as np
        NUM_HEADS = 16
        D_MODEL = 128
        D_K = D_MODEL // NUM_HEADS
        B, S = (2, 256)
        key = jax.random.key(seed)
        ks = jax.random.split(key, 8)
        scale = 1.0 / np.sqrt(D_MODEL)
        return {'x': jax.random.normal(ks[0], (B, S, D_MODEL), jnp.float32), 'y': jax.random.normal(ks[1], (B, S, D_MODEL), jnp.float32), 'mask': jnp.ones((B, S), jnp.float32), 'wq': jax.random.normal(ks[2], (D_MODEL, D_MODEL), jnp.float32) * scale, 'bq': jnp.zeros((D_MODEL,), jnp.float32), 'wk': jax.random.normal(ks[3], (D_MODEL, D_MODEL), jnp.float32) * scale, 'bk': jnp.zeros((D_MODEL,), jnp.float32), 'wv': jax.random.normal(ks[4], (D_MODEL, D_MODEL), jnp.float32) * scale, 'bv': jnp.zeros((D_MODEL,), jnp.float32), 'wo': jax.random.normal(ks[5], (D_MODEL, D_MODEL), jnp.float32) * scale, 'bo': jnp.zeros((D_MODEL,), jnp.float32)}
    _L3_xattn_all = _L3_xattn_setup()
    _L3_xattn_in = {k: v for k, v in _L3_xattn_all.items() if k in ('wq', 'bq', 'wk', 'bk', 'wv', 'bv', 'wo', 'bo')}
    del _L3_xattn_all

    def _L3_ffn_setup():
        import jax, jax.numpy as jnp
        import numpy as np
        TOP_K = 2
        key = jax.random.key(seed)
        ks = jax.random.split(key, 4)
        B, S, D, F, E = (4, 512, 128, 256, 8)
        x = jax.random.normal(ks[0], (B, S, D), dtype=jnp.float32)
        router_w = jax.random.normal(ks[1], (E, D), dtype=jnp.float32) * 0.03
        w1 = jax.random.normal(ks[2], (E, D, F), dtype=jnp.float32) * 0.02
        b1 = jnp.zeros((E, F), dtype=jnp.float32)
        w2 = jax.random.normal(ks[3], (E, F, D), dtype=jnp.float32) * 0.02
        b2 = jnp.zeros((E, D), dtype=jnp.float32)
        return {'x': x, 'router_w': router_w, 'w1': w1, 'b1': b1, 'w2': w2, 'b2': b2}
    _L3_ffn_all = _L3_ffn_setup()
    _L3_ffn_in = {k: v for k, v in _L3_ffn_all.items() if k in ('router_w', 'w1', 'b1', 'w2', 'b2')}
    del _L3_ffn_all
    return {'x': x, 'ctx_1024': ctx_1024, 'mask_BxSxS2_bf1': mask_BxSxS2_bf1, 'mask_BxS2_bf1': mask_BxS2_bf1, 'mask_BxS2_ff1': mask_BxS2_ff1, 'L0_xattn_qkv_w': _L0_xattn_in['qkv_w'], 'L0_xattn_qkv_b': _L0_xattn_in['qkv_b'], 'L0_xattn_sa_out_w': _L0_xattn_in['sa_out_w'], 'L0_xattn_sa_out_b': _L0_xattn_in['sa_out_b'], 'L0_xattn_in_proj_w': _L0_xattn_in['in_proj_w'], 'L0_xattn_in_proj_b': _L0_xattn_in['in_proj_b'], 'L0_xattn_mha_out_w': _L0_xattn_in['mha_out_w'], 'L0_xattn_mha_out_b': _L0_xattn_in['mha_out_b'], 'L0_xattn_lin1_w': _L0_xattn_in['lin1_w'], 'L0_xattn_lin1_b': _L0_xattn_in['lin1_b'], 'L0_xattn_lin2_w': _L0_xattn_in['lin2_w'], 'L0_xattn_lin2_b': _L0_xattn_in['lin2_b'], 'L0_xattn_ln1_g': _L0_xattn_in['ln1_g'], 'L0_xattn_ln1_b': _L0_xattn_in['ln1_b'], 'L0_xattn_ln2_g': _L0_xattn_in['ln2_g'], 'L0_xattn_ln2_b': _L0_xattn_in['ln2_b'], 'L0_xattn_ln3_g': _L0_xattn_in['ln3_g'], 'L0_xattn_ln3_b': _L0_xattn_in['ln3_b'], 'L0_ffn_w_switch': _L0_ffn_in['w_switch'], 'L0_ffn_b_switch': _L0_ffn_in['b_switch'], 'L0_ffn_w1': _L0_ffn_in['w1'], 'L0_ffn_b1': _L0_ffn_in['b1'], 'L0_ffn_w2': _L0_ffn_in['w2'], 'L0_ffn_b2': _L0_ffn_in['b2'], 'L1_xattn_Wq': _L1_xattn_in['Wq'], 'L1_xattn_Wkv': _L1_xattn_in['Wkv'], 'L1_xattn_Wo': _L1_xattn_in['Wo'], 'L1_ffn_slot_query': _L1_ffn_in['slot_query'], 'L1_ffn_d_Wq': _L1_ffn_in['d_Wq'], 'L1_ffn_d_Wk': _L1_ffn_in['d_Wk'], 'L1_ffn_d_Wv': _L1_ffn_in['d_Wv'], 'L1_ffn_d_Wo': _L1_ffn_in['d_Wo'], 'L1_ffn_d_bq': _L1_ffn_in['d_bq'], 'L1_ffn_d_bk': _L1_ffn_in['d_bk'], 'L1_ffn_d_bv': _L1_ffn_in['d_bv'], 'L1_ffn_d_bo': _L1_ffn_in['d_bo'], 'L1_ffn_c_Wq': _L1_ffn_in['c_Wq'], 'L1_ffn_c_Wk': _L1_ffn_in['c_Wk'], 'L1_ffn_c_Wv': _L1_ffn_in['c_Wv'], 'L1_ffn_c_Wo': _L1_ffn_in['c_Wo'], 'L1_ffn_c_bq': _L1_ffn_in['c_bq'], 'L1_ffn_c_bk': _L1_ffn_in['c_bk'], 'L1_ffn_c_bv': _L1_ffn_in['c_bv'], 'L1_ffn_c_bo': _L1_ffn_in['c_bo'], 'L1_ffn_e_ln_g': _L1_ffn_in['e_ln_g'], 'L1_ffn_e_ln_b': _L1_ffn_in['e_ln_b'], 'L1_ffn_e_W1': _L1_ffn_in['e_W1'], 'L1_ffn_e_b1': _L1_ffn_in['e_b1'], 'L1_ffn_e_Wg': _L1_ffn_in['e_Wg'], 'L1_ffn_e_bg': _L1_ffn_in['e_bg'], 'L1_ffn_e_W2': _L1_ffn_in['e_W2'], 'L1_ffn_e_b2': _L1_ffn_in['e_b2'], 'L2_xattn_Wq': _L2_xattn_in['Wq'], 'L2_xattn_Wk': _L2_xattn_in['Wk'], 'L2_xattn_Wv': _L2_xattn_in['Wv'], 'L2_xattn_Wout': _L2_xattn_in['Wout'], 'L2_ffn_w_g': _L2_ffn_in['w_g'], 'L2_ffn_c_fc': _L2_ffn_in['c_fc'], 'L2_ffn_c_proj': _L2_ffn_in['c_proj'], 'L3_xattn_wq': _L3_xattn_in['wq'], 'L3_xattn_bq': _L3_xattn_in['bq'], 'L3_xattn_wk': _L3_xattn_in['wk'], 'L3_xattn_bk': _L3_xattn_in['bk'], 'L3_xattn_wv': _L3_xattn_in['wv'], 'L3_xattn_bv': _L3_xattn_in['bv'], 'L3_xattn_wo': _L3_xattn_in['wo'], 'L3_xattn_bo': _L3_xattn_in['bo'], 'L3_ffn_router_w': _L3_ffn_in['router_w'], 'L3_ffn_w1': _L3_ffn_in['w1'], 'L3_ffn_b1': _L3_ffn_in['b1'], 'L3_ffn_w2': _L3_ffn_in['w2'], 'L3_ffn_b2': _L3_ffn_in['b2']}

def reference(x, ctx_1024, mask_BxSxS2_bf1, mask_BxS2_bf1, mask_BxS2_ff1, L0_xattn_qkv_w, L0_xattn_qkv_b, L0_xattn_sa_out_w, L0_xattn_sa_out_b, L0_xattn_in_proj_w, L0_xattn_in_proj_b, L0_xattn_mha_out_w, L0_xattn_mha_out_b, L0_xattn_lin1_w, L0_xattn_lin1_b, L0_xattn_lin2_w, L0_xattn_lin2_b, L0_xattn_ln1_g, L0_xattn_ln1_b, L0_xattn_ln2_g, L0_xattn_ln2_b, L0_xattn_ln3_g, L0_xattn_ln3_b, L0_ffn_w_switch, L0_ffn_b_switch, L0_ffn_w1, L0_ffn_b1, L0_ffn_w2, L0_ffn_b2, L1_xattn_Wq, L1_xattn_Wkv, L1_xattn_Wo, L1_ffn_slot_query, L1_ffn_d_Wq, L1_ffn_d_Wk, L1_ffn_d_Wv, L1_ffn_d_Wo, L1_ffn_d_bq, L1_ffn_d_bk, L1_ffn_d_bv, L1_ffn_d_bo, L1_ffn_c_Wq, L1_ffn_c_Wk, L1_ffn_c_Wv, L1_ffn_c_Wo, L1_ffn_c_bq, L1_ffn_c_bk, L1_ffn_c_bv, L1_ffn_c_bo, L1_ffn_e_ln_g, L1_ffn_e_ln_b, L1_ffn_e_W1, L1_ffn_e_b1, L1_ffn_e_Wg, L1_ffn_e_bg, L1_ffn_e_W2, L1_ffn_e_b2, L2_xattn_Wq, L2_xattn_Wk, L2_xattn_Wv, L2_xattn_Wout, L2_ffn_w_g, L2_ffn_c_fc, L2_ffn_c_proj, L3_xattn_wq, L3_xattn_bq, L3_xattn_wk, L3_xattn_bk, L3_xattn_wv, L3_xattn_bv, L3_xattn_wo, L3_xattn_bo, L3_ffn_router_w, L3_ffn_w1, L3_ffn_b1, L3_ffn_w2, L3_ffn_b2):
    import jax
    import jax.numpy as jnp

    def _L0_xattn_ref(tgt, memory, qkv_w, qkv_b, sa_out_w, sa_out_b, in_proj_w, in_proj_b, mha_out_w, mha_out_b, lin1_w, lin1_b, lin2_w, lin2_b, ln1_g, ln1_b, ln2_g, ln2_b, ln3_g, ln3_b):
        import jax, jax.numpy as jnp
        import numpy as np
        B, NT, NM, C, H, FF = (8, 128, 256, 128, 8, 512)

        def _ln(x, g, b):
            m = x.mean(-1, keepdims=True)
            v = jnp.mean((x - m) ** 2, axis=-1, keepdims=True)
            return (x - m) / jnp.sqrt(v + 1e-05) * g + b
        Bx, N, Cx = tgt.shape
        qkv = tgt @ qkv_w.T + qkv_b
        q, k, v = jnp.split(qkv, 3, axis=-1)
        scores = jnp.einsum('bnc,bmc->bnm', q, k) * jnp.sqrt(jnp.float32(Cx))
        diag = jnp.eye(N, dtype=bool)
        scores = jnp.where(diag[None, :, :], scores, -jnp.inf)
        attn = jax.nn.softmax(scores, axis=-1)
        sa = jnp.einsum('bnm,bmc->bnc', attn, v) @ sa_out_w.T + sa_out_b
        x = _ln(tgt + sa, ln1_g, ln1_b)
        d = Cx // H
        wq, wk, wv = jnp.split(in_proj_w, 3, axis=0)
        bq, bk, bv = jnp.split(in_proj_b, 3, axis=0)
        qh = (x @ wq.T + bq).reshape(Bx, N, H, d).transpose(0, 2, 1, 3)
        kh = (memory @ wk.T + bk).reshape(Bx, -1, H, d).transpose(0, 2, 1, 3)
        vh = (memory @ wv.T + bv).reshape(Bx, -1, H, d).transpose(0, 2, 1, 3)
        a = jax.nn.softmax(jnp.einsum('bhnd,bhmd->bhnm', qh, kh) / jnp.sqrt(jnp.float32(d)), axis=-1)
        ca = jnp.einsum('bhnm,bhmd->bhnd', a, vh).transpose(0, 2, 1, 3).reshape(Bx, N, Cx)
        ca = ca @ mha_out_w.T + mha_out_b
        x = _ln(x + ca, ln2_g, ln2_b)
        ff = jax.nn.relu(x @ lin1_w.T + lin1_b) @ lin2_w.T + lin2_b
        return _ln(x + ff, ln3_g, ln3_b)

    def _L0_ffn_ref(input, w_switch, b_switch, w1, b1, w2, b2):
        import jax, jax.numpy as jnp
        import numpy as np
        D_MODEL = 128
        EXPERT_DIM = 512
        N_EXPERTS = 8
        CAP_FACTOR = 0.5
        B, S, D = input.shape
        T = B * S
        E = b_switch.shape[0]
        capacity = int(CAP_FACTOR * T / E)
        x = input.reshape(T, D)
        logits = x @ w_switch + b_switch
        probs = jax.nn.softmax(logits, axis=-1)
        pmax = probs.max(axis=-1)
        routes = probs.argmax(axis=-1)
        oh = (routes[:, None] == jnp.arange(E)[None, :]).astype(jnp.int32)
        pos = (jnp.cumsum(oh, axis=0) * oh).sum(-1) - 1
        keep = pos < capacity
        slot = jnp.where(keep, routes * capacity + pos, E * capacity)
        buf = jnp.zeros((E * capacity + 1, D), x.dtype).at[slot].set(x)
        buf_e = buf[:E * capacity].reshape(E, capacity, D)
        h = jax.nn.relu(jnp.einsum('ecd,edh->ech', buf_e, w1) + b1[:, None, :])
        y = jnp.einsum('ech,ehd->ecd', h, w2) + b2[:, None, :]
        y_flat = jnp.concatenate([y.reshape(E * capacity, D), jnp.zeros((1, D), x.dtype)], axis=0)
        out = jnp.where(keep[:, None], y_flat[slot], x)
        scale = pmax / jax.lax.stop_gradient(pmax)
        out = out * scale[:, None]
        return out.reshape(B, S, D)

    def _L1_xattn_ref(x, context, mask, Wq, Wkv, Wo):
        import jax, jax.numpy as jnp
        import numpy as np
        DIM = 128
        HEAD_DIM = 64
        NUM_HEADS = DIM // HEAD_DIM
        SCALE = HEAD_DIM ** (-0.5)
        B, N, C = x.shape
        M = context.shape[1]
        H, D = (NUM_HEADS, HEAD_DIM)
        q = (x @ Wq).reshape(B, N, H, D).transpose(0, 2, 1, 3)
        kv = (context @ Wkv).reshape(B, M, 2, H, D).transpose(2, 0, 3, 1, 4)
        k, v = (kv[0], kv[1])
        attn = jnp.einsum('bhnd,bhmd->bhnm', q, k) * SCALE
        attn = jnp.where(mask[:, None, :, :], attn, -jnp.inf)
        attn = jax.nn.softmax(attn, axis=-1)
        out = jnp.einsum('bhnm,bhmd->bhnd', attn, v)
        out = out.transpose(0, 2, 1, 3).reshape(B, N, C)
        return out @ Wo

    def _L1_ffn_ref(x, slot_query, d_Wq, d_Wk, d_Wv, d_Wo, d_bq, d_bk, d_bv, d_bo, c_Wq, c_Wk, c_Wv, c_Wo, c_bq, c_bk, c_bv, c_bo, e_ln_g, e_ln_b, e_W1, e_b1, e_Wg, e_bg, e_W2, e_b2):
        import jax, jax.numpy as jnp
        import numpy as np
        B, L, D = (4, 256, 128)
        H = 16
        E = 16
        NS = 16
        S = NS // E
        F = 512
        EPS = 1e-05

        def _layernorm(x, g, b):
            mu = jnp.mean(x, axis=-1, keepdims=True)
            var = jnp.mean(jnp.square(x - mu), axis=-1, keepdims=True)
            return (x - mu) * jax.lax.rsqrt(var + EPS) * g + b

        def _mha(q, k, v, Wq, bq, Wk, bk, Wv, bv, Wo, bo):
            Bq, Lq, Dm = q.shape
            dh = Dm // H
            qh = (q @ Wq + bq).reshape(Bq, Lq, H, dh)
            kh = (k @ Wk + bk).reshape(Bq, -1, H, dh)
            vh = (v @ Wv + bv).reshape(Bq, -1, H, dh)
            scores = jnp.einsum('bqhd,bkhd->bhqk', qh, kh) / jnp.asarray(np.sqrt(dh), q.dtype)
            attn = jax.nn.softmax(scores, axis=-1)
            out = jnp.einsum('bhqk,bkhd->bqhd', attn, vh).reshape(Bq, Lq, Dm)
            return out @ Wo + bo
        Bx = x.shape[0]
        q = jnp.broadcast_to(slot_query, (Bx, NS, D))
        o = q + _mha(q, x, x, d_Wq, d_bq, d_Wk, d_bk, d_Wv, d_bv, d_Wo, d_bo)
        os = o.reshape(Bx, E, S, D)
        h = _layernorm(os, e_ln_g[None, :, None, :], e_ln_b[None, :, None, :])
        u = jax.nn.silu(jnp.einsum('besd,edf->besf', h, e_W1) + e_b1[None, :, None, :])
        g = jax.nn.silu(jnp.einsum('besd,edf->besf', h, e_Wg) + e_bg[None, :, None, :])
        y = jnp.einsum('besf,efd->besd', u * g, e_W2) + e_b2[None, :, None, :]
        o = o + y.reshape(Bx, NS, D)
        out = _mha(x, o, o, c_Wq, c_bq, c_Wk, c_bk, c_Wv, c_bv, c_Wo, c_bo)
        return out

    def _L2_xattn_ref(q, k, v, mask, Wq, Wk, Wv, Wout):
        import jax, jax.numpy as jnp
        import numpy as np
        PROJ_DIM = 64
        D_MODEL = 128
        qp = jnp.einsum('bqd,pd->bqp', q, Wq)
        kp = jnp.einsum('bkd,pd->bkp', k, Wk)
        vp = jnp.einsum('bkd,pd->bkp', v, Wv)
        scale = 1.0 / jnp.sqrt(jnp.asarray(PROJ_DIM, dtype=qp.dtype))
        scores = jnp.einsum('bqp,bkp->bqk', qp, kp) * scale
        neg_inf = jnp.asarray(-jnp.inf, dtype=scores.dtype)
        scores = jnp.where(mask[:, None, :], scores, neg_inf)
        probs = jax.nn.softmax(scores, axis=-1)
        attended = jnp.einsum('bqk,bkp->bqp', probs, vp)
        out = jnp.einsum('bqp,dp->bqd', attended, Wout)
        return out

    def _L2_ffn_ref(x, w_g, c_fc, c_proj):
        import jax, jax.numpy as jnp
        import numpy as np
        N_EXP = 8
        TOP_K = 2
        CAP_FACTOR = 1.25
        NEG_INF = -1000000000.0

        def _moe_forward(x, w_g, c_fc, c_proj):
            B, T, D = x.shape
            N = B * T
            xf = x.reshape(N, D)
            logits = xf @ w_g
            topv, topi = jax.lax.top_k(logits, TOP_K)
            full = jnp.full_like(logits, NEG_INF)
            full = full.at[jnp.arange(N)[:, None], topi].set(topv)
            probs = jax.nn.softmax(full, axis=-1)
            capacity = int(TOP_K * CAP_FACTOR * N / N_EXP)
            capacity += capacity % 2
            mask = jax.nn.one_hot(jnp.swapaxes(topi, 0, 1), N_EXP, dtype=jnp.int32)
            rank = jnp.cumsum(mask.reshape(TOP_K * N, N_EXP), axis=0).reshape(TOP_K, N, N_EXP) - 1
            mask = mask * (rank < capacity)
            rank_sel = jnp.sum(mask * rank, axis=-1)
            wts = jnp.sum(mask * probs[None], axis=-1)
            cb = jnp.zeros((N, N_EXP, capacity), x.dtype)
            tok = jnp.arange(N)
            for k in range(TOP_K):
                cb = cb.at[tok, topi[:, k], rank_sel[k]].add(wts[k])
            sec_mask = (cb != 0).astype(x.dtype)
            exp_batches = jnp.einsum('nec,nd->ecd', sec_mask, xf)
            h = jax.nn.gelu(jnp.einsum('ecd,edh->ech', exp_batches, c_fc), approximate=False)
            exp_out = jnp.einsum('ech,ehd->ecd', h, c_proj)
            out = jnp.einsum('nec,ecd->nd', cb, exp_out)
            return out.reshape(B, T, D)
        return _moe_forward(x, w_g, c_fc, c_proj)

    def _L3_xattn_ref(x, y, mask, wq, bq, wk, bk, wv, bv, wo, bo):
        import jax, jax.numpy as jnp
        import numpy as np
        NUM_HEADS = 16
        D_MODEL = 128
        D_K = D_MODEL // NUM_HEADS
        B, S = (2, 256)
        b, s, d = x.shape

        def split_heads(t):
            return t.reshape(b, -1, NUM_HEADS, D_K).transpose(0, 2, 1, 3)
        q = split_heads(x @ wq.T + bq)
        k = split_heads(y @ wk.T + bk)
        v = split_heads(y @ wv.T + bv)
        scores = jnp.einsum('bhqd,bhkd->bhqk', q, k) / np.sqrt(D_K)
        scores = scores + (1.0 - mask[:, None, None, :]) * -10000.0
        attn = jax.nn.softmax(scores, axis=-1)
        z = jnp.einsum('bhqk,bhkd->bhqd', attn, v)
        z = z.transpose(0, 2, 1, 3).reshape(b, -1, d)
        return z @ wo.T + bo

    def _L3_ffn_ref(x, router_w, w1, b1, w2, b2):
        import jax, jax.numpy as jnp
        import numpy as np
        TOP_K = 2
        B, S, D = x.shape
        E = router_w.shape[0]
        xf = x.reshape(-1, D)
        logits = xf @ router_w.T
        probs = jax.nn.softmax(logits, axis=-1)
        top_v, top_i = jax.lax.top_k(probs, TOP_K)
        gates = top_v / (jnp.sum(top_v, axis=-1, keepdims=True) + 1e-09)
        out = jnp.zeros_like(xf)
        for e in range(E):
            ge = jnp.sum(jnp.where(top_i == e, gates, 0.0), axis=-1, keepdims=True)
            h = jax.nn.gelu(xf @ w1[e] + b1[e], approximate=False)
            out = out + ge * (h @ w2[e] + b2[e])
        return out.reshape(B, S, D)
    x = x + _L0_xattn_ref(_layernorm(x, axis=-1), ctx_1024, L0_xattn_qkv_w, L0_xattn_qkv_b, L0_xattn_sa_out_w, L0_xattn_sa_out_b, L0_xattn_in_proj_w, L0_xattn_in_proj_b, L0_xattn_mha_out_w, L0_xattn_mha_out_b, L0_xattn_lin1_w, L0_xattn_lin1_b, L0_xattn_lin2_w, L0_xattn_lin2_b, L0_xattn_ln1_g, L0_xattn_ln1_b, L0_xattn_ln2_g, L0_xattn_ln2_b, L0_xattn_ln3_g, L0_xattn_ln3_b)
    x = x + _L0_ffn_ref(_layernorm(x, axis=-1), L0_ffn_w_switch, L0_ffn_b_switch, L0_ffn_w1, L0_ffn_b1, L0_ffn_w2, L0_ffn_b2)
    x = x + _L1_xattn_ref(_layernorm(x, axis=-1), ctx_1024, mask_BxSxS2_bf1, L1_xattn_Wq, L1_xattn_Wkv, L1_xattn_Wo)
    x = x + _L1_ffn_ref(_layernorm(x, axis=-1), L1_ffn_slot_query, L1_ffn_d_Wq, L1_ffn_d_Wk, L1_ffn_d_Wv, L1_ffn_d_Wo, L1_ffn_d_bq, L1_ffn_d_bk, L1_ffn_d_bv, L1_ffn_d_bo, L1_ffn_c_Wq, L1_ffn_c_Wk, L1_ffn_c_Wv, L1_ffn_c_Wo, L1_ffn_c_bq, L1_ffn_c_bk, L1_ffn_c_bv, L1_ffn_c_bo, L1_ffn_e_ln_g, L1_ffn_e_ln_b, L1_ffn_e_W1, L1_ffn_e_b1, L1_ffn_e_Wg, L1_ffn_e_bg, L1_ffn_e_W2, L1_ffn_e_b2)
    x = x + _L2_xattn_ref(_layernorm(x, axis=-1), ctx_1024, ctx_1024, mask_BxS2_bf1, L2_xattn_Wq, L2_xattn_Wk, L2_xattn_Wv, L2_xattn_Wout)
    x = x + _L2_ffn_ref(_layernorm(x, axis=-1), L2_ffn_w_g, L2_ffn_c_fc, L2_ffn_c_proj)
    x = x + _L3_xattn_ref(_layernorm(x, axis=-1), ctx_1024, mask_BxS2_ff1, L3_xattn_wq, L3_xattn_bq, L3_xattn_wk, L3_xattn_bk, L3_xattn_wv, L3_xattn_bv, L3_xattn_wo, L3_xattn_bo)
    x = x + _L3_ffn_ref(_layernorm(x, axis=-1), L3_ffn_router_w, L3_ffn_w1, L3_ffn_b1, L3_ffn_w2, L3_ffn_b2)
    return x

_drawn_inputs = setup_inputs


def setup_inputs(seed=0):
    import zlib

    import numpy as np

    out = dict(_drawn_inputs(seed))
    spreads = {'L0_xattn_qkv_b': (0.0, 0.1),
     'L0_xattn_sa_out_b': (0.0, 0.1),
     'L0_xattn_in_proj_b': (0.0, 0.1),
     'L0_xattn_mha_out_b': (0.0, 0.1),
     'L0_xattn_lin1_b': (0.0, 0.1),
     'L0_xattn_lin2_b': (0.0, 0.1),
     'L0_xattn_ln1_g': (1.0, 0.2),
     'L0_xattn_ln1_b': (0.0, 0.1),
     'L0_xattn_ln2_g': (1.0, 0.2),
     'L0_xattn_ln2_b': (0.0, 0.1),
     'L0_xattn_ln3_g': (1.0, 0.2),
     'L0_xattn_ln3_b': (0.0, 0.1),
     'L0_ffn_b_switch': (0.0, 0.1),
     'L0_ffn_b1': (0.0, 0.8),
     'L0_ffn_b2': (0.0, 0.336),
     'L1_ffn_d_bq': (0.0, 0.8),
     'L1_ffn_d_bk': (0.0, 2.0),
     'L1_ffn_d_bv': (0.0, 0.8),
     'L1_ffn_d_bo': (0.0, 0.8),
     'L1_ffn_c_bq': (0.0, 0.8),
     'L1_ffn_c_bk': (0.0, 2.0),
     'L1_ffn_c_bv': (0.0, 2.0),
     'L1_ffn_c_bo': (0.0, 0.8),
     'L1_ffn_e_ln_g': (1.0, 0.6),
     'L1_ffn_e_ln_b': (0.0, 0.8),
     'L1_ffn_e_b1': (0.0, 0.8),
     'L1_ffn_e_bg': (0.0, 0.8),
     'L1_ffn_e_b2': (0.0, 0.8),
     'L3_xattn_bq': (0.0, 0.1),
     'L3_xattn_bk': (0.0, 0.1),
     'L3_xattn_bv': (0.0, 0.8),
     'L3_xattn_bo': (0.0, 0.8),
     'L3_ffn_b1': (0.0, 2.0),
     'L3_ffn_b2': (0.0, 2.0)}
    factors = {'L0_ffn_w1': 3.804,
     'L0_ffn_w2': 2.958,
     'L1_ffn_slot_query': 8.0,
     'L1_ffn_d_Wq': 8.0,
     'L1_ffn_d_Wk': 8.0,
     'L1_ffn_d_Wv': 8.0,
     'L1_ffn_d_Wo': 8.0,
     'L1_ffn_c_Wq': 8.0,
     'L1_ffn_c_Wk': 8.0,
     'L1_ffn_c_Wv': 8.0,
     'L1_ffn_c_Wo': 6.764,
     'L1_ffn_e_W1': 8.0,
     'L1_ffn_e_Wg': 8.0,
     'L1_ffn_e_W2': 8.0,
     'L2_ffn_w_g': 19.667,
     'L2_ffn_c_fc': 17.225,
     'L2_ffn_c_proj': 15.344,
     'L3_ffn_w1': 18.471,
     'L3_ffn_w2': 5.753,
     'L2_xattn_Wq': 8.0,
     'L2_xattn_Wk': 8.0,
     'L2_xattn_Wv': 5.801,
     'L2_xattn_Wout': 5.607,
     'L3_xattn_wv': 2.987,
     'L3_xattn_wo': 3.241}
    for name, (base, spread) in spreads.items():
        noise = np.random.default_rng([zlib.crc32(name.encode()), seed]).standard_normal(out[name].shape)
        drawn = base * np.exp(spread * noise) if base else spread * noise
        out[name] = jnp.asarray(drawn.astype(out[name].dtype))
    for name, factor in factors.items():
        out[name] = (out[name] * factor).astype(out[name].dtype)
    return out
```

```python
from contextlib import ExitStack

import numpy as np

import concourse.bass as bass
from concourse import mybir

ALU = mybir.AluOpType
ACT = mybir.ActivationFunctionType
AX = mybir.AxisListType
F32 = mybir.dt.float32
BF16 = mybir.dt.bfloat16
U8 = mybir.dt.uint8

P = 128
B = 4
S = 512
D = 128
NK = 32
C = S // P
E = 8
SE = 16
SLOTS = 16
EPS = 1e-5
BIG = 1e30

ATT = {
    "L0": dict(H=8, nk=NK, dh=16, scale=16 ** -0.5),
    "L1": dict(H=2, nk=NK, dh=64, scale=64 ** -0.5),
    "CB": dict(H=16, nk=SLOTS, dh=8, scale=8 ** -0.5),
    "L2": dict(H=1, nk=NK, dh=64, scale=64 ** -0.5),
    "L3": dict(H=16, nk=NK, dh=8, scale=8 ** -0.5),
}
for _a in ATT.values():
    _a["PD"] = _a["H"] * _a["dh"]
    _a["R"] = _a["H"] * _a["nk"]
    _a["RB"] = min(P, _a["R"])
    _a["G"] = _a["R"] // _a["RB"]
    _a["hb"] = _a["RB"] // _a["nk"]
    _a["cpu"] = min(C, 512 // _a["R"])
    _a["nu"] = C // _a["cpu"]

SQUARES = [("L0v", 128), ("L0so", 128), ("L0q", 128), ("L0k", 128), ("L0mv", 128), ("L0o", 128),
           ("L0l1", 512), ("L0l2", 512),
           ("L1q", 128), ("L1k", 128), ("L1v", 128), ("L1o", 128),
           ("L2q", 64), ("L2k", 64), ("L2v", 64),
           ("L3q", 128), ("L3k", 128), ("L3v", 128), ("L3o", 128),
           ("Dq", 128), ("Dk", 128), ("Dv", 128), ("Do", 128),
           ("CBq", 128), ("CBk", 128), ("CBv", 128), ("CBo", 128),
           ("wr0", 8), ("wr2", 8), ("wr3", 8)]
COLUMNS = [("L0bv", 1), ("L0bq", 1), ("L0bk", 1), ("L0bl1", 4), ("L3bq", 1), ("L3bk", 1),
           ("Dbq", 1), ("Dbk", 1), ("Dbv", 1), ("CBbq", 1), ("CBbk", 1),
           ("m0b1", 32), ("m3b1", 16), ("eb1", 64), ("ebg", 64), ("eb2", 16), ("sqT", 16),
           ("ctxT", 128)]
ROWS = [("so_b", 128), ("g1", 128), ("b1", 128), ("mo_b", 128), ("g2", 128), ("b2", 128),
        ("l2_b", 128), ("g3", 128), ("b3", 128), ("L0mvb", 128), ("L3vb", 128), ("L3ob", 128),
        ("CBvb", 128), ("CBob", 128), ("Dob", 128), ("sw_b", 8)]
CONSTS = [("ident", 128), ("tri", 128), ("ones", 128), ("first", 8)]
for _n, _a in ATT.items():
    CONSTS += [(_n + "_dim", _a["H"]), (_n + "_sel", _a["G"] * _a["H"]), (_n + "_neg", _a["R"])]


def places(fields):
    at, out = 0, {}
    for name, n in fields:
        out[name] = (at, at + n)
        at += n
    return out, at


SQ_AT, SQ_N = places(SQUARES)
COL_AT, COL_N = places(COLUMNS)
ROW_AT, ROW_N = places(ROWS)
CON_AT, CON_N = places(CONSTS)


def constants():
    out = np.zeros((P, CON_N), np.float32)
    p = np.arange(P)
    out[:, slice(*CON_AT["ident"])] = np.eye(P)
    out[:, slice(*CON_AT["tri"])] = p[:, None] <= p[None, :]
    out[:, slice(*CON_AT["ones"])] = 1.0
    out[:, slice(*CON_AT["first"])] = E - np.arange(E)
    for n, a in ATT.items():
        h = np.arange(a["H"])
        out[:, slice(*CON_AT[n + "_dim"])] = (p[:, None] // a["dh"]) == h
        sel = np.zeros((P, a["G"], a["H"]), np.float32)
        for g in range(a["G"]):
            sel[:, g, :] = (g * a["hb"] + p[:, None] // a["nk"]) == h
        sel[a["RB"]:] = 0
        out[:, slice(*CON_AT[n + "_sel"])] = sel.reshape(P, -1)
        neg = np.zeros((P, a["R"]), np.float32)
        neg[:a["H"]] = np.where(np.arange(a["R"])[None, :] // a["nk"] == h[:, None], -1.0, 0.0)
        out[:, slice(*CON_AT[n + "_neg"])] = neg
    return out


def build(nc, ins, out):
    ctx = ExitStack()
    with ctx:
        def sb(name, shape, dt=F32):
            return ctx.enter_context(nc.sbuf_tensor(name, shape, dt))

        def sem(name):
            return ctx.enter_context(nc.semaphore(name))

        x = sb("x", [P, B * C, D])
        r = sb("r", [P, B * C, D])
        xn = sb("xn", [P, B * C, D])
        xT = sb("xT", [P, B, S])
        qT = sb("qT", [P, B, S])
        mT = xn[0:16, :, :].rearrange("p (b c) d -> p b (c d)", b=B)
        big = sb("big", [P, 4, B, S])
        sq = sb("sq", [P, SQ_N])
        wout2 = sb("wout2", [64, D])
        col = sb("col", [P, COL_N])
        row = sb("row", [P, ROW_N])
        con = sb("con", [P, CON_N])
        mask_tok = sb("mask_tok", [P, B * C, NK], U8)
        mask_key = sb("mask_key", [NK, B * S], U8)
        mask2 = sb("mask2", [P, B, NK], U8)
        mask2c = sb("mask2c", [NK, B], U8)
        mask3 = sb("mask3", [P, B, NK])
        mask3c = sb("mask3c", [P, B])
        b2m0 = sb("b2m0", [E, D])
        b2m3 = sb("b2m3", [E, D])
        moe_w = sb("moe_w", [P, E, 1024])
        RING = 5
        ring = sb("ring", [P, RING, 3 * 512])
        sqrow = sb("sqrow", [B * SLOTS, D])
        lng = sb("lng", [B * SLOTS, D])
        lnb = sb("lnb", [B * SLOTS, D])
        KB, VB, KTs, REP, VR = {}, {}, {}, {}, {}
        for n, a in ATT.items():
            if n == "CB":
                continue
            if n != "L3":
                KB[n] = sb("kb_" + n, [P, B, a["R"]])
            if n != "L3":
                VB[n] = sb("vb_" + n, [P, B, a["G"], P + 16 if n == "L0" else a["PD"] + a["H"]])
        KB["CB"] = KB["L0"]
        VB["CB"] = VB["L0"]
        ring_flat = ring[:, :, :].rearrange("p a b -> p (a b)")
        w3 = ring_flat[:, 0:E * 512].rearrange("p (e n) -> p e n", e=E)
        VB["L3"] = ring_flat[:, E * 512:E * 512 + B * 4 * 144].rearrange("p (b g w) -> p b g w", b=B, g=4)
        KB["L3"] = r[:, :, :].rearrange("p (b c) d -> p b (c d)", b=B)
        kts = sb("kts", [P, B * NK])
        rep = sb("rep", [P, B, P])
        vr = sb("vr", [P, B, D])
        st = sb("st", [P, B * C, 6])
        mv = sb("mv", [P, B * C, 2])
        rstd = sb("rstd", [P, B * C])
        half = sb("half", [P, C])
        mx = sb("mx", [P, B * C, 16])
        rs = sb("rs", [P, B * C, 16])
        msc = sb("msc", [P, C, 2, NK])
        madd_t = sb("madd_t", [P, B * C, NK])
        madd_k = r[0:NK, :, :].rearrange("p a b -> p (a b)")
        m2c = sb("m2c", [NK, B])
        m2r = sb("m2r", [P, B, NK])
        m3c = sb("m3c", [P, B])
        m3r = sb("m3r", [P, B, NK])
        rep2 = sb("rep2", [NK, 2, NK])
        lg = sb("lg", [P, B * C, E])
        lg2 = sb("lg2", [P, B * C, E])
        ga = sb("ga", [P, 2 * B * C, E])
        gb = sb("gb", [P, 2 * B * C, E])
        gt = sb("gt", [P, 2 * B * C, E])
        oh = sb("oh", [P, 2 * B * C, E])
        gm = sb("gm", [P, B * C])
        gs = sb("gs", [P, B * C])
        gate = sb("gate", [P, B * C, E])
        drop = sb("drop", [P, B * C])
        gateT = qT[0:E, :, :]
        qblk = sb("qblk", [P, SE, SLOTS])
        dqT = sb("dqT", [P, SLOTS])
        dm = sb("dm", [P, B, 2])
        dsum = sb("dsum", [P, B, 2])
        drs = sb("drs", [P, B, 2])
        pair = sb("pair", [P, SE, SLOTS])
        attT = sb("attT", [P, B * SLOTS])
        orow = sb("orow", [B * SLOTS, D])
        hrow = sb("hrow", [B * SLOTS, D])
        hT = sb("hT", [P, B, SLOTS])
        oT = sb("oT", [P, B, SLOTS])
        uu, gg, eu, eg = (big[:, 0, 0, 256 * j:256 * j + 256].rearrange(
            "p (e f b) -> p e f b", e=SE, f=4) if j < 2 else
            big[:, 0, 1, 256 * (j - 2):256 * (j - 1)].rearrange("p (e f b) -> p e f b", e=SE, f=4)
            for j in range(4))
        ps = [ctx.enter_context(nc.psum_tensor(f"ps{i}", [P, 512], F32)) for i in range(8)]

        ld_w = sem("ld_w")
        ld_w2 = sem("ld_w2")
        ld_c = sem("ld_c")
        ld_x = sem("ld_x")
        ld_s = sem("ld_s")
        ld_m0 = sem("ld_m0")
        ld_m2 = sem("ld_m2")
        ld_m3 = sem("ld_m3")
        ld_e = [sem(f"ld_e{i}") for i in range(RING)]
        stored = sem("stored")
        dve_chain, pool_chain = sem("dve_chain"), sem("pool_chain")
        masks, minus_half = sem("masks"), sem("minus_half")
        var_ready, rstd_ready = sem("var_ready"), sem("rstd_ready")
        tok_ready, turned, xT_ready = sem("tok_ready"), sem("turned"), sem("xT_ready")
        proj_mm, proj_ready = sem("proj_mm"), sem("proj_ready")
        out_mm = sem("out_mm")
        kv_rep, k_mm, k_sb, v_mm, v_sb, kv_ready = (sem(n) for n in ("kv_rep", "k_mm", "k_sb", "v_mm", "v_sb", "kv_ready"))
        s_mm, s_max, m_turned, mT_ready = sem("s_mm"), sem("s_max"), sem("m_turned"), sem("mT_ready")
        sT_mm, probs = sem("sT_mm"), sem("probs")
        av_mm = sem("av_mm")
        h_mm, h_act, y_mm, y_used = sem("h_mm"), sem("h_act"), sem("y_mm"), sem("y_used")
        lg_mm, oh_ready, cum_mm = sem("lg_mm"), sem("oh_ready"), sem("cum_mm")
        gate_e, gate_ep, gate_ready, gT_mm, gT_sb, gb_mm = (sem(n) for n in ("gate_e", "gate_ep", "gate_ready", "gT_mm", "gT_sb", "gb_mm"))
        dq_mm, qblk_ready, dv_mm, dv_sb, ds_mm, dmax, dexp, dnorm, dp_mm, dp_sb, da_mm, att_ready = (
            sem(n) for n in ("dq_mm", "qblk_ready", "dv_mm", "dv_sb", "ds_mm", "dmax", "dexp", "dnorm",
                             "dp_mm", "dp_sb", "da_mm", "att_ready"))
        do_mm, h_rows, hT_mm, hT_ready, e_mm, e_h, e_exp, e_act, ey_mm, oT_ready = (
            sem(n) for n in ("do_mm", "h_rows", "hT_mm", "hT_ready", "e_mm", "e_h", "e_exp", "e_act", "ey_mm", "oT_ready"))

        def W(name):
            return sq[:, slice(*SQ_AT[name])]

        def V(name, i=0, n=None):
            lo, hi = COL_AT[name]
            return col[:, lo + i:lo + i + (n or 1)]

        def ROW(name):
            return row[:, slice(*ROW_AT[name])]

        def K(name):
            return con[:, slice(*CON_AT[name])]

        ident = K("ident")

        def bc(ap, shape, axes):
            for i in axes:
                ap = ap.unsqueeze(i)
            return ap.to_broadcast(shape)

        cols = lambda c: slice(P * c, P * c + P)
        CTX_ATT = ["L0", "L1", "L2"]
        block = ctx.enter_context(nc.Block())

        def slot_bank(e):
            return (3, 4, 6, 7)[e % 4]

        def probs_T(t, c):
            return big[:, 2:4, t, :].rearrange("p g (c n) -> p g c n", c=C)[:, :, c, :]

        def moe_load(sp, name, w, F, done):
            for e in range(E):
                sp.dma_start(w[:, e, 0:F], ins[name + "w1"][e]).then_inc(done, 16)
                sp.dma_start(w[:, e, F:2 * F].rearrange("p (c n) -> p c n", n=D),
                             ins[name + "w2"][e].rearrange("(c p) n -> p c n", p=P)).then_inc(done, 16)

        @block.sync
        def _(sp):
            sp.dma_start(x[:, :, :], ins["x"].rearrange("b (c p) d -> p (b c) d", p=P)).then_inc(ld_x, 16)
            sp.dma_start(con[:, :], ins["con"]).then_inc(ld_c, 16)
            sp.dma_start(col[:, :], ins["col"]).then_inc(ld_c, 16)
            sp.dma_start(row[:, :], ins["row"].to_broadcast([P, ROW_N])).then_inc(ld_c, 16)
            sp.dma_start(sq[:, :], ins["sq"]).then_inc(ld_w, 16)
            sp.dma_start(wout2[:, :], ins["wout2"]).then_inc(ld_w, 16)
            sp.dma_start(mask_tok[:, :, :], ins["mask"].rearrange("b (c p) k -> p (b c) k", p=P)).then_inc(ld_s, 16)
            sp.dma_start(mask_key[:, :], ins["maskT"]).then_inc(ld_s, 16)
            sp.dma_start(mask2[:, :, :], ins["mask2"].to_broadcast([P, B * NK]).rearrange("p (b k) -> p b k", b=B)).then_inc(ld_s, 16)
            sp.dma_start(mask2c[:, :], ins["mask2c"]).then_inc(ld_s, 16)
            sp.dma_start(mask3[:, :, :], ins["mask3"].to_broadcast([P, B * NK]).rearrange("p (b k) -> p b k", b=B)).then_inc(ld_s, 16)
            sp.dma_start(mask3c[:, :], ins["mask3c"]).then_inc(ld_s, 16)
            sp.dma_start(b2m0[:, :], ins["m0b2"]).then_inc(ld_s, 16)
            sp.dma_start(b2m3[:, :], ins["m3b2"]).then_inc(ld_s, 16)
            for b in range(B):
                rows = slice(b * SLOTS, (b + 1) * SLOTS)
                sp.dma_start(sqrow[rows, :], ins["sqrow"]).then_inc(ld_s, 16)
                sp.dma_start(lng[rows, :], ins["lng"]).then_inc(ld_s, 16)
                sp.dma_start(lnb[rows, :], ins["lnb"]).then_inc(ld_s, 16)
            moe_load(sp, "m0", moe_w, 512, ld_m0)

            def expert_load(e):
                w = ring[:, e % RING, :]
                sp.dma_start(w[:, 0:512], ins["ew1"][e]).then_inc(ld_e[e % RING], 16)
                sp.dma_start(w[:, 512:1024], ins["ewg"][e]).then_inc(ld_e[e % RING], 16)
                sp.dma_start(w[:, 1024:1536].rearrange("p (c n) -> p c n", c=4),
                             ins["ew2"][e].rearrange("(c p) n -> p c n", p=P)).then_inc(ld_e[e % RING], 16)
            for e in range(RING):
                expert_load(e)
            sp.wait_ge(y_mm, E * B)
            moe_load(sp, "m2", moe_w, 512, ld_m2)
            for e in range(RING, SE):
                sp.wait_ge(ey_mm, e - RING + 1)
                expert_load(e)
            sp.wait_ge(ey_mm, SE)
            moe_load(sp, "m3", w3, 256, ld_m3)
            for t in range(B):
                sp.wait_ge(y_used, 3 * E * B + 2 - B + t + 1)
                sp.dma_start(out[t].rearrange("(c p) d -> p c d", p=P), x[:, C * t:C * t + C, :]).then_inc(stored, 16)
            sp.wait_ge(stored, 16 * B)

        @block.tensor
        def _(pe):
            mm = nc.tensor.matmul
            n = dict(turn=0, proj=0, out=0, smax=0, mt=0, sT=0, av=0, kv=0, moe=0, h=0, y=0, lg=0, lin=0)

            def turn(src, width=D):
                k = n["turn"]
                for t in range(B):
                    pe.wait_ge(tok_ready, 4 * k + t + 1)
                    for c in range(C):
                        last = nc.tensor.transpose(ps[2 * t][0:width, cols(c)], src[:, C * t + c, 0:width], ident)
                    last.then_inc(turned, 1)
                n["turn"] += 1

            def need_xT(t):
                pe.wait_ge(xT_ready, 4 * (n["turn"] - 1) + t + 1)

            def project(w, width=D):
                for t in range(B):
                    need_xT(t)
                    mm(ps[2 * t + 1][0:width, :], w, xT[:, t, :], start=True, stop=True).then_inc(proj_mm, 1)
                n["proj"] += 1

            def need_proj(t):
                pe.wait_ge(proj_ready, 4 * (n["proj"] - 1) + t + 1)

            def out_tokens(src, w, bank=1):
                for t in range(B):
                    if src is qT:
                        need_proj(t)
                    else:
                        need_xT(t)
                    width = w.shape[0]
                    for c in range(C):
                        last = mm(ps[2 * t + bank][:, cols(c)], src[0:width, t, cols(c)], w, start=True, stop=True)
                    last.then_inc(out_mm, 1)
                n["out"] += 1

            def prepare(name, keys):
                a = ATT[name]
                k = n["kv"]
                pe.wait_ge(kv_rep, k + 1)
                mm(ps[0][0:a["PD"], 0:B * a["nk"]], W(name + "k") if name != "L0" else W("L0k"), keys,
                   start=True, stop=True).then_inc(k_mm, 1)
                wv = W("L0mv") if name == "L0" else W(name + "v")
                for b in range(B):
                    last = mm(ps[1][0:a["RB"], b * a["PD"]:(b + 1) * a["PD"]], rep[:, b, 0:a["RB"]], wv,
                              start=True, stop=True)
                last.then_inc(v_mm, 1)
                n["kv"] += 1
                pe.wait_ge(k_sb, n["kv"])
                pe.wait_ge(v_sb, n["kv"])

            def attend(name):
                a = ATT[name]
                R, RB, G, H, nu, cpu, PD = (a[i] for i in ("R", "RB", "G", "H", "nu", "cpu", "PD"))
                kb, vb = KB[name], VB[name]
                pe.wait_ge(kv_ready, {"L0": 1, "L1": 2, "L2": 3, "CB": 4, "L3": 5}[name])
                if name == "L0":
                    pe.wait_ge(masks, 1)
                for u in range(nu):
                    for t in range(B):
                        if u == 0:
                            need_proj(t)
                        if u >= 2:
                            pe.wait_ge(s_max, n["smax"] + 4 * (u - 2) + t + 1)
                        for i in range(cpu):
                            c = u * cpu + i
                            o = ps[2 * t + u % 2][:, i * R:(i + 1) * R]
                            if name == "L3":
                                mm(o, K("ones")[0:1, :], bc(m3r[0:1, t, :], [1, H, NK], [1]), start=True, stop=False)
                            if name == "L2":
                                mm(o, K("ones")[0:1, :], m2r[0:1, t, :], start=True, stop=False)
                            last = mm(o, qT[0:PD, t, cols(c)], kb[0:PD, t, :], start=name not in ("L2", "L3"), stop=True)
                        last.then_inc(s_mm, 1)
                for t in range(B):
                    pe.wait_ge(s_max, n["smax"] + 4 * (nu - 1) + t + 1)
                    for c in range(C):
                        last = nc.tensor.transpose(ps[2 * t][0:H, cols(c)], mx[:, C * t + c, 0:H], ident)
                    last.then_inc(m_turned, 1)
                n["smax"] += 4 * nu
                if name == "L1":
                    pe.wait_ge(masks, 2)
                for g in range(G):
                    for t in range(B):
                        if g == 0:
                            pe.wait_ge(mT_ready, n["mt"] + t + 1)
                        if g >= 2:
                            pe.wait_ge(probs, n["sT"] + 4 * (g - 2) + t + 1)
                        o = ps[2 * t + 1 - g % 2][0:RB, :]
                        mm(o, kb[0:PD, t, g * RB:(g + 1) * RB], qT[0:PD, t, :], start=True, stop=False)
                        if name == "L1":
                            mm(o, rep2[:, :, :].rearrange("p a b -> p (a b)"), madd_k[:, t * S:(t + 1) * S], start=False, stop=False)
                        mm(o, K(name + "_neg")[0:H, g * RB:(g + 1) * RB], mT[0:H, t, :], start=False, stop=True).then_inc(sT_mm, 1)
                wd = PD + H
                for t in range(B):
                    pe.wait_ge(probs, n["sT"] + 4 * (G - 1) + t + 1)
                    for c in range(C):
                        o = ps[2 * t + c // 2][:, (c % 2) * wd:(c % 2 + 1) * wd]
                        for g in range(G):
                            last = mm(o, big[0:RB, g, t, cols(c)], vb[0:RB, t, g, 0:wd], start=g == 0, stop=g == G - 1)
                    last.then_inc(av_mm, 1)
                n["mt"] += 4
                n["sT"] += 4 * G
                turn(xn, PD)

            def mixture(name, w, F, loaded, wr, ranks, bias):
                k = n["moe"]
                FC = F // P
                turn(xn)
                for t in range(B):
                    need_xT(t)
                    for c in range(C):
                        last = mm(ps[2 * t + 1][:, c * E:(c + 1) * E], xT[:, t, cols(c)], wr, start=True, stop=True)
                    last.then_inc(lg_mm, 1)
                if ranks:
                    pe.wait_ge(oh_ready, min(k, 1) + 1)
                    m = ranks * B * C * E
                    chosen = oh[:, :, :].rearrange("p a b -> p (a b)")[:, 0:m]
                    mm(ps[0][:, 0:m], K("tri"), chosen, start=True, stop=True)
                    mm(ps[2][:, 0:m], K("ones"), chosen, start=True, stop=True).then_inc(cum_mm, 1)
                if bias is not None:
                    pe.wait_ge(gate_ready, k + 1)
                    kb = 0 if k == 0 else 1
                    for t in range(B):
                        for c in range(C):
                            last = nc.tensor.transpose(ps[2 * t][0:E, cols(c)], gate[:, C * t + c, :], ident)
                        last.then_inc(gT_mm, 1)
                    for t in range(B):
                        pe.wait_ge(gT_sb, 4 * kb + t + 1)
                        for c in range(C):
                            last = mm(ps[2 * t + 1][:, cols(c)], gateT[:, t, cols(c)], bias[:, :], start=True, stop=True)
                        last.then_inc(gb_mm, 1)
                    pe.wait_ge(y_used, n["y"] + k + 1 - (1 if k == 2 else 0))
                else:
                    pe.wait_ge(gate_ready, k + 1)
                ybase = n["y"]
                used0 = n["y"] + {0: 1, 1: 1, 2: 2}[k]

                def hidden(i):
                    e, t = divmod(i, B)
                    if t == 0:
                        pe.wait_ge(loaded, 32 * E if True else 0)
                    for f in range(FC):
                        u = n["h"]
                        if i * FC + f >= 6:
                            pe.wait_ge(h_act, u - 5)
                        mm(ps[(i * FC + f) % 6][:, :], w[:, e, cols(f)], xT[:, t, :], start=True, stop=True).then_inc(h_mm, 1)
                        n["h"] += 1
                    return n["h"]

                def outputs(i, have):
                    e, t = divmod(i, B)
                    pe.wait_ge(h_act, have)
                    if i >= 2:
                        pe.wait_ge(y_used, used0 + i - 1)
                    for c in range(C):
                        for f in range(FC):
                            last = mm(ps[6 + i % 2][:, cols(c)], big[:, f, i % B, cols(c)],
                                      w[:, e, F + P * f:F + P * f + P], start=f == 0, stop=f == FC - 1)
                    last.then_inc(y_mm, 1)
                    n["y"] += 1

                have = hidden(0)
                for i in range(E * B):
                    nxt = hidden(i + 1) if i + 1 < E * B else None
                    outputs(i, have)
                    have = nxt
                n["moe"] += 1

            def slot_layer():
                turn(xn)
                project(W("Dk"))
                for t in range(B):
                    for c in range(C):
                        last = mm(ps[2 * t][:, cols(c)], xT[:, t, cols(c)], W("Dv"), start=True, stop=True)
                    last.then_inc(dv_mm, 1)
                qb = qblk[:, :, :].rearrange("p h s -> p (h s)")
                for g in range(2):
                    for t in range(B):
                        if g == 0:
                            need_proj(t)
                        else:
                            pe.wait_ge(dv_sb, t + 1)
                        mm(ps[2 * t + 1 - g][:, :], qb[:, cols(g)], qT[:, t, :], start=True, stop=True).then_inc(ds_mm, 1)
                for g in range(2):
                    for t in range(B):
                        pe.wait_ge(dnorm, 4 * g + t + 1)
                        for c in range(C):
                            last = nc.tensor.transpose(ps[2 * t + 1 - g][:, cols(c)], big[:, g, t, cols(c)], ident)
                        last.then_inc(dp_mm, 1)
                for t in range(B):
                    pe.wait_ge(dp_sb, 4 + t + 1)
                    o = ps[2 * t][:, 0:2 * P]
                    for c in range(C):
                        last = mm(o, r[:, C * t + c, :], probs_T(t, c), start=c == 0, stop=c == C - 1)
                    last.then_inc(da_mm, 1)
                pe.wait_ge(att_ready, 4)
                mm(ps[0][0:B * SLOTS, 0:D], attT[:, :], W("Do"), start=True, stop=True).then_inc(do_mm, 1)
                pe.wait_ge(h_rows, 1)
                nc.tensor.transpose(ps[1][:, 0:B * SLOTS], hrow[:, :], ident[0:B * SLOTS, 0:B * SLOTS])
                nc.tensor.transpose(ps[2][:, 0:B * SLOTS], orow[:, :], ident[0:B * SLOTS, 0:B * SLOTS]).then_inc(hT_mm, 1)
                pe.wait_ge(hT_ready, 1)
                U = lambda e, f: ps[slot_bank(e)][:, 4 * f:4 * f + 4]
                Gt = lambda e, f: ps[slot_bank(e)][:, 16 + 4 * f:16 + 4 * f + 4]
                for e in range(SE):
                    w = ring[:, e % RING, :]
                    pe.wait_ge(ld_e[e % RING], 48 * (e // RING + 1))
                    if e >= 4:
                        pe.wait_ge(e_h, e - 3)
                    for f in range(4):
                        mm(U(e, f), w[:, cols(f)], hT[:, :, e], start=True, stop=True)
                        last = mm(Gt(e, f), w[:, 512 + P * f:512 + P * f + P], hT[:, :, e], start=True, stop=True)
                    last.then_inc(e_mm, 1)
                    if e >= 1:
                        second(e - 1)
                second(SE - 1)
                pe.wait_ge(oT_ready, 1)
                prepare("CB", oT[:, :, :].rearrange("p b s -> p (b s)"))
                project(W("CBq"))
                attend("CB")
                out_tokens(xT, W("CBo"))

            def second(e):
                w = ring[:, e % RING, :]
                pe.wait_ge(e_act, e + 1)
                for f in range(4):
                    last = mm(ps[5][:, 4 * e:4 * e + 4], w[:, 1024 + P * f:1024 + P * f + P], uu[:, e, f, :],
                              start=f == 0, stop=f == 3)
                last.then_inc(ey_mm, 1)

            pe.wait_ge(ld_w, 32)
            pe.wait_ge(ld_c, 48)
            for name in CTX_ATT:
                prepare(name, V("ctxT", 0, B * NK))
            mm(ps[2][:, 0:SLOTS], W("Dq"), V("sqT", 0, SLOTS), start=True, stop=True).then_inc(dq_mm, 1)
            pe.wait_ge(qblk_ready, 1)
            turn(r)
            project(W("L0v"))
            out_tokens(qT, W("L0so"), 0)
            turn(r)
            project(W("L0q"))
            attend("L0")
            out_tokens(xT, W("L0o"))
            turn(r)
            for f in range(4):
                for t in range(B):
                    if f == 0:
                        need_xT(t)
                    if f >= 2:
                        pe.wait_ge(h_act, 4 * (f - 2) + t + 1)
                    mm(ps[2 * t + 1 - f % 2][:, :], W("L0l1")[:, cols(f)], xT[:, t, :], start=True, stop=True).then_inc(h_mm, 1)
            n["h"] = 16
            for t in range(B):
                pe.wait_ge(h_act, 12 + t + 1)
                for c in range(C):
                    for f in range(4):
                        last = mm(ps[2 * t + 1][:, cols(c)], big[:, f, t, cols(c)], W("L0l2")[:, cols(f)], start=f == 0, stop=f == 3)
                last.then_inc(out_mm, 1)
            mixture("m0", moe_w, 512, ld_m0, W("wr0"), 1, b2m0)
            turn(xn)
            project(W("L1q"))
            attend("L1")
            out_tokens(xT, W("L1o"))
            slot_layer()
            pe.wait_ge(tok_ready, 4 * n["turn"] + 1)
            prepare("L3", V("ctxT", 0, B * NK))
            turn(xn)
            project(W("L2q"), 64)
            attend("L2")
            out_tokens(xT, wout2[:, :])
            mixture("m2", moe_w, 512, ld_m2, W("wr2"), 2, None)
            turn(xn)
            project(W("L3q"))
            attend("L3")
            out_tokens(xT, W("L3o"))
            mixture("m3", w3, 256, ld_m3, W("wr3"), 0, b2m3)

        @block.scalar
        def _(act):
            A = nc.scalar.activation
            n = dict(turn=0, proj=0, sT=0, h=0, moe=0)

            def turn(width=D):
                for t in range(B):
                    k = 4 * n["turn"] + t + 1
                    act.wait_ge(turned, k)
                    A(xT[0:width, t, :], ps[2 * t][0:width, :], ACT.Identity).then_inc(xT_ready, 1)
                n["turn"] += 1

            def project(bias, width=D):
                for t in range(B):
                    act.wait_ge(proj_mm, 4 * n["proj"] + t + 1)
                    A(qT[0:width, t, :], ps[2 * t + 1][0:width, :], ACT.Identity,
                      bias=bias if bias is not None else 0.0).then_inc(proj_ready, 1)
                n["proj"] += 1

            def attend(name):
                a = ATT[name]
                RB, G = a["RB"], a["G"]
                for g in range(G):
                    for t in range(B):
                        act.wait_ge(sT_mm, n["sT"] + 1)
                        bias = m2c[:, t:t + 1] if name == "L2" else m3c[:, t:t + 1] if name == "L3" else 0.0
                        A(big[0:RB, g, t, :], ps[2 * t + 1 - g % 2][0:RB, :], ACT.Exp, bias=bias,
                          scale=a["scale"]).then_inc(probs, 1)
                        n["sT"] += 1
                turn(a["PD"])

            def mixture(F, fn, bias):
                FC = F // P
                turn()
                if n["moe"] > 0:
                    act.wait_ge(gate_e, n["moe"])
                    A(ga[:, 0:B * C, :], gb[:, 0:B * C, :], ACT.Exp).then_inc(gate_ep, 1)
                if bias:
                    for t in range(B):
                        act.wait_ge(gT_mm, (4 if n["moe"] else 0) + t + 1)
                        A(gateT[:, t, :], ps[2 * t][0:E, :], ACT.Identity).then_inc(gT_sb, 1)
                for i in range(E * B):
                    e, t = divmod(i, B)
                    for f in range(FC):
                        act.wait_ge(h_mm, n["h"] + 1)
                        if i >= B and f == 0:
                            act.wait_ge(y_mm, E * B * n["moe"] + i - B + 1)
                        A(big[:, f, i % B, :], ps[(i * FC + f) % 6][:, :], fn,
                          bias=V(bias, e * FC + f) if bias else 0.0).then_inc(h_act, 1)
                        n["h"] += 1
                n["moe"] += 1

            act.wait_ge(ld_c, 48)
            turn()
            project(V("L0bv"))
            turn()
            project(V("L0bq"))
            act.wait_ge(masks, 1)
            attend("L0")
            turn()
            for f in range(4):
                for t in range(B):
                    act.wait_ge(h_mm, n["h"] + 1)
                    A(big[:, f, t, :], ps[2 * t + 1 - f % 2][:, :], ACT.Relu, bias=V("L0bl1", f)).then_inc(h_act, 1)
                    n["h"] += 1
            mixture(512, ACT.Relu, "m0b1")
            turn()
            project(None)
            attend("L1")
            turn()
            project(V("Dbk"))
            for g in range(2):
                for t in range(B):
                    act.wait_ge(dmax, 4 * g + t + 1)
                    A(big[:, g, t, :], ps[2 * t + 1 - g][:, :], ACT.Exp, bias=dm[:, t, g:g + 1],
                      scale=ATT["CB"]["scale"], accum_out=dsum[:, t, g:g + 1]).then_inc(dexp, 1)
            for g in range(2):
                for t in range(B):
                    act.wait_ge(dp_mm, 4 * g + t + 1)
                    A(big[:, 2 + g, t, :], ps[2 * t + 1 - g][:, :], ACT.Identity).then_inc(dp_sb, 1)
            for e in range(SE):
                act.wait_ge(e_h, e + 1)
                A(eu[:, e, :, :], uu[:, e, :, :], ACT.Exp, scale=-1.0)
                A(eg[:, e, :, :], gg[:, e, :, :], ACT.Exp, scale=-1.0).then_inc(e_exp, 1)
            project(V("CBbq"))
            attend("CB")
            turn()
            project(None, 64)
            attend("L2")
            mixture(512, ACT.Gelu, None)
            turn()
            project(V("L3bq"))
            attend("L3")
            mixture(256, ACT.Gelu, "m3b1")

        @block.vector
        def _(dve):
            v = nc.vector
            n = dict(chain=0, out=0, smax=0, mt=0, av=0, lg=0, y=0, moe=0, tok=0, norm=0)

            def link(i):
                n["chain"] += 1
                i.then_inc(dve_chain, 1)
                dve.wait_ge(dve_chain, n["chain"])

            def chunks(t):
                return slice(C * t, C * t + C)

            def norms(src, dst, gain=None, shift=None, before=None, after=None):
                for t in range(B):
                    if before:
                        before(t)
                    for c in range(C):
                        i = v.bn_stats(st[:, C * t + c, :], src[:, C * t + c, :])
                    link(i)
                    for c in range(C):
                        i = v.bn_aggr(mv[:, C * t + c, :], st[:, C * t + c, :])
                    i.then_inc(var_ready, 1)
                n["norm"] += B
                for t in range(B):
                    tt = chunks(t)
                    dve.wait_ge(rstd_ready, n["norm"] - B + t + 1)
                    for c in range(C):
                        i = v.tensor_scalar(dst[:, C * t + c, :], src[:, C * t + c, :], mv[:, C * t + c, 0:1],
                                            rstd[:, C * t + c:C * t + c + 1], ALU.subtract, ALU.mult)
                    if gain is not None:
                        link(i)
                        link(v.tensor_tensor(dst[:, tt, :], dst[:, tt, :], bc(ROW(gain), [P, C, D], [1]), ALU.mult))
                        i = v.tensor_tensor(dst[:, tt, :], dst[:, tt, :], bc(ROW(shift), [P, C, D], [1]), ALU.add)
                    if after:
                        link(i)
                        after(t)
                    else:
                        ready(i)

            def ready(i):
                n["tok"] += 1
                i.then_inc(tok_ready, 1)

            def add_out(dst, t, bias, bank=1):
                tt = chunks(t)
                dve.wait_ge(out_mm, 4 * n["out"] + t + 1)
                i = v.tensor_tensor(dst[:, tt, :], dst[:, tt, :],
                                    ps[2 * t + bank][:, :].rearrange("p (c d) -> p c d", c=C), ALU.add)
                link(i)
                if bias:
                    link(v.tensor_tensor(dst[:, tt, :], dst[:, tt, :], bc(ROW(bias), [P, C, D], [1]), ALU.add))

            def prepared(name, k):
                a = ATT[name]
                dve.wait_ge(k_mm, k + 1)
                if k >= 1:
                    dve.wait_ge(kv_ready, k)
                o, i_ = kts[0:a["PD"], 0:B * a["nk"]], ps[0][0:a["PD"], 0:B * a["nk"]]
                b = {"L0": "L0bk", "L3": "L3bk", "CB": "CBbk"}.get(name)
                if b:
                    v.tensor_scalar(o, i_, V(b), None, ALU.add).then_inc(k_sb, 1)
                else:
                    v.tensor_copy(o, i_).then_inc(k_sb, 1)
                dve.wait_ge(v_mm, k + 1)
                RB, PD = a["RB"], a["PD"]
                o = vr[0:RB, :, 0:PD]
                i_ = ps[1][0:RB, 0:B * PD].rearrange("p (b d) -> p b d", b=B)
                b = {"L0": "L0mvb", "L3": "L3vb", "CB": "CBvb"}.get(name)
                if b:
                    v.tensor_tensor(o, i_, bc(ROW(b)[0:RB, :], [RB, B, PD], [1]), ALU.add).then_inc(v_sb, 1)
                else:
                    v.tensor_copy(o, i_).then_inc(v_sb, 1)

            def attend(name):
                a = ATT[name]
                R, H, nu, cpu, PD, dh = (a[i] for i in ("R", "H", "nu", "cpu", "PD", "dh"))
                for u in range(nu):
                    for t in range(B):
                        n["smax"] += 1
                        dve.wait_ge(s_mm, n["smax"])
                        c0 = C * t + u * cpu
                        src = ps[2 * t + u % 2][:, 0:cpu * R].rearrange("p (c h k) -> p c h k", c=cpu, h=H)
                        if name == "L1":
                            if t:
                                dve.wait_ge(s_max, n["smax"] - 1)
                            link(v.tensor_tensor(msc[:, :, :, :], src, bc(madd_t[:, c0:c0 + C, :], [P, C, H, NK], [2]), ALU.add))
                            src = msc[:, :, :, :]
                        v.tensor_reduce(mx[:, c0:c0 + cpu, 0:H], src, AX.X, ALU.max).then_inc(s_max, 1)
                for t in range(B):
                    dve.wait_ge(m_turned, n["mt"] + t + 1)
                    v.tensor_copy(mT[0:H, t, :], ps[2 * t][0:H, :]).then_inc(mT_ready, 1)
                n["mt"] += 4
                wd = PD + H
                for t in range(B):
                    dve.wait_ge(av_mm, n["av"] + t + 1)
                    for j in range(2):
                        s_ = ps[2 * t + j][:, 0:2 * wd].rearrange("p (c w) -> p c w", c=2)
                        i = v.reciprocal(rs[:, C * t + 2 * j:C * t + 2 * j + 2, 0:H], s_[:, :, PD:wd])
                    link(i)
                    for j in range(2):
                        cc = slice(C * t + 2 * j, C * t + 2 * j + 2)
                        s_ = ps[2 * t + j][:, 0:2 * wd].rearrange("p (c w) -> p c w", c=2)
                        o = xn[:, cc, 0:PD].rearrange("p c (h d) -> p c h d", h=H)
                        i = v.tensor_tensor(o, s_[:, :, 0:PD].rearrange("p c (h d) -> p c h d", h=H),
                                            bc(rs[:, cc, 0:H], [P, 2, H, dh], [3]), ALU.mult)
                    ready(i)
                n["av"] += 4

            def first_largest(src, dst):
                nb = B * C
                link(v.tensor_reduce(gm[:, :], src, AX.X, ALU.max))
                link(v.tensor_tensor(ga[:, 0:nb, :], src, bc(gm[:, :], [P, nb, E], [2]), ALU.is_equal))
                link(v.tensor_tensor(ga[:, 0:nb, :], ga[:, 0:nb, :], bc(K("first"), [P, nb, E], [1]), ALU.mult))
                link(v.tensor_reduce(gs[:, :], ga[:, 0:nb, :], AX.X, ALU.max))
                link(v.tensor_tensor(dst, ga[:, 0:nb, :], bc(gs[:, :], [P, nb, E], [2]), ALU.is_equal))

            def kept(m, capacity):
                k = m * B * C
                mine = lambda ap: ap[:, 0:k, :]
                link(v.tensor_copy(mine(gt[:, :, :]), ps[2][:, 0:k * E].rearrange("p (c e) -> p c e", e=E)))
                cur, nxt, s = gt, ga, 1
                while s < k:
                    v.tensor_copy(nxt[:, 0:s, :], cur[:, 0:s, :])
                    link(v.tensor_tensor(nxt[:, s:k, :], cur[:, s:k, :], cur[:, 0:k - s, :], ALU.add))
                    cur, nxt = nxt, cur
                    s *= 2
                link(v.tensor_tensor(mine(cur[:, :, :]), mine(cur[:, :, :]),
                                     ps[2][:, 0:k * E].rearrange("p (c e) -> p c e", e=E), ALU.subtract))
                link(v.tensor_tensor(mine(cur[:, :, :]), mine(cur[:, :, :]),
                                     ps[0][:, 0:k * E].rearrange("p (c e) -> p c e", e=E), ALU.add))
                link(v.tensor_scalar(mine(gt[:, :, :]), mine(cur[:, :, :]), float(capacity), None, ALU.is_le))
                link(v.tensor_tensor(mine(gt[:, :, :]), mine(gt[:, :, :]), mine(oh[:, :, :]), ALU.mult))

            def logits(bias):
                nb = B * C
                for t in range(B):
                    dve.wait_ge(lg_mm, n["lg"] + t + 1)
                    s_ = ps[2 * t + 1][:, 0:C * E].rearrange("p (c e) -> p c e", e=E)
                    if bias:
                        i = v.tensor_tensor(lg[:, chunks(t), :], s_, bc(ROW(bias), [P, C, E], [1]), ALU.add)
                    else:
                        i = v.tensor_copy(lg[:, chunks(t), :], s_)
                link(i)
                n["lg"] += 4

            def two_largest():
                nb = B * C
                first_largest(lg[:, :, :], oh[:, 0:nb, :])
                link(v.scalar_tensor_tensor(out=lg2[:, :, :], in0=oh[:, 0:nb, :], scalar=-BIG, in1=lg[:, :, :],
                                            op0=ALU.mult, op1=ALU.add))
                link(v.tensor_reduce(gm[:, :], lg[:, :, :], AX.X, ALU.max))
                link(v.tensor_tensor(lg[:, :, :], lg[:, :, :], bc(gm[:, :], [P, nb, E], [2]), ALU.subtract))
                first_largest(lg2[:, :, :], oh[:, nb:2 * nb, :])

            def add_bias_rows(k):
                for t in range(B):
                    dve.wait_ge(gb_mm, 4 * (1 if k else 0) + t + 1)
                    i = v.tensor_tensor(x[:, chunks(t), :], x[:, chunks(t), :],
                                        ps[2 * t + 1][:, :].rearrange("p (c d) -> p c d", c=C), ALU.add)
                i.then_inc(y_used, 1)
                n["y"] += 1
                dve.wait_ge(y_used, n["y"])

            def experts(FC):
                for i in range(E * B):
                    e, t = divmod(i, B)
                    dve.wait_ge(y_mm, E * B * n["moe"] + i + 1)
                    if i >= B:
                        dve.wait_ge(y_used, n["y"] - B + 1)
                    for c in range(C):
                        ins_ = v.scalar_tensor_tensor(out=x[:, C * t + c, :], in0=ps[6 + i % 2][:, cols(c)],
                                                      scalar=gate[:, C * t + c, e:e + 1], in1=x[:, C * t + c, :],
                                                      op0=ALU.mult, op1=ALU.add)
                    ins_.then_inc(y_used, 1)
                    n["y"] += 1
                n["moe"] += 1
                dve.wait_ge(y_used, n["y"])

            dve.wait_ge(ld_s, 16 * (8 + 3 * B))
            dve.wait_ge(ld_c, 48)
            v.tensor_scalar(madd_t[:, :, :], mask_tok[:, :, :], -1.0, BIG, ALU.add, ALU.mult)
            v.tensor_scalar(m2c[:, :], mask2c[:, :], -1.0, BIG, ALU.add, ALU.mult)
            v.tensor_scalar(m2r[:, :, :], mask2[:, :, :], -1.0, BIG, ALU.add, ALU.mult)
            v.tensor_scalar(m3c[:, :], mask3c[:, :], -1.0, 1e4, ALU.add, ALU.mult)
            v.tensor_scalar(m3r[:, :, :], mask3[:, :, :], -1.0, 1e4 / ATT["L3"]["scale"], ALU.add, ALU.mult)
            for h in range(2):
                i = v.tensor_copy(rep2[:, h, :], ident[0:NK, 0:NK])
            i.then_inc(masks, 1)
            dve.wait_ge(ld_x, 16)
            for k, name in enumerate(CTX_ATT):
                prepared(name, k)
            dve.wait_ge(dq_mm, 1)
            link(v.tensor_scalar(dqT[:, :], ps[2][:, 0:SLOTS], V("Dbq"), None, ALU.add))
            v.tensor_tensor(qblk[:, :, :], bc(dqT[:, :], [P, SE, SLOTS], [1]), bc(K("CB_dim"), [P, SE, SLOTS], [2]),
                            ALU.mult).then_inc(qblk_ready, 1)
            norms(x, r)
            norms(r, r, "g1", "b1", before=lambda t: add_out(r, t, "so_b", 0))
            n["out"] += 1
            attend("L0")
            norms(r, r, "g2", "b2", before=lambda t: add_out(r, t, "mo_b"))
            n["out"] += 1
            norms(r, r, "g3", "b3", before=lambda t: add_out(r, t, "l2_b"), after=lambda t: link(
                v.tensor_tensor(x[:, chunks(t), :], x[:, chunks(t), :], r[:, chunks(t), :], ALU.add)))
            norms(x, xn)
            n["out"] += 1
            nb = B * C
            logits("sw_b")
            first_largest(lg[:, :, :], oh[:, 0:nb, :])
            v.tensor_copy(oh[0:1, 0, 0:1], oh[0:1, 0, 0:1]).then_inc(oh_ready, 1)
            dve.wait_ge(oh_ready, 1)
            dve.wait_ge(cum_mm, 1)
            kept(1, int(0.5 * B * S / E))
            link(v.tensor_copy(gate[:, :, :], gt[:, 0:nb, :]))
            link(v.tensor_reduce(drop[:, :], gt[:, 0:nb, :], AX.X, ALU.add))
            link(v.tensor_scalar(drop[:, :], drop[:, :], -1.0, 1.0, ALU.mult, ALU.add))
            for c in range(nb):
                i = v.scalar_tensor_tensor(out=x[:, c, :], in0=xn[:, c, :], scalar=drop[:, c:c + 1], in1=x[:, c, :],
                                           op0=ALU.mult, op1=ALU.add)
            i.then_inc(gate_ready, 1)
            dve.wait_ge(gate_ready, 1)
            add_bias_rows(0)
            experts(4)
            v.tensor_scalar(madd_k, mask_key[:, :], -1.0, BIG, ALU.add, ALU.mult).then_inc(masks, 1)
            norms(x, xn)
            attend("L1")
            norms(x, xn, before=lambda t: add_out(x, t, None))
            n["out"] += 1
            for t in range(B):
                dve.wait_ge(dv_mm, t + 1)
                v.tensor_copy(r[:, chunks(t), :], ps[2 * t][:, :].rearrange("p (c d) -> p c d", c=C)).then_inc(dv_sb, 1)
            for g in range(2):
                for t in range(B):
                    dve.wait_ge(ds_mm, 4 * g + t + 1)
                    link(v.tensor_reduce(dm[:, t, g:g + 1], ps[2 * t + 1 - g][:, :], AX.X, ALU.max))
                    v.tensor_scalar(dm[:, t, g:g + 1], dm[:, t, g:g + 1], -ATT["CB"]["scale"], None, ALU.mult).then_inc(dmax, 1)
            for g in range(2):
                for t in range(B):
                    dve.wait_ge(dexp, 4 * g + t + 1)
                    link(v.reciprocal(drs[:, t, g:g + 1], dsum[:, t, g:g + 1]))
                    v.tensor_scalar(big[:, g, t, :], big[:, g, t, :], drs[:, t, g:g + 1], None, ALU.mult).then_inc(dnorm, 1)
            for t in range(B):
                dve.wait_ge(da_mm, t + 1)
                link(v.tensor_tensor(pair[:, :, :], ps[2 * t][:, 0:2 * P].rearrange("p (h s) -> p h s", h=SE),
                                     bc(K("CB_dim"), [P, SE, SLOTS], [2]), ALU.mult))
                a_ = attT[:, SLOTS * t:SLOTS * (t + 1)]
                link(v.tensor_reduce(a_, pair[:, :, :].rearrange("p h s -> p s h"), AX.X, ALU.add))
                v.tensor_scalar(a_, a_, V("Dbv"), None, ALU.add).then_inc(att_ready, 1)
            dve.wait_ge(do_mm, 1)
            nr = B * SLOTS
            link(v.tensor_tensor(orow[:, :], ps[0][0:nr, 0:D], ROW("Dob")[0:nr, :], ALU.add))
            link(v.tensor_tensor(orow[:, :], orow[:, :], sqrow[:, :], ALU.add))
            link(v.bn_stats(st[0:nr, 0, :], orow[:, :]))
            v.bn_aggr(mv[0:nr, 0, :], st[0:nr, 0, :]).then_inc(var_ready, 1)
            n["norm"] += 1
            dve.wait_ge(rstd_ready, n["norm"])
            link(v.tensor_scalar(hrow[:, :], orow[:, :], mv[0:nr, 0, 0:1], rstd[0:nr, 0:1], ALU.subtract, ALU.mult))
            link(v.tensor_tensor(hrow[:, :], hrow[:, :], lng[:, :], ALU.mult))
            v.tensor_tensor(hrow[:, :], hrow[:, :], lnb[:, :], ALU.add).then_inc(h_rows, 1)
            dve.wait_ge(hT_mm, 1)
            v.tensor_copy(oT[:, :, :], ps[2][:, 0:nr].rearrange("p (b s) -> p b s", b=B))
            v.tensor_copy(hT[:, :, :], ps[1][:, 0:nr].rearrange("p (b s) -> p b s", b=B)).then_inc(hT_ready, 1)
            dve.wait_ge(hT_ready, 1)
            for e in range(SE):
                dve.wait_ge(e_mm, e + 1)
                for dst, at, b_ in ((uu, 0, "eb1"), (gg, 16, "ebg")):
                    i = v.tensor_tensor(dst[:, e, :, :], ps[slot_bank(e)][:, at:at + 16].rearrange("p (f b) -> p f b", f=4),
                                        bc(V(b_, 4 * e, 4), [P, 4, B], [2]), ALU.add)
                i.then_inc(e_h, 1)
                dve.wait_ge(e_exp, e + 1)
                link(v.tensor_scalar(eu[:, e, :, :], eu[:, e, :, :], 1.0, None, ALU.add))
                link(v.tensor_scalar(eg[:, e, :, :], eg[:, e, :, :], 1.0, None, ALU.add))
                v.reciprocal(eu[:, e, :, :], eu[:, e, :, :])
                link(v.reciprocal(eg[:, e, :, :], eg[:, e, :, :]))
                v.tensor_tensor(uu[:, e, :, :], uu[:, e, :, :], eu[:, e, :, :], ALU.mult)
                link(v.tensor_tensor(gg[:, e, :, :], gg[:, e, :, :], eg[:, e, :, :], ALU.mult))
                v.tensor_tensor(uu[:, e, :, :], uu[:, e, :, :], gg[:, e, :, :], ALU.mult).then_inc(e_act, 1)
            dve.wait_ge(ey_mm, SE)
            link(v.tensor_tensor(oT[:, :, :], oT[:, :, :],
                                 ps[5][:, 0:4 * SE].rearrange("p (e b) -> p b e", b=B), ALU.add))
            v.tensor_tensor(oT[:, :, :], oT[:, :, :], bc(V("eb2", 0, SE), [P, B, SLOTS], [1]), ALU.add).then_inc(oT_ready, 1)
            prepared("CB", 3)
            attend("CB")
            norms(x, xn, before=lambda t: add_out(x, t, "CBob"))
            n["out"] += 1
            prepared("L3", 4)
            attend("L2")
            norms(x, xn, before=lambda t: add_out(x, t, None))
            n["out"] += 1
            logits(None)
            two_largest()
            link(v.tensor_tensor(lg2[:, :, :], oh[:, 0:nb, :], oh[:, nb:2 * nb, :], ALU.add))
            v.tensor_copy(gb[:, 0:nb, :], lg[:, :, :]).then_inc(gate_e, 1)
            dve.wait_ge(gate_ep, 1)
            link(v.tensor_tensor(lg2[:, :, :], lg2[:, :, :], ga[:, 0:nb, :], ALU.mult))
            link(v.tensor_reduce(gs[:, :], lg2[:, :, :], AX.X, ALU.add))
            link(v.reciprocal(gs[:, :], gs[:, :]))
            v.tensor_tensor(lg2[:, :, :], lg2[:, :, :], bc(gs[:, :], [P, nb, E], [2]), ALU.mult).then_inc(oh_ready, 1)
            dve.wait_ge(oh_ready, 2)
            dve.wait_ge(cum_mm, 2)
            kept(2, CAP2)
            link(v.tensor_tensor(gt[:, 0:nb, :], gt[:, 0:nb, :], gt[:, nb:2 * nb, :], ALU.add))
            v.tensor_tensor(gate[:, :, :], gt[:, 0:nb, :], lg2[:, :, :], ALU.mult).then_inc(gate_ready, 1)
            dve.wait_ge(gate_ready, 2)
            experts(4)
            norms(x, xn)
            attend("L3")
            norms(x, xn, before=lambda t: add_out(x, t, "L3ob"))
            n["out"] += 1
            logits(None)
            two_largest()
            link(v.tensor_tensor(lg2[:, :, :], oh[:, 0:nb, :], oh[:, nb:2 * nb, :], ALU.add))
            v.tensor_copy(gb[:, 0:nb, :], lg[:, :, :]).then_inc(gate_e, 1)
            dve.wait_ge(gate_ep, 2)
            link(v.tensor_reduce(gs[:, :], ga[:, 0:nb, :], AX.X, ALU.add))
            link(v.reciprocal(gs[:, :], gs[:, :]))
            link(v.tensor_tensor(ga[:, 0:nb, :], ga[:, 0:nb, :], bc(gs[:, :], [P, nb, E], [2]), ALU.mult))
            link(v.tensor_tensor(lg2[:, :, :], lg2[:, :, :], ga[:, 0:nb, :], ALU.mult))
            link(v.tensor_reduce(gs[:, :], lg2[:, :, :], AX.X, ALU.add))
            link(v.tensor_scalar(gs[:, :], gs[:, :], 1e-9, None, ALU.add))
            link(v.reciprocal(gs[:, :], gs[:, :]))
            v.tensor_tensor(gate[:, :, :], lg2[:, :, :], bc(gs[:, :], [P, nb, E], [2]), ALU.mult).then_inc(gate_ready, 1)
            dve.wait_ge(gate_ready, 3)
            add_bias_rows(2)
            experts(2)

        @block.gpsimd
        def _(pool):
            g_ = nc.gpsimd

            def prepare(name, k, keys):
                a = ATT[name]
                PD, H, nk, RB, G, hb, dh = (a[i] for i in ("PD", "H", "nk", "RB", "G", "hb", "dh"))
                if k >= 1:
                    pool.wait_ge(v_mm, k)
                g_.tensor_copy(rep[:, :, 0:RB].rearrange("p b (h k) -> p b h k", h=hb),
                               bc(keys, [P, B, hb, nk], [2])).then_inc(kv_rep, 1)
                pool.wait_ge(k_sb, k + 1)
                for b in range(B):
                    g_.tensor_tensor(KB[name][0:PD, b, :].rearrange("p (h k) -> p h k", h=H),
                                     bc(kts[0:PD, b * nk:(b + 1) * nk], [PD, H, nk], [1]),
                                     bc(K(name + "_dim")[0:PD, :], [PD, H, nk], [2]), ALU.mult)
                pool.wait_ge(v_sb, k + 1)
                sel = K(name + "_sel")[0:RB, :].rearrange("p (g h) -> p g h", g=G)
                for b in range(B):
                    for g in range(G):
                        g_.tensor_tensor(VB[name][0:RB, b, g, 0:PD].rearrange("p (h d) -> p h d", h=H),
                                         vr[0:RB, b, 0:PD].rearrange("p (h d) -> p h d", h=H),
                                         bc(sel[:, g, :], [RB, H, dh], [2]), ALU.mult)
                i = g_.tensor_copy(VB[name][0:RB, :, :, PD:PD + H], bc(sel, [RB, B, G, H], [1]))
                i.then_inc(kv_ready, 1)

            n = dict(norm=0)

            def rstds(times=1, rows=P, tiles=B, width=C):
                for _ in range(times):
                    for t in range(tiles):
                        tt = slice(C * t, C * t + width)
                        n["norm"] += 1
                        pool.wait_ge(var_ready, n["norm"])
                        g_.tensor_scalar(rstd[0:rows, tt], mv[0:rows, tt, 1], EPS, None, ALU.add).then_inc(pool_chain, 1)
                        pool.wait_ge(pool_chain, n["norm"])
                        g_.tensor_tensor(rstd[0:rows, tt], rstd[0:rows, tt], half[0:rows, 0:width], ALU.pow).then_inc(rstd_ready, 1)

            g_.memset(half[:, :], -0.5).then_inc(minus_half, 1)
            pool.wait_ge(minus_half, 1)
            pool.wait_ge(ld_c, 48)
            for k, name in enumerate(CTX_ATT):
                prepare(name, k, V("ctxT", 0, B * NK).rearrange("p (b k) -> p b k", b=B))
            rstds(7)
            rstds(1, rows=B * SLOTS, tiles=1, width=1)
            pool.wait_ge(oT_ready, 1)
            prepare("CB", 3, oT[:, :, :])
            rstds(1)
            prepare("L3", 4, V("ctxT", 0, B * NK).rearrange("p (b k) -> p b k", b=B))
            rstds(3)


CAP2 = int(2 * 1.25 * B * S / E)
CAP2 += CAP2 % 2


def kernel(**inputs):
    import concourse.bacc as _bacc
    from concourse.bass_utils import run_bass_kernel_spmd as _run

    i = {k: np.asarray(v) for k, v in inputs.items()}
    T = lambda a: a.T
    rows_of = lambda a: np.concatenate([a[j * P:(j + 1) * P] for j in range(a.shape[0] // P)], axis=1)
    qkv, inp = i["L0_xattn_qkv_w"], i["L0_xattn_in_proj_w"]
    wkv = i["L1_xattn_Wkv"]
    squares = {
        "L0v": T(qkv[256:384]), "L0so": T(i["L0_xattn_sa_out_w"]), "L0q": T(inp[0:128]), "L0k": T(inp[128:256]),
        "L0mv": T(inp[256:384]), "L0o": T(i["L0_xattn_mha_out_w"]), "L0l1": T(i["L0_xattn_lin1_w"]),
        "L0l2": rows_of(T(i["L0_xattn_lin2_w"])),
        "L1q": i["L1_xattn_Wq"], "L1k": wkv[:, 0:128], "L1v": wkv[:, 128:256], "L1o": i["L1_xattn_Wo"],
        "L2q": T(i["L2_xattn_Wq"]), "L2k": T(i["L2_xattn_Wk"]), "L2v": T(i["L2_xattn_Wv"]),
        "L3q": T(i["L3_xattn_wq"]), "L3k": T(i["L3_xattn_wk"]), "L3v": T(i["L3_xattn_wv"]), "L3o": T(i["L3_xattn_wo"]),
        "Dq": i["L1_ffn_d_Wq"], "Dk": i["L1_ffn_d_Wk"], "Dv": i["L1_ffn_d_Wv"], "Do": i["L1_ffn_d_Wo"],
        "CBq": i["L1_ffn_c_Wq"], "CBk": i["L1_ffn_c_Wk"], "CBv": i["L1_ffn_c_Wv"], "CBo": i["L1_ffn_c_Wo"],
        "wr0": i["L0_ffn_w_switch"], "wr2": i["L2_ffn_w_g"], "wr3": T(i["L3_ffn_router_w"]),
    }
    on_p = lambda a: a.reshape(-1, P).T
    ib = i["L0_xattn_in_proj_b"]
    columns = {
        "L0bv": on_p(i["L0_xattn_qkv_b"][256:384]), "L0bq": on_p(ib[0:128]), "L0bk": on_p(ib[128:256]),
        "L0bl1": on_p(i["L0_xattn_lin1_b"]), "L3bq": on_p(i["L3_xattn_bq"]), "L3bk": on_p(i["L3_xattn_bk"]),
        "Dbq": on_p(i["L1_ffn_d_bq"]), "Dbk": on_p(i["L1_ffn_d_bk"]), "Dbv": on_p(i["L1_ffn_d_bv"]),
        "CBbq": on_p(i["L1_ffn_c_bq"]), "CBbk": on_p(i["L1_ffn_c_bk"]),
        "m0b1": on_p(i["L0_ffn_b1"]), "m3b1": on_p(i["L3_ffn_b1"]),
        "eb1": on_p(i["L1_ffn_e_b1"]), "ebg": on_p(i["L1_ffn_e_bg"]), "eb2": T(i["L1_ffn_e_b2"]),
        "sqT": T(i["L1_ffn_slot_query"][0]), "ctxT": T(i["ctx_1024"].reshape(B * NK, D)),
    }
    rows = {
        "so_b": i["L0_xattn_sa_out_b"], "g1": i["L0_xattn_ln1_g"], "b1": i["L0_xattn_ln1_b"],
        "mo_b": i["L0_xattn_mha_out_b"], "g2": i["L0_xattn_ln2_g"], "b2": i["L0_xattn_ln2_b"],
        "l2_b": i["L0_xattn_lin2_b"], "g3": i["L0_xattn_ln3_g"], "b3": i["L0_xattn_ln3_b"],
        "L0mvb": ib[256:384], "L3vb": i["L3_xattn_bv"], "L3ob": i["L3_xattn_bo"],
        "CBvb": i["L1_ffn_c_bv"], "CBob": i["L1_ffn_c_bo"], "Dob": i["L1_ffn_d_bo"], "sw_b": i["L0_ffn_b_switch"],
    }
    bits = lambda a: a.view(np.uint8)
    m3 = i["mask_BxS2_ff1"]
    given = {
        "x": i["x"], "con": constants(),
        "sq": np.concatenate([squares[k] for k, _ in SQUARES], axis=1), "wout2": T(i["L2_xattn_Wout"]),
        "col": np.concatenate([columns[k] for k, _ in COLUMNS], axis=1),
        "row": np.concatenate([rows[k] for k, _ in ROWS])[None, :],
        "mask": bits(i["mask_BxSxS2_bf1"]),
        "maskT": bits(np.ascontiguousarray(i["mask_BxSxS2_bf1"].transpose(2, 0, 1).reshape(NK, B * S))),
        "mask2": bits(i["mask_BxS2_bf1"].reshape(1, B * NK)), "mask2c": bits(np.ascontiguousarray(i["mask_BxS2_bf1"].T)),
        "mask3": m3.reshape(1, B * NK), "mask3c": np.concatenate([m3.T] * 4, axis=0),
        "m0b2": i["L0_ffn_b2"], "m3b2": i["L3_ffn_b2"],
        "sqrow": i["L1_ffn_slot_query"][0], "lng": i["L1_ffn_e_ln_g"], "lnb": i["L1_ffn_e_ln_b"],
        "m0w1": i["L0_ffn_w1"], "m0w2": i["L0_ffn_w2"], "m2w1": i["L2_ffn_c_fc"], "m2w2": i["L2_ffn_c_proj"],
        "m3w1": i["L3_ffn_w1"], "m3w2": i["L3_ffn_w2"],
        "ew1": i["L1_ffn_e_W1"], "ewg": i["L1_ffn_e_Wg"], "ew2": i["L1_ffn_e_W2"],
    }
    nc = _bacc.Bacc("TRN2", target_bir_lowering=False, num_devices=1)
    arrays, ins = {}, {}
    for name, a in given.items():
        a = np.ascontiguousarray(a)
        arrays[f"in_{name}"] = a
        ins[name] = nc.dram_tensor(f"in_{name}", a.shape, mybir.dt.from_np(a.dtype), kind="ExternalInput").ap()
    out = nc.dram_tensor("out_x", (B, S, D), F32, kind="ExternalOutput").ap()
    build(nc, ins, out)
    got = _run(nc, [arrays], core_ids=[0])
    return got.results[0]["out_x"]
```

```python
from contextlib import ExitStack

import numpy as np

import concourse.bass as bass
from concourse import mybir

ALU = mybir.AluOpType
ACT = mybir.ActivationFunctionType
AX = mybir.AxisListType
F32 = mybir.dt.float32
BF16 = mybir.dt.bfloat16
U8 = mybir.dt.uint8
U32 = mybir.dt.uint32

P = 128
B = 4
S = 512
D = 128
NK = 32
C = S // P
E = 8
SE = 16
SLOTS = 16
EPS = 1e-5
CAP0 = int(0.5 * B * S / E)
CAP2 = int(2 * 1.25 * B * S / E)
CAP2 += CAP2 % 2
SKIP = 1e6
BIG = 1e30

ATT = {
    "L0": dict(H=8, nk=NK, dh=16, scale=16 ** -0.5),
    "L1": dict(H=2, nk=NK, dh=64, scale=64 ** -0.5),
    "CB": dict(H=16, nk=SLOTS, dh=8, scale=8 ** -0.5),
    "L2": dict(H=1, nk=NK, dh=64, scale=64 ** -0.5),
    "L3": dict(H=16, nk=NK, dh=8, scale=8 ** -0.5),
}
for _a in ATT.values():
    _a["PD"] = _a["H"] * _a["dh"]
    _a["R"] = _a["H"] * _a["nk"]
    _a["RB"] = min(P, _a["R"])
    _a["G"] = _a["R"] // _a["RB"]
    _a["hb"] = _a["RB"] // _a["nk"]
    _a["cpu"] = min(C, 512 // _a["R"])
    _a["nu"] = C // _a["cpu"]

SQUARES = [("L0v", 128), ("L0so", 128), ("L0q", 128), ("L0k", 128), ("L0mv", 128), ("L0o", 128),
           ("L0l1", 512), ("L0l2", 512),
           ("L1q", 128), ("L1k", 128), ("L1v", 128), ("L1o", 128),
           ("L2q", 64), ("L2k", 64), ("L2v", 64),
           ("L3q", 128), ("L3k", 128), ("L3v", 128), ("L3o", 128),
           ("Dq", 128), ("Dk", 128), ("Dv", 128), ("Do", 128),
           ("CBq", 128), ("CBk", 128), ("CBv", 128), ("CBo", 128),
           ("wr0", 8), ("wr2", 8), ("wr3", 8)]
COLUMNS = [("L0bv", 1), ("L0bq", 1), ("L0bk", 1), ("L0bl1", 4), ("L3bq", 1), ("L3bk", 1),
           ("Dbq", 1), ("Dbk", 1), ("Dbv", 1), ("CBbq", 1), ("CBbk", 1),
           ("m0b1", 32), ("m3b1", 16), ("eb1", 64), ("ebg", 64), ("eb2", 16), ("sqT", 16),
           ("ctxT", 128)]
ROWS = [("so_b", 128), ("g1", 128), ("b1", 128), ("mo_b", 128), ("g2", 128), ("b2", 128),
        ("l2_b", 128), ("g3", 128), ("b3", 128), ("L0mvb", 128), ("L3vb", 128), ("L3ob", 128),
        ("CBvb", 128), ("CBob", 128), ("Dob", 128), ("sw_b", 8)]
CONSTS = [("ident", 128), ("tri", 128), ("ones", 128), ("first", 8), ("base0", 8), ("base2", 8)]
for _n, _a in ATT.items():
    CONSTS += [(_n + "_dim", _a["H"]), (_n + "_sel", _a["G"] * _a["H"]), (_n + "_neg", _a["R"])]


def places(fields):
    at, out = 0, {}
    for name, n in fields:
        out[name] = (at, at + n)
        at += n
    return out, at


SQ_AT, SQ_N = places(SQUARES)
COL_AT, COL_N = places(COLUMNS)
ROW_AT, ROW_N = places(ROWS)
CON_AT, CON_N = places(CONSTS)


def constants():
    out = np.zeros((P, CON_N), np.float32)
    p = np.arange(P)
    out[:, slice(*CON_AT["ident"])] = np.eye(P)
    out[:, slice(*CON_AT["tri"])] = p[:, None] <= p[None, :]
    out[:, slice(*CON_AT["ones"])] = 1.0
    out[:, slice(*CON_AT["first"])] = E - np.arange(E)
    out[:, slice(*CON_AT["base0"])] = CAP0 * np.arange(E) - 1
    out[:, slice(*CON_AT["base2"])] = CAP2 * np.arange(E) - 1
    for n, a in ATT.items():
        h = np.arange(a["H"])
        out[:, slice(*CON_AT[n + "_dim"])] = (p[:, None] // a["dh"]) == h
        sel = np.zeros((P, a["G"], a["H"]), np.float32)
        for g in range(a["G"]):
            sel[:, g, :] = (g * a["hb"] + p[:, None] // a["nk"]) == h
        sel[a["RB"]:] = 0
        out[:, slice(*CON_AT[n + "_sel"])] = sel.reshape(P, -1)
        neg = np.zeros((P, a["R"]), np.float32)
        neg[:a["H"]] = np.where(np.arange(a["R"])[None, :] // a["nk"] == h[:, None], -1.0, 0.0)
        out[:, slice(*CON_AT[n + "_neg"])] = neg
    return out


def build(nc, ins, out):
    ctx = ExitStack()
    with ctx:
        def sb(name, shape, dt=F32):
            return ctx.enter_context(nc.sbuf_tensor(name, shape, dt))

        def sem(name):
            return ctx.enter_context(nc.semaphore(name))

        x = sb("x", [P, B * C, D])
        r = sb("r", [P, B * C, D])
        xn = sb("xn", [P, B * C, D])
        xT = sb("xT", [P, B, S])
        qT = sb("qT", [P, B, S])
        mT = xn[0:16, :, :].rearrange("p (b c) d -> p b (c d)", b=B)
        big = sb("big", [P, 4, B, S])
        sq = sb("sq", [P, SQ_N])
        wout2 = sb("wout2", [64, D])
        col = sb("col", [P, COL_N])
        row = sb("row", [P, ROW_N])
        con = sb("con", [P, CON_N])
        mask_tok = sb("mask_tok", [P, B * C, NK], U8)
        mask_key = sb("mask_key", [NK, B * S], U8)
        mask2 = sb("mask2", [P, B, NK], U8)
        mask2c = sb("mask2c", [NK, B], U8)
        mask3 = sb("mask3", [P, B, NK])
        mask3c = sb("mask3c", [P, B])
        b2m0 = sb("b2m0", [E, D])
        b2m3 = sb("b2m3", [E, D])
        moe_w = sb("moe_w", [P, E, 1024])
        RING = 5
        SLOT_BUFS = 10
        ring = sb("ring", [P, RING, 3 * 512])
        sqrow = sb("sqrow", [B * SLOTS, D])
        lng = sb("lng", [B * SLOTS, D])
        lnb = sb("lnb", [B * SLOTS, D])
        KB, VB, KTs, REP, VR = {}, {}, {}, {}, {}
        for n, a in ATT.items():
            if n == "CB":
                continue
            if n != "L3":
                KB[n] = sb("kb_" + n, [P, B, a["R"]])
            if n != "L3":
                VB[n] = sb("vb_" + n, [P, B, a["G"], P + 16 if n == "L0" else a["PD"] + a["H"]])
        KB["CB"] = KB["L0"]
        VB["CB"] = VB["L0"]
        ring_flat = ring[:, :, :].rearrange("p a b -> p (a b)")
        w3 = ring_flat[:, 0:E * 512].rearrange("p (e n) -> p e n", e=E)
        VB["L3"] = ring_flat[:, E * 512:E * 512 + B * 4 * 144].rearrange("p (b g w) -> p b g w", b=B, g=4)
        KB["L3"] = r[:, :, :].rearrange("p (b c) d -> p b (c d)", b=B)
        kts = sb("kts", [P, B * NK])
        rep = sb("rep", [P, B, P])
        vr = sb("vr", [P, B, D])
        st = sb("st", [P, B * C, 6])
        mv = sb("mv", [P, B * C, 2])
        rstd = sb("rstd", [P, B * C])
        half = sb("half", [P, C])
        mx = sb("mx", [P, B * C, 16])
        rs = sb("rs", [P, B * C, 16])
        msc = sb("msc", [P, C, 2, NK])
        madd_t = sb("madd_t", [P, B * C, NK])
        madd_k = r[0:NK, :, :].rearrange("p a b -> p (a b)")
        m2c = sb("m2c", [NK, B])
        m2r = sb("m2r", [P, B, NK])
        m3c = sb("m3c", [P, B])
        m3r = sb("m3r", [P, B, NK])
        rep2 = sb("rep2", [NK, 2, NK])
        lg = sb("lg", [P, B * C, E])
        lg2 = sb("lg2", [P, B * C, E])
        ga = sb("ga", [P, 2 * B * C, E])
        gb = sb("gb", [P, 2 * B * C, E])
        gt = sb("gt", [P, 2 * B * C, E])
        oh = sb("oh", [P, 2 * B * C, E])
        gm = sb("gm", [P, B * C])
        gs = sb("gs", [P, B * C])
        gate = sb("gate", [P, B * C, E])
        slot = sb("slot", [P, 2 * B * C])
        have = sb("have", [P, 2 * B * C])
        wgt = sb("wgt", [P, 2 * B * C])
        to_slot = sb("to_slot", [P, 2 * B * C], U32)
        at_slot = sb("at_slot", [P, 2 * B * C], U32)
        zero = sb("zero", [P, D])
        drop = sb("drop", [P, B * C])
        gateT = qT[0:E, :, :]
        qblk = sb("qblk", [P, SE, SLOTS])
        dqT = sb("dqT", [P, SLOTS])
        dm = sb("dm", [P, B, 2])
        dsum = sb("dsum", [P, B, 2])
        drs = sb("drs", [P, B, 2])
        pair = sb("pair", [P, SE, SLOTS])
        attT = sb("attT", [P, B * SLOTS])
        orow = sb("orow", [B * SLOTS, D])
        hrow = sb("hrow", [B * SLOTS, D])
        hT = sb("hT", [P, B, SLOTS])
        oT = sb("oT", [P, B, SLOTS])
        uu, gg, eu, eg = (big[:, 0, 0, 256 * j:256 * j + 256].rearrange(
            "p (e f b) -> p e f b", e=SE, f=4) if j < 2 else
            big[:, 0, 1, 256 * (j - 2):256 * (j - 1)].rearrange("p (e f b) -> p e f b", e=SE, f=4)
            for j in range(4))
        flat = big[:, :, :, :].rearrange("p a b n -> p (a b n)")
        xg = flat[:, 0:1280].rearrange("p (g n) -> p g n", g=2)
        xgT = flat[:, 1280:2560].rearrange("p (g n) -> p g n", g=2)
        hid = flat[:, 2560:7680].rearrange("p (g f n) -> p g f n", g=2, f=4)
        yg = flat[:, 0:4096].rearrange("p (k c d) -> p k c d", k=2, c=B * C)
        ysb = qT[:, :, :].rearrange("p a b -> p (a b)")[:, 0:1280].rearrange("p (g n) -> p g n", g=2)
        tok_d = {"m0": nc.dram_tensor("tok0", (E * CAP0, D), F32, kind="Internal").ap(),
                 "m2": nc.dram_tensor("tok2", (E * CAP2, D), F32, kind="Internal").ap()}
        res_d = {"m0": nc.dram_tensor("res0", (E * CAP0, D), F32, kind="Internal").ap(),
                 "m2": nc.dram_tensor("res2", (E * CAP2, D), F32, kind="Internal").ap()}
        ps = [ctx.enter_context(nc.psum_tensor(f"ps{i}", [P, 512], F32)) for i in range(8)]

        ld_w = sem("ld_w")
        ld_w2 = sem("ld_w2")
        ld_c = sem("ld_c")
        ld_x = sem("ld_x")
        ld_s = sem("ld_s")
        ld_m0 = sem("ld_m0")
        ld_m2 = sem("ld_m2")
        ld_m3 = sem("ld_m3")
        ld_e = [sem(f"ld_e{i}") for i in range(SLOT_BUFS)]
        zeroed, cleared = sem("zeroed"), sem("cleared")
        idx_ready, sent = sem("idx_ready"), sem("sent")
        g_ld = [sem("g_ld0"), sem("g_ld1")]
        gT_m, gT_s = sem("gT_m"), sem("gT_s")
        gy_mm, gy_sb = sem("gy_mm"), sem("gy_sb")
        gy_st = [sem("gy_st0"), sem("gy_st1")]
        back = [sem(f"back{t}") for t in range(B)]
        stored = sem("stored")
        dve_chain, pool_chain = sem("dve_chain"), sem("pool_chain")
        masks, minus_half = sem("masks"), sem("minus_half")
        var_ready, rstd_ready = sem("var_ready"), sem("rstd_ready")
        tok_ready, turned, xT_ready = sem("tok_ready"), sem("turned"), sem("xT_ready")
        proj_mm, proj_ready = sem("proj_mm"), sem("proj_ready")
        out_mm = sem("out_mm")
        kv_rep, k_mm, k_sb, v_mm, v_sb, kv_ready = (sem(n) for n in ("kv_rep", "k_mm", "k_sb", "v_mm", "v_sb", "kv_ready"))
        s_mm, s_max, m_turned, mT_ready = sem("s_mm"), sem("s_max"), sem("m_turned"), sem("mT_ready")
        sT_mm, probs = sem("sT_mm"), sem("probs")
        av_mm = sem("av_mm")
        h_mm, h_act, y_mm, y_used = sem("h_mm"), sem("h_act"), sem("y_mm"), sem("y_used")
        lg_mm, oh_ready, cum_mm = sem("lg_mm"), sem("oh_ready"), sem("cum_mm")
        gate_e, gate_ep, gate_ready, gT_mm, gT_sb, gb_mm = (sem(n) for n in ("gate_e", "gate_ep", "gate_ready", "gT_mm", "gT_sb", "gb_mm"))
        dq_mm, qblk_ready, dv_mm, dv_sb, ds_mm, dmax, dexp, dnorm, dp_mm, dp_sb, da_mm, att_ready = (
            sem(n) for n in ("dq_mm", "qblk_ready", "dv_mm", "dv_sb", "ds_mm", "dmax", "dexp", "dnorm",
                             "dp_mm", "dp_sb", "da_mm", "att_ready"))
        do_mm, h_rows, hT_mm, hT_ready, e_mm, e_h, e_exp, e_act, ey_mm, oT_ready = (
            sem(n) for n in ("do_mm", "h_rows", "hT_mm", "hT_ready", "e_mm", "e_h", "e_exp", "e_act", "ey_mm", "oT_ready"))

        def W(name):
            return sq[:, slice(*SQ_AT[name])]

        def V(name, i=0, n=None):
            lo, hi = COL_AT[name]
            return col[:, lo + i:lo + i + (n or 1)]

        def ROW(name):
            return row[:, slice(*ROW_AT[name])]

        def K(name):
            return con[:, slice(*CON_AT[name])]

        ident = K("ident")

        def bc(ap, shape, axes):
            for i in axes:
                ap = ap.unsqueeze(i)
            return ap.to_broadcast(shape)

        units0 = {"m0": 4 * B}
        units0["m2"] = units0["m0"] + 4 * E
        cols = lambda c: slice(P * c, P * c + P)
        CTX_ATT = ["L0", "L1", "L2"]
        block = ctx.enter_context(nc.Block())

        def slot_w(e):
            i = e % SLOT_BUFS
            return ring[:, i, :] if i < RING else moe_w[:, :, :].rearrange("p a b -> p (a b)")[:, 1536 * (i - RING):1536 * (i - RING + 1)]

        PLACED = {"m0": dict(cap=CAP0, eg=4, ranks=1), "m2": dict(cap=CAP2, eg=1, ranks=2)}
        for a in PLACED.values():
            a["nb"] = a["cap"] // P
            a["groups"] = E // a["eg"]
            a["gb"] = a["nb"] * a["eg"]
            a["pieces"] = 1 if a["cap"] <= 512 else 2
            a["N"] = a["cap"] // a["pieces"]

        def probs_T(t, c):
            return big[:, 2:4, t, :].rearrange("p g (c n) -> p g c n", c=C)[:, :, c, :]

        def moe_load(sp, name, w, F, done):
            for e in range(E):
                sp.dma_start(w[:, e, 0:F], ins[name + "w1"][e]).then_inc(done, 16)
                sp.dma_start(w[:, e, F:2 * F].rearrange("p (c n) -> p c n", n=D),
                             ins[name + "w2"][e].rearrange("(c p) n -> p c n", p=P)).then_inc(done, 16)

        @block.sync
        def _(sp):
            sp.dma_start(x[:, :, :], ins["x"].rearrange("b (c p) d -> p (b c) d", p=P)).then_inc(ld_x, 16)
            sp.dma_start(con[:, :], ins["con"]).then_inc(ld_c, 16)
            sp.wait_ge(zeroed, 1)
            for name, a in PLACED.items():
                nb = E * a["nb"]
                sp.dma_start(tok_d[name].rearrange("(p b) d -> p b d", b=nb), bc(zero[:, :], [P, nb, D], [1])).then_inc(cleared, 16)
            sp.dma_start(col[:, :], ins["col"]).then_inc(ld_c, 16)
            sp.dma_start(row[:, :], ins["row"].to_broadcast([P, ROW_N])).then_inc(ld_c, 16)
            sp.dma_start(sq[:, :], ins["sq"]).then_inc(ld_w, 16)
            sp.dma_start(wout2[:, :], ins["wout2"]).then_inc(ld_w, 16)
            sp.dma_start(mask_tok[:, :, :], ins["mask"].rearrange("b (c p) k -> p (b c) k", p=P)).then_inc(ld_s, 16)
            sp.dma_start(mask_key[:, :], ins["maskT"]).then_inc(ld_s, 16)
            sp.dma_start(mask2[:, :, :], ins["mask2"].to_broadcast([P, B * NK]).rearrange("p (b k) -> p b k", b=B)).then_inc(ld_s, 16)
            sp.dma_start(mask2c[:, :], ins["mask2c"]).then_inc(ld_s, 16)
            sp.dma_start(mask3[:, :, :], ins["mask3"].to_broadcast([P, B * NK]).rearrange("p (b k) -> p b k", b=B)).then_inc(ld_s, 16)
            sp.dma_start(mask3c[:, :], ins["mask3c"]).then_inc(ld_s, 16)
            sp.dma_start(b2m0[:, :], ins["m0b2"]).then_inc(ld_s, 16)
            sp.dma_start(b2m3[:, :], ins["m3b2"]).then_inc(ld_s, 16)
            for b in range(B):
                rows = slice(b * SLOTS, (b + 1) * SLOTS)
                sp.dma_start(sqrow[rows, :], ins["sqrow"]).then_inc(ld_s, 16)
                sp.dma_start(lng[rows, :], ins["lng"]).then_inc(ld_s, 16)
                sp.dma_start(lnb[rows, :], ins["lnb"]).then_inc(ld_s, 16)
            moe_load(sp, "m0", moe_w, 512, ld_m0)

            def expert_load(e):
                w, done = slot_w(e), ld_e[e % SLOT_BUFS]
                sp.dma_start(w[:, 0:512], ins["ew1"][e]).then_inc(done, 16)
                sp.dma_start(w[:, 512:1024], ins["ewg"][e]).then_inc(done, 16)
                sp.dma_start(w[:, 1024:1536].rearrange("p (c n) -> p c n", c=4),
                             ins["ew2"][e].rearrange("(c p) n -> p c n", p=P)).then_inc(done, 16)

            def placed_traffic(name, k):
                a = PLACED[name]
                g0 = 0 if name == "m0" else PLACED["m0"]["groups"]
                sp.wait_ge(sent, 16 * B * C * (1 if name == "m0" else 3))

                def load(g):
                    i = g0 + g
                    if g >= 2:
                        sp.wait_ge(gT_m, i - 1)
                    rows = slice(g * a["gb"] * P, (g + 1) * a["gb"] * P)
                    sp.dma_start(xg[:, g % 2, 0:a["gb"] * D].rearrange("p (b d) -> p b d", d=D),
                                 tok_d[name][rows, :].rearrange("(b p) d -> p b d", p=P)).then_inc(g_ld[g % 2], 16)
                for g in range(min(3, a["groups"])):
                    load(g)
                for e in range(E):
                    if e + 3 < a["groups"]:
                        load(e + 3)
                    sp.wait_ge(gy_sb, k * E + e + 1)
                    rows = slice(e * a["cap"], (e + 1) * a["cap"])
                    sp.dma_start(res_d[name][rows, :].rearrange("(b p) d -> p b d", p=P),
                                 ysb[:, e % 2, 0:a["nb"] * D].rearrange("p (b d) -> p b d", d=D)).then_inc(gy_st[e % 2], 16)
            for e in range(RING):
                expert_load(e)
            placed_traffic("m0", 0)
            for e in range(RING, SLOT_BUFS):
                expert_load(e)
            for e in range(SLOT_BUFS, SE):
                sp.wait_ge(ey_mm, (e - SLOT_BUFS) // 4 + 1)
                expert_load(e)
            sp.wait_ge(ey_mm, SE // 4)
            moe_load(sp, "m2", moe_w, 512, ld_m2)
            moe_load(sp, "m3", w3, 256, ld_m3)
            placed_traffic("m2", 1)
            for t in range(B):
                sp.wait_ge(y_used, E * B + 1 - B + t + 1)
                sp.dma_start(out[t].rearrange("(c p) d -> p c d", p=P), x[:, C * t:C * t + C, :]).then_inc(stored, 16)
            sp.wait_ge(stored, 16 * B)

        @block.tensor
        def _(pe):
            mm = nc.tensor.matmul
            n = dict(turn=0, proj=0, out=0, smax=0, mt=0, sT=0, av=0, kv=0, h=0, oh=0, g=0)

            def turn(src, width=D):
                k = n["turn"]
                for t in range(B):
                    pe.wait_ge(tok_ready, 4 * k + t + 1)
                    for c in range(C):
                        last = nc.tensor.transpose(ps[2 * t][0:width, cols(c)], src[:, C * t + c, 0:width], ident)
                    last.then_inc(turned, 1)
                n["turn"] += 1

            def need_xT(t):
                pe.wait_ge(xT_ready, 4 * (n["turn"] - 1) + t + 1)

            def project(w, width=D):
                for t in range(B):
                    need_xT(t)
                    mm(ps[2 * t + 1][0:width, :], w, xT[:, t, :], start=True, stop=True).then_inc(proj_mm, 1)
                n["proj"] += 1

            def need_proj(t):
                pe.wait_ge(proj_ready, 4 * (n["proj"] - 1) + t + 1)

            def out_tokens(src, w, bank=1):
                for t in range(B):
                    if src is qT:
                        need_proj(t)
                    else:
                        need_xT(t)
                    width = w.shape[0]
                    for c in range(C):
                        last = mm(ps[2 * t + bank][:, cols(c)], src[0:width, t, cols(c)], w, start=True, stop=True)
                    last.then_inc(out_mm, 1)
                n["out"] += 1

            def prepare(name, keys):
                a = ATT[name]
                k = n["kv"]
                pe.wait_ge(kv_rep, k + 1)
                mm(ps[0][0:a["PD"], 0:B * a["nk"]], W(name + "k") if name != "L0" else W("L0k"), keys,
                   start=True, stop=True).then_inc(k_mm, 1)
                wv = W("L0mv") if name == "L0" else W(name + "v")
                for b in range(B):
                    last = mm(ps[1][0:a["RB"], b * a["PD"]:(b + 1) * a["PD"]], rep[:, b, 0:a["RB"]], wv,
                              start=True, stop=True)
                last.then_inc(v_mm, 1)
                n["kv"] += 1
                pe.wait_ge(k_sb, n["kv"])
                pe.wait_ge(v_sb, n["kv"])

            def attend(name):
                a = ATT[name]
                R, RB, G, H, nu, cpu, PD = (a[i] for i in ("R", "RB", "G", "H", "nu", "cpu", "PD"))
                kb, vb = KB[name], VB[name]
                pe.wait_ge(kv_ready, {"L0": 1, "L1": 2, "L2": 3, "CB": 4, "L3": 5}[name])
                if name == "L0":
                    pe.wait_ge(masks, 1)
                for u in range(nu):
                    for t in range(B):
                        if u == 0:
                            need_proj(t)
                        if u >= 2:
                            pe.wait_ge(s_max, n["smax"] + 4 * (u - 2) + t + 1)
                        for i in range(cpu):
                            c = u * cpu + i
                            o = ps[2 * t + u % 2][:, i * R:(i + 1) * R]
                            if name == "L3":
                                mm(o, K("ones")[0:1, :], bc(m3r[0:1, t, :], [1, H, NK], [1]), start=True, stop=False)
                            if name == "L2":
                                mm(o, K("ones")[0:1, :], m2r[0:1, t, :], start=True, stop=False)
                            last = mm(o, qT[0:PD, t, cols(c)], kb[0:PD, t, :], start=name not in ("L2", "L3"), stop=True)
                        last.then_inc(s_mm, 1)
                for t in range(B):
                    pe.wait_ge(s_max, n["smax"] + 4 * (nu - 1) + t + 1)
                    for c in range(C):
                        last = nc.tensor.transpose(ps[2 * t][0:H, cols(c)], mx[:, C * t + c, 0:H], ident)
                    last.then_inc(m_turned, 1)
                n["smax"] += 4 * nu
                if name == "L1":
                    pe.wait_ge(masks, 2)
                for g in range(G):
                    for t in range(B):
                        if g == 0:
                            pe.wait_ge(mT_ready, n["mt"] + t + 1)
                        if g >= 2:
                            pe.wait_ge(probs, n["sT"] + 4 * (g - 2) + t + 1)
                        o = ps[2 * t + 1 - g % 2][0:RB, :]
                        mm(o, kb[0:PD, t, g * RB:(g + 1) * RB], qT[0:PD, t, :], start=True, stop=False)
                        if name == "L1":
                            mm(o, rep2[:, :, :].rearrange("p a b -> p (a b)"), madd_k[:, t * S:(t + 1) * S], start=False, stop=False)
                        mm(o, K(name + "_neg")[0:H, g * RB:(g + 1) * RB], mT[0:H, t, :], start=False, stop=True).then_inc(sT_mm, 1)
                wd = PD + H
                for t in range(B):
                    pe.wait_ge(probs, n["sT"] + 4 * (G - 1) + t + 1)
                    for c in range(C):
                        o = ps[2 * t + c // 2][:, (c % 2) * wd:(c % 2 + 1) * wd]
                        for g in range(G):
                            last = mm(o, big[0:RB, g, t, cols(c)], vb[0:RB, t, g, 0:wd], start=g == 0, stop=g == G - 1)
                    last.then_inc(av_mm, 1)
                n["mt"] += 4
                n["sT"] += 4 * G
                turn(xn, PD)

            def router(wr, ranks):
                for t in range(B):
                    need_xT(t)
                    for c in range(C):
                        last = mm(ps[2 * t + 1][:, c * E:(c + 1) * E], xT[:, t, cols(c)], wr, start=True, stop=True)
                    last.then_inc(lg_mm, 1)
                if ranks:
                    n["oh"] += 1
                    pe.wait_ge(oh_ready, n["oh"])
                    m = ranks * B * C * E
                    chosen = oh[:, :, :].rearrange("p a b -> p (a b)")[:, 0:m]
                    mm(ps[0][:, 0:m], K("tri"), chosen, start=True, stop=True)
                    mm(ps[2][:, 0:m], K("ones"), chosen, start=True, stop=True).then_inc(cum_mm, 1)

            def placed(name, k, loaded, wr, bias):
                a = PLACED[name]
                nb, gb, eg, N = a["nb"], a["gb"], a["eg"], a["N"]
                turn(xn)
                router(wr, a["ranks"])
                pe.wait_ge(idx_ready, k + 1)
                g0 = n["g"]
                h0 = n["h"]
                pe.wait_ge(loaded, 32 * E)

                def turn_group(g):
                    done = sum(1 for q in range(g + 1) if q % 2 == g % 2) + sum(1 for q in range(g0) if q % 2 == g % 2)
                    pe.wait_ge(g_ld[g % 2], 16 * done)
                    if g >= 1:
                        pe.wait_ge(gT_s, g0 + g)
                    for b in range(gb):
                        last = nc.tensor.transpose(ps[b // 4][:, cols(b % 4)], xg[:, g % 2, cols(b)], ident)
                    last.then_inc(gT_m, 1)
                    n["g"] += 1

                def hidden(e):
                    g = e // eg
                    pe.wait_ge(gT_s, g0 + g + 1)
                    at = (e % eg) * a["cap"]
                    for f in range(4):
                        for j in range(a["pieces"]):
                            u = n["h"] - h0
                            if u >= 4:
                                pe.wait_ge(h_act, n["h"] - 3)
                            mm(ps[2 + u % 4][:, 0:N], moe_w[:, e, cols(f)], xgT[:, g % 2, at + j * N:at + (j + 1) * N],
                               start=True, stop=True).then_inc(h_mm, 1)
                            n["h"] += 1
                    if e % eg == eg - 1 and g + 2 < a["groups"]:
                        turn_group(g + 2)
                    return n["h"]

                def results(e, units):
                    pe.wait_ge(h_act, units)
                    if e >= 2 or (e >= 1 and nb > 4):
                        pe.wait_ge(gy_sb, k * E + e - (1 if nb <= 4 else 0))
                    for b in range(nb):
                        o = ps[6 + (b // 4 if nb > 4 else e % 2)][:, cols(b % 4)]
                        for f in range(4):
                            last = mm(o, hid[:, e % 2, f, cols(b)], moe_w[:, e, 512 + P * f:512 + P * f + P],
                                      start=f == 0, stop=f == 3 and bias is None)
                        if bias is not None:
                            last = mm(o, ident[0:E, e:e + 1].to_broadcast([E, P]), bias[:, :], start=False, stop=True)
                    last.then_inc(gy_mm, 1)

                turn_group(0)
                turn_group(1)
                units = hidden(0)
                for e in range(E):
                    nxt = hidden(e + 1) if e + 1 < E else None
                    results(e, units)
                    units = nxt

            def mixture(w, F, loaded, wr, bias):
                FC = F // P
                turn(xn)
                router(wr, 0)
                pe.wait_ge(gate_ready, 1)
                for t in range(B):
                    for c in range(C):
                        last = nc.tensor.transpose(ps[2 * t][0:E, cols(c)], gate[:, C * t + c, :], ident)
                    last.then_inc(gT_mm, 1)
                for t in range(B):
                    pe.wait_ge(gT_sb, t + 1)
                    for c in range(C):
                        last = mm(ps[2 * t + 1][:, cols(c)], gateT[:, t, cols(c)], bias[:, :], start=True, stop=True)
                    last.then_inc(gb_mm, 1)
                pe.wait_ge(y_used, 1)
                pe.wait_ge(loaded, 32 * E)

                def hidden(i):
                    e, t = divmod(i, B)
                    for f in range(FC):
                        u = n["h"]
                        if i * FC + f >= 6:
                            pe.wait_ge(h_act, u - 5)
                        mm(ps[(i * FC + f) % 6][:, :], w[:, e, cols(f)], xT[:, t, :], start=True, stop=True).then_inc(h_mm, 1)
                        n["h"] += 1
                    return n["h"]

                def outputs(i, have):
                    e, t = divmod(i, B)
                    pe.wait_ge(h_act, have)
                    if i >= 2:
                        pe.wait_ge(y_used, i)
                    for c in range(C):
                        for f in range(FC):
                            last = mm(ps[6 + i % 2][:, cols(c)], big[:, f, i % B, cols(c)],
                                      w[:, e, F + P * f:F + P * f + P], start=f == 0, stop=f == FC - 1)
                    last.then_inc(y_mm, 1)

                units = hidden(0)
                for i in range(E * B):
                    nxt = hidden(i + 1) if i + 1 < E * B else None
                    outputs(i, units)
                    units = nxt

            def slot_layer():
                turn(xn)
                project(W("Dk"))
                for t in range(B):
                    for c in range(C):
                        last = mm(ps[2 * t][:, cols(c)], xT[:, t, cols(c)], W("Dv"), start=True, stop=True)
                    last.then_inc(dv_mm, 1)
                qb = qblk[:, :, :].rearrange("p h s -> p (h s)")
                for g in range(2):
                    for t in range(B):
                        if g == 0:
                            need_proj(t)
                        else:
                            pe.wait_ge(dv_sb, t + 1)
                        mm(ps[2 * t + 1 - g][:, :], qb[:, cols(g)], qT[:, t, :], start=True, stop=True).then_inc(ds_mm, 1)
                for g in range(2):
                    for t in range(B):
                        pe.wait_ge(dnorm, 4 * g + t + 1)
                        for c in range(C):
                            last = nc.tensor.transpose(ps[2 * t + 1 - g][:, cols(c)], big[:, g, t, cols(c)], ident)
                        last.then_inc(dp_mm, 1)
                for t in range(B):
                    pe.wait_ge(dp_sb, 4 + t + 1)
                    o = ps[2 * t][:, 0:2 * P]
                    for c in range(C):
                        last = mm(o, r[:, C * t + c, :], probs_T(t, c), start=c == 0, stop=c == C - 1)
                    last.then_inc(da_mm, 1)
                pe.wait_ge(att_ready, 4)
                mm(ps[0][0:B * SLOTS, 0:D], attT[:, :], W("Do"), start=True, stop=True).then_inc(do_mm, 1)
                pe.wait_ge(h_rows, 1)
                nc.tensor.transpose(ps[1][:, 0:B * SLOTS], hrow[:, :], ident[0:B * SLOTS, 0:B * SLOTS])
                nc.tensor.transpose(ps[2][:, 0:B * SLOTS], orow[:, :], ident[0:B * SLOTS, 0:B * SLOTS]).then_inc(hT_mm, 1)
                pe.wait_ge(hT_ready, 1)
                for g in range(SE // 4):
                    if g >= 2:
                        pe.wait_ge(e_h, g - 1)
                    for e in range(4 * g, 4 * g + 4):
                        w = slot_w(e)
                        pe.wait_ge(ld_e[e % SLOT_BUFS], 48 * (e // SLOT_BUFS + 1))
                        for f in range(4):
                            at = 16 * (e % 4) + 4 * f
                            mm(ps[3 + g % 2][:, at:at + 4], w[:, cols(f)], hT[:, :, e], start=True, stop=True)
                            last = mm(ps[3 + g % 2][:, 64 + at:68 + at], w[:, 512 + P * f:512 + P * f + P], hT[:, :, e],
                                      start=True, stop=True)
                    last.then_inc(e_mm, 1)
                    if g >= 1:
                        second(g - 1)
                second(SE // 4 - 1)
                pe.wait_ge(oT_ready, 1)
                prepare("CB", oT[:, :, :].rearrange("p b s -> p (b s)"))
                project(W("CBq"))
                attend("CB")
                out_tokens(xT, W("CBo"))

            def second(g):
                pe.wait_ge(e_act, g + 1)
                for e in range(4 * g, 4 * g + 4):
                    w = slot_w(e)
                    for f in range(4):
                        last = mm(ps[5][:, 4 * e:4 * e + 4], w[:, 1024 + P * f:1024 + P * f + P], uu[:, e, f, :],
                                  start=f == 0, stop=f == 3)
                last.then_inc(ey_mm, 1)

            pe.wait_ge(ld_w, 32)
            pe.wait_ge(ld_c, 48)
            for name in CTX_ATT:
                prepare(name, V("ctxT", 0, B * NK))
            mm(ps[2][:, 0:SLOTS], W("Dq"), V("sqT", 0, SLOTS), start=True, stop=True).then_inc(dq_mm, 1)
            pe.wait_ge(qblk_ready, 1)
            turn(r)
            project(W("L0v"))
            out_tokens(qT, W("L0so"), 0)
            turn(r)
            project(W("L0q"))
            attend("L0")
            out_tokens(xT, W("L0o"))
            turn(r)
            for f in range(4):
                for t in range(B):
                    if f == 0:
                        need_xT(t)
                    if f >= 2:
                        pe.wait_ge(h_act, 4 * (f - 2) + t + 1)
                    mm(ps[2 * t + 1 - f % 2][:, :], W("L0l1")[:, cols(f)], xT[:, t, :], start=True, stop=True).then_inc(h_mm, 1)
            n["h"] = 16
            for t in range(B):
                pe.wait_ge(h_act, 12 + t + 1)
                for c in range(C):
                    for f in range(4):
                        last = mm(ps[2 * t + 1][:, cols(c)], big[:, f, t, cols(c)], W("L0l2")[:, cols(f)], start=f == 0, stop=f == 3)
                last.then_inc(out_mm, 1)
            placed("m0", 0, ld_m0, W("wr0"), b2m0)
            turn(xn)
            project(W("L1q"))
            attend("L1")
            out_tokens(xT, W("L1o"))
            slot_layer()
            pe.wait_ge(tok_ready, 4 * n["turn"] + 1)
            prepare("L3", V("ctxT", 0, B * NK))
            turn(xn)
            project(W("L2q"), 64)
            attend("L2")
            out_tokens(xT, wout2[:, :])
            placed("m2", 1, ld_m2, W("wr2"), None)
            turn(xn)
            project(W("L3q"))
            attend("L3")
            out_tokens(xT, W("L3o"))
            mixture(w3, 256, ld_m3, W("wr3"), b2m3)

        @block.scalar
        def _(act):
            A = nc.scalar.activation
            n = dict(turn=0, proj=0, sT=0, h=0, moe=0)

            def turn(width=D):
                for t in range(B):
                    k = 4 * n["turn"] + t + 1
                    act.wait_ge(turned, k)
                    A(xT[0:width, t, :], ps[2 * t][0:width, :], ACT.Identity).then_inc(xT_ready, 1)
                n["turn"] += 1

            def project(bias, width=D):
                for t in range(B):
                    act.wait_ge(proj_mm, 4 * n["proj"] + t + 1)
                    A(qT[0:width, t, :], ps[2 * t + 1][0:width, :], ACT.Identity,
                      bias=bias if bias is not None else 0.0).then_inc(proj_ready, 1)
                n["proj"] += 1

            def attend(name):
                a = ATT[name]
                RB, G = a["RB"], a["G"]
                for g in range(G):
                    for t in range(B):
                        act.wait_ge(sT_mm, n["sT"] + 1)
                        bias = m2c[:, t:t + 1] if name == "L2" else m3c[:, t:t + 1] if name == "L3" else 0.0
                        A(big[0:RB, g, t, :], ps[2 * t + 1 - g % 2][0:RB, :], ACT.Exp, bias=bias,
                          scale=a["scale"]).then_inc(probs, 1)
                        n["sT"] += 1
                turn(a["PD"])

            def chances():
                act.wait_ge(gate_e, n["moe"] + 1)
                A(ga[:, 0:B * C, :], gb[:, 0:B * C, :], ACT.Exp).then_inc(gate_ep, 1)
                n["moe"] += 1

            def placed(name, k, fn, bias):
                a = PLACED[name]
                for e in range(E):
                    if e >= 2:
                        act.wait_ge(gy_mm, k * E + e - 1)
                    for f in range(4):
                        for j in range(a["pieces"]):
                            u = n["h"] - n["h0"]
                            act.wait_ge(h_mm, n["h"] + 1)
                            A(hid[:, e % 2, f, j * a["N"]:(j + 1) * a["N"]], ps[2 + u % 4][:, 0:a["N"]], fn,
                              bias=V(bias, e * 4 + f) if bias else 0.0).then_inc(h_act, 1)
                            n["h"] += 1

            def mixture(F, fn, bias):
                FC = F // P
                for t in range(B):
                    act.wait_ge(gT_mm, t + 1)
                    A(gateT[:, t, :], ps[2 * t][0:E, :], ACT.Identity).then_inc(gT_sb, 1)
                for i in range(E * B):
                    e, t = divmod(i, B)
                    for f in range(FC):
                        act.wait_ge(h_mm, n["h"] + 1)
                        if i >= B and f == 0:
                            act.wait_ge(y_mm, i - B + 1)
                        A(big[:, f, i % B, :], ps[(i * FC + f) % 6][:, :], fn,
                          bias=V(bias, e * FC + f)).then_inc(h_act, 1)
                        n["h"] += 1

            act.wait_ge(ld_c, 48)
            turn()
            project(V("L0bv"))
            turn()
            project(V("L0bq"))
            act.wait_ge(masks, 1)
            attend("L0")
            turn()
            for f in range(4):
                for t in range(B):
                    act.wait_ge(h_mm, n["h"] + 1)
                    A(big[:, f, t, :], ps[2 * t + 1 - f % 2][:, :], ACT.Relu, bias=V("L0bl1", f)).then_inc(h_act, 1)
                    n["h"] += 1
            turn()
            n["h0"] = n["h"]
            placed("m0", 0, ACT.Relu, "m0b1")
            turn()
            project(None)
            attend("L1")
            turn()
            project(V("Dbk"))
            for g in range(2):
                for t in range(B):
                    act.wait_ge(dmax, 4 * g + t + 1)
                    A(big[:, g, t, :], ps[2 * t + 1 - g][:, :], ACT.Exp, bias=dm[:, t, g:g + 1],
                      scale=ATT["CB"]["scale"], accum_out=dsum[:, t, g:g + 1]).then_inc(dexp, 1)
            for g in range(2):
                for t in range(B):
                    act.wait_ge(dp_mm, 4 * g + t + 1)
                    A(big[:, 2 + g, t, :], ps[2 * t + 1 - g][:, :], ACT.Identity).then_inc(dp_sb, 1)
            for g in range(SE // 4):
                act.wait_ge(e_h, g + 1)
                gr = slice(4 * g, 4 * g + 4)
                A(eu[:, gr, :, :], uu[:, gr, :, :], ACT.Exp, scale=-1.0)
                A(eg[:, gr, :, :], gg[:, gr, :, :], ACT.Exp, scale=-1.0).then_inc(e_exp, 1)
            project(V("CBbq"))
            attend("CB")
            turn()
            project(None, 64)
            attend("L2")
            turn()
            chances()
            n["h0"] = n["h"]
            placed("m2", 1, ACT.Gelu, None)
            turn()
            project(V("L3bq"))
            attend("L3")
            turn()
            chances()
            mixture(256, ACT.Gelu, "m3b1")

        @block.vector
        def _(dve):
            v = nc.vector
            n = dict(chain=0, out=0, smax=0, mt=0, av=0, lg=0, y=0, moe=0, tok=0, norm=0)

            def link(i):
                n["chain"] += 1
                i.then_inc(dve_chain, 1)
                dve.wait_ge(dve_chain, n["chain"])

            def chunks(t):
                return slice(C * t, C * t + C)

            def norms(src, dst, gain=None, shift=None, before=None, after=None):
                for t in range(B):
                    if before:
                        before(t)
                    for c in range(C):
                        i = v.bn_stats(st[:, C * t + c, :], src[:, C * t + c, :])
                    link(i)
                    for c in range(C):
                        i = v.bn_aggr(mv[:, C * t + c, :], st[:, C * t + c, :])
                    i.then_inc(var_ready, 1)
                n["norm"] += B
                for t in range(B):
                    tt = chunks(t)
                    dve.wait_ge(rstd_ready, n["norm"] - B + t + 1)
                    for c in range(C):
                        i = v.tensor_scalar(dst[:, C * t + c, :], src[:, C * t + c, :], mv[:, C * t + c, 0:1],
                                            rstd[:, C * t + c:C * t + c + 1], ALU.subtract, ALU.mult)
                    if gain is not None:
                        link(i)
                        link(v.tensor_tensor(dst[:, tt, :], dst[:, tt, :], bc(ROW(gain), [P, C, D], [1]), ALU.mult))
                        i = v.tensor_tensor(dst[:, tt, :], dst[:, tt, :], bc(ROW(shift), [P, C, D], [1]), ALU.add)
                    if after:
                        link(i)
                        after(t)
                    else:
                        ready(i)

            def ready(i):
                n["tok"] += 1
                i.then_inc(tok_ready, 1)

            def add_out(dst, t, bias, bank=1):
                tt = chunks(t)
                dve.wait_ge(out_mm, 4 * n["out"] + t + 1)
                i = v.tensor_tensor(dst[:, tt, :], dst[:, tt, :],
                                    ps[2 * t + bank][:, :].rearrange("p (c d) -> p c d", c=C), ALU.add)
                link(i)
                if bias:
                    link(v.tensor_tensor(dst[:, tt, :], dst[:, tt, :], bc(ROW(bias), [P, C, D], [1]), ALU.add))

            def prepared(name, k):
                a = ATT[name]
                dve.wait_ge(k_mm, k + 1)
                if k >= 1:
                    dve.wait_ge(kv_ready, k)
                o, i_ = kts[0:a["PD"], 0:B * a["nk"]], ps[0][0:a["PD"], 0:B * a["nk"]]
                b = {"L0": "L0bk", "L3": "L3bk", "CB": "CBbk"}.get(name)
                if b:
                    v.tensor_scalar(o, i_, V(b), None, ALU.add).then_inc(k_sb, 1)
                else:
                    v.tensor_copy(o, i_).then_inc(k_sb, 1)
                dve.wait_ge(v_mm, k + 1)
                RB, PD = a["RB"], a["PD"]
                o = vr[0:RB, :, 0:PD]
                i_ = ps[1][0:RB, 0:B * PD].rearrange("p (b d) -> p b d", b=B)
                b = {"L0": "L0mvb", "L3": "L3vb", "CB": "CBvb"}.get(name)
                if b:
                    v.tensor_tensor(o, i_, bc(ROW(b)[0:RB, :], [RB, B, PD], [1]), ALU.add).then_inc(v_sb, 1)
                else:
                    v.tensor_copy(o, i_).then_inc(v_sb, 1)

            def attend(name):
                a = ATT[name]
                R, H, nu, cpu, PD, dh = (a[i] for i in ("R", "H", "nu", "cpu", "PD", "dh"))
                for u in range(nu):
                    for t in range(B):
                        n["smax"] += 1
                        dve.wait_ge(s_mm, n["smax"])
                        c0 = C * t + u * cpu
                        src = ps[2 * t + u % 2][:, 0:cpu * R].rearrange("p (c h k) -> p c h k", c=cpu, h=H)
                        if name == "L1":
                            if t:
                                dve.wait_ge(s_max, n["smax"] - 1)
                            link(v.tensor_tensor(msc[:, :, :, :], src, bc(madd_t[:, c0:c0 + C, :], [P, C, H, NK], [2]), ALU.add))
                            src = msc[:, :, :, :]
                        v.tensor_reduce(mx[:, c0:c0 + cpu, 0:H], src, AX.X, ALU.max).then_inc(s_max, 1)
                for t in range(B):
                    dve.wait_ge(m_turned, n["mt"] + t + 1)
                    v.tensor_copy(mT[0:H, t, :], ps[2 * t][0:H, :]).then_inc(mT_ready, 1)
                n["mt"] += 4
                wd = PD + H
                for t in range(B):
                    dve.wait_ge(av_mm, n["av"] + t + 1)
                    for j in range(2):
                        s_ = ps[2 * t + j][:, 0:2 * wd].rearrange("p (c w) -> p c w", c=2)
                        i = v.reciprocal(rs[:, C * t + 2 * j:C * t + 2 * j + 2, 0:H], s_[:, :, PD:wd])
                    link(i)
                    for j in range(2):
                        cc = slice(C * t + 2 * j, C * t + 2 * j + 2)
                        s_ = ps[2 * t + j][:, 0:2 * wd].rearrange("p (c w) -> p c w", c=2)
                        o = xn[:, cc, 0:PD].rearrange("p c (h d) -> p c h d", h=H)
                        i = v.tensor_tensor(o, s_[:, :, 0:PD].rearrange("p c (h d) -> p c h d", h=H),
                                            bc(rs[:, cc, 0:H], [P, 2, H, dh], [3]), ALU.mult)
                    ready(i)
                n["av"] += 4

            def first_largest(src, dst):
                nb = B * C
                link(v.tensor_reduce(gm[:, :], src, AX.X, ALU.max))
                link(v.tensor_tensor(ga[:, 0:nb, :], src, bc(gm[:, :], [P, nb, E], [2]), ALU.is_equal))
                link(v.tensor_tensor(ga[:, 0:nb, :], ga[:, 0:nb, :], bc(K("first"), [P, nb, E], [1]), ALU.mult))
                link(v.tensor_reduce(gs[:, :], ga[:, 0:nb, :], AX.X, ALU.max))
                link(v.tensor_tensor(dst, ga[:, 0:nb, :], bc(gs[:, :], [P, nb, E], [2]), ALU.is_equal))

            def kept(m, capacity, base):
                k = m * B * C
                mine = lambda ap: ap[:, 0:k, :]
                link(v.tensor_copy(mine(gt[:, :, :]), ps[2][:, 0:k * E].rearrange("p (c e) -> p c e", e=E)))
                cur, nxt, s = gt, ga, 1
                while s < k:
                    v.tensor_copy(nxt[:, 0:s, :], cur[:, 0:s, :])
                    link(v.tensor_tensor(nxt[:, s:k, :], cur[:, s:k, :], cur[:, 0:k - s, :], ALU.add))
                    cur, nxt = nxt, cur
                    s *= 2
                link(v.tensor_tensor(mine(cur[:, :, :]), mine(cur[:, :, :]),
                                     ps[2][:, 0:k * E].rearrange("p (c e) -> p c e", e=E), ALU.subtract))
                link(v.tensor_tensor(mine(cur[:, :, :]), mine(cur[:, :, :]),
                                     ps[0][:, 0:k * E].rearrange("p (c e) -> p c e", e=E), ALU.add))
                link(v.tensor_scalar(mine(gb[:, :, :]), mine(cur[:, :, :]), float(capacity), None, ALU.is_le))
                link(v.tensor_tensor(mine(gb[:, :, :]), mine(gb[:, :, :]), mine(oh[:, :, :]), ALU.mult))
                link(v.tensor_tensor(mine(cur[:, :, :]), mine(cur[:, :, :]), bc(K(base), [P, k, E], [1]), ALU.add))
                link(v.tensor_tensor(mine(cur[:, :, :]), mine(cur[:, :, :]), mine(oh[:, :, :]), ALU.mult))
                v.tensor_reduce(slot[:, 0:k], mine(cur[:, :, :]), AX.X, ALU.add)
                link(v.tensor_reduce(have[:, 0:k], mine(gb[:, :, :]), AX.X, ALU.add))
                link(v.scalar_tensor_tensor(out=wgt[:, 0:k], in0=have[:, 0:k], scalar=-SKIP, in1=slot[:, 0:k],
                                            op0=ALU.mult, op1=ALU.add))
                v.tensor_scalar(to_slot[:, 0:k], wgt[:, 0:k], SKIP, None, ALU.add)
                v.tensor_tensor(at_slot[:, 0:k], slot[:, 0:k], have[:, 0:k], ALU.mult).then_inc(idx_ready, 1)

            def evacuate(name, k):
                a = PLACED[name]
                nb, gb, eg = a["nb"], a["gb"], a["eg"]
                g0 = 0 if name == "m0" else PLACED["m0"]["groups"]

                def group(g):
                    dve.wait_ge(gT_m, g0 + g + 1)
                    if g >= 2:
                        dve.wait_ge(h_mm, units0[name] + 4 * a["pieces"] * eg * (g - 1))
                    for j in range(0, gb, 4):
                        m = min(4, gb - j)
                        i = v.tensor_copy(xgT[:, g % 2, j * P:(j + m) * P], ps[j // 4][:, 0:m * P])
                    i.then_inc(gT_s, 1)

                group(0)
                group(1)
                for e in range(E):
                    g = e // eg
                    if e % eg == eg - 1 and g + 2 < a["groups"]:
                        group(g + 2)
                    dve.wait_ge(gy_mm, k * E + e + 1)
                    if e >= 2 or k:
                        dve.wait_ge(gy_st[e % 2], 16 * (4 * k + e // 2))
                    for j in range(0, nb, 4):
                        m = min(4, nb - j)
                        i = v.tensor_copy(ysb[:, e % 2, j * P:(j + m) * P], ps[6 + (j // 4 if nb > 4 else e % 2)][:, 0:m * P])
                    i.then_inc(gy_sb, 1)

            def gather_in(ranks, seen):
                def tile(t):
                    dve.wait_ge(back[t], 16 * C * (seen + ranks))
                    for k in range(ranks):
                        for c in range(C * t, C * t + C):
                            i = v.scalar_tensor_tensor(out=x[:, c, :], in0=yg[:, k, c, :],
                                                       scalar=wgt[:, B * C * k + c:B * C * k + c + 1], in1=x[:, c, :],
                                                       op0=ALU.mult, op1=ALU.add)
                        link(i)
                return tile

            def logits(bias):
                nb = B * C
                for t in range(B):
                    dve.wait_ge(lg_mm, n["lg"] + t + 1)
                    s_ = ps[2 * t + 1][:, 0:C * E].rearrange("p (c e) -> p c e", e=E)
                    if bias:
                        i = v.tensor_tensor(lg[:, chunks(t), :], s_, bc(ROW(bias), [P, C, E], [1]), ALU.add)
                    else:
                        i = v.tensor_copy(lg[:, chunks(t), :], s_)
                link(i)
                n["lg"] += 4

            def two_largest():
                nb = B * C
                first_largest(lg[:, :, :], oh[:, 0:nb, :])
                link(v.scalar_tensor_tensor(out=lg2[:, :, :], in0=oh[:, 0:nb, :], scalar=-BIG, in1=lg[:, :, :],
                                            op0=ALU.mult, op1=ALU.add))
                link(v.tensor_reduce(gm[:, :], lg[:, :, :], AX.X, ALU.max))
                link(v.tensor_tensor(lg[:, :, :], lg[:, :, :], bc(gm[:, :], [P, nb, E], [2]), ALU.subtract))
                first_largest(lg2[:, :, :], oh[:, nb:2 * nb, :])

            def add_bias_rows():
                for t in range(B):
                    dve.wait_ge(gb_mm, t + 1)
                    i = v.tensor_tensor(x[:, chunks(t), :], x[:, chunks(t), :],
                                        ps[2 * t + 1][:, :].rearrange("p (c d) -> p c d", c=C), ALU.add)
                i.then_inc(y_used, 1)
                dve.wait_ge(y_used, 1)

            def experts():
                for i in range(E * B):
                    e, t = divmod(i, B)
                    dve.wait_ge(y_mm, i + 1)
                    if i >= B:
                        dve.wait_ge(y_used, 1 + i - B + 1)
                    for c in range(C):
                        last = v.scalar_tensor_tensor(out=x[:, C * t + c, :], in0=ps[6 + i % 2][:, cols(c)],
                                                      scalar=gate[:, C * t + c, e:e + 1], in1=x[:, C * t + c, :],
                                                      op0=ALU.mult, op1=ALU.add)
                    last.then_inc(y_used, 1)

            dve.wait_ge(ld_s, 16 * (8 + 3 * B))
            dve.wait_ge(ld_c, 48)
            v.tensor_scalar(madd_t[:, :, :], mask_tok[:, :, :], -1.0, BIG, ALU.add, ALU.mult)
            v.tensor_scalar(m2c[:, :], mask2c[:, :], -1.0, BIG, ALU.add, ALU.mult)
            v.tensor_scalar(m2r[:, :, :], mask2[:, :, :], -1.0, BIG, ALU.add, ALU.mult)
            v.tensor_scalar(m3c[:, :], mask3c[:, :], -1.0, 1e4, ALU.add, ALU.mult)
            v.tensor_scalar(m3r[:, :, :], mask3[:, :, :], -1.0, 1e4 / ATT["L3"]["scale"], ALU.add, ALU.mult)
            for h in range(2):
                i = v.tensor_copy(rep2[:, h, :], ident[0:NK, 0:NK])
            i.then_inc(masks, 1)
            dve.wait_ge(ld_x, 16)
            for k, name in enumerate(CTX_ATT):
                prepared(name, k)
            dve.wait_ge(dq_mm, 1)
            link(v.tensor_scalar(dqT[:, :], ps[2][:, 0:SLOTS], V("Dbq"), None, ALU.add))
            v.tensor_tensor(qblk[:, :, :], bc(dqT[:, :], [P, SE, SLOTS], [1]), bc(K("CB_dim"), [P, SE, SLOTS], [2]),
                            ALU.mult).then_inc(qblk_ready, 1)
            norms(x, r)
            norms(r, r, "g1", "b1", before=lambda t: add_out(r, t, "so_b", 0))
            n["out"] += 1
            attend("L0")
            norms(r, r, "g2", "b2", before=lambda t: add_out(r, t, "mo_b"))
            n["out"] += 1
            norms(r, r, "g3", "b3", before=lambda t: add_out(r, t, "l2_b"), after=lambda t: link(
                v.tensor_tensor(x[:, chunks(t), :], x[:, chunks(t), :], r[:, chunks(t), :], ALU.add)))
            norms(x, xn)
            n["out"] += 1
            nb = B * C
            logits("sw_b")
            first_largest(lg[:, :, :], oh[:, 0:nb, :])
            v.tensor_copy(oh[0:1, 0, 0:1], oh[0:1, 0, 0:1]).then_inc(oh_ready, 1)
            dve.wait_ge(oh_ready, 1)
            dve.wait_ge(cum_mm, 1)
            kept(1, CAP0, "base0")
            link(v.tensor_scalar(drop[:, :], have[:, 0:nb], -1.0, 1.0, ALU.mult, ALU.add))
            link(v.tensor_copy(wgt[:, 0:nb], have[:, 0:nb]))
            for c in range(nb):
                i = v.scalar_tensor_tensor(out=x[:, c, :], in0=xn[:, c, :], scalar=drop[:, c:c + 1], in1=x[:, c, :],
                                           op0=ALU.mult, op1=ALU.add)
            link(i)
            evacuate("m0", 0)
            v.tensor_scalar(madd_k, mask_key[:, :], -1.0, BIG, ALU.add, ALU.mult).then_inc(masks, 1)
            norms(x, xn, before=gather_in(1, 0))
            attend("L1")
            norms(x, xn, before=lambda t: add_out(x, t, None))
            n["out"] += 1
            for t in range(B):
                dve.wait_ge(dv_mm, t + 1)
                v.tensor_copy(r[:, chunks(t), :], ps[2 * t][:, :].rearrange("p (c d) -> p c d", c=C)).then_inc(dv_sb, 1)
            for g in range(2):
                for t in range(B):
                    dve.wait_ge(ds_mm, 4 * g + t + 1)
                    link(v.tensor_reduce(dm[:, t, g:g + 1], ps[2 * t + 1 - g][:, :], AX.X, ALU.max))
                    v.tensor_scalar(dm[:, t, g:g + 1], dm[:, t, g:g + 1], -ATT["CB"]["scale"], None, ALU.mult).then_inc(dmax, 1)
            for g in range(2):
                for t in range(B):
                    dve.wait_ge(dexp, 4 * g + t + 1)
                    link(v.reciprocal(drs[:, t, g:g + 1], dsum[:, t, g:g + 1]))
                    v.tensor_scalar(big[:, g, t, :], big[:, g, t, :], drs[:, t, g:g + 1], None, ALU.mult).then_inc(dnorm, 1)
            for t in range(B):
                dve.wait_ge(da_mm, t + 1)
                link(v.tensor_tensor(pair[:, :, :], ps[2 * t][:, 0:2 * P].rearrange("p (h s) -> p h s", h=SE),
                                     bc(K("CB_dim"), [P, SE, SLOTS], [2]), ALU.mult))
                a_ = attT[:, SLOTS * t:SLOTS * (t + 1)]
                link(v.tensor_reduce(a_, pair[:, :, :].rearrange("p h s -> p s h"), AX.X, ALU.add))
                v.tensor_scalar(a_, a_, V("Dbv"), None, ALU.add).then_inc(att_ready, 1)
            dve.wait_ge(do_mm, 1)
            nr = B * SLOTS
            link(v.tensor_tensor(orow[:, :], ps[0][0:nr, 0:D], ROW("Dob")[0:nr, :], ALU.add))
            link(v.tensor_tensor(orow[:, :], orow[:, :], sqrow[:, :], ALU.add))
            link(v.bn_stats(st[0:nr, 0, :], orow[:, :]))
            v.bn_aggr(mv[0:nr, 0, :], st[0:nr, 0, :]).then_inc(var_ready, 1)
            n["norm"] += 1
            dve.wait_ge(rstd_ready, n["norm"])
            link(v.tensor_scalar(hrow[:, :], orow[:, :], mv[0:nr, 0, 0:1], rstd[0:nr, 0:1], ALU.subtract, ALU.mult))
            link(v.tensor_tensor(hrow[:, :], hrow[:, :], lng[:, :], ALU.mult))
            v.tensor_tensor(hrow[:, :], hrow[:, :], lnb[:, :], ALU.add).then_inc(h_rows, 1)
            dve.wait_ge(hT_mm, 1)
            v.tensor_copy(oT[:, :, :], ps[2][:, 0:nr].rearrange("p (b s) -> p b s", b=B))
            v.tensor_copy(hT[:, :, :], ps[1][:, 0:nr].rearrange("p (b s) -> p b s", b=B)).then_inc(hT_ready, 1)
            dve.wait_ge(hT_ready, 1)
            for g in range(SE // 4):
                dve.wait_ge(e_mm, g + 1)
                gr = slice(4 * g, 4 * g + 4)
                for dst, at, b_ in ((uu, 0, "eb1"), (gg, 64, "ebg")):
                    i = v.tensor_tensor(dst[:, gr, :, :].rearrange("p e f b -> p (e f) b"),
                                        ps[3 + g % 2][:, at:at + 64].rearrange("p (f b) -> p f b", b=B),
                                        bc(V(b_, 16 * g, 16), [P, 16, B], [2]), ALU.add)
                i.then_inc(e_h, 1)
                dve.wait_ge(e_exp, g + 1)
                v.tensor_scalar(eu[:, gr, :, :], eu[:, gr, :, :], 1.0, None, ALU.add)
                link(v.tensor_scalar(eg[:, gr, :, :], eg[:, gr, :, :], 1.0, None, ALU.add))
                v.reciprocal(eu[:, gr, :, :], eu[:, gr, :, :])
                link(v.reciprocal(eg[:, gr, :, :], eg[:, gr, :, :]))
                v.tensor_tensor(uu[:, gr, :, :], uu[:, gr, :, :], eu[:, gr, :, :], ALU.mult)
                link(v.tensor_tensor(gg[:, gr, :, :], gg[:, gr, :, :], eg[:, gr, :, :], ALU.mult))
                v.tensor_tensor(uu[:, gr, :, :], uu[:, gr, :, :], gg[:, gr, :, :], ALU.mult).then_inc(e_act, 1)
            dve.wait_ge(ey_mm, SE // 4)
            link(v.tensor_tensor(oT[:, :, :], oT[:, :, :],
                                 ps[5][:, 0:4 * SE].rearrange("p (e b) -> p b e", b=B), ALU.add))
            v.tensor_tensor(oT[:, :, :], oT[:, :, :], bc(V("eb2", 0, SE), [P, B, SLOTS], [1]), ALU.add).then_inc(oT_ready, 1)
            prepared("CB", 3)
            attend("CB")
            norms(x, xn, before=lambda t: add_out(x, t, "CBob"))
            n["out"] += 1
            prepared("L3", 4)
            attend("L2")
            norms(x, xn, before=lambda t: add_out(x, t, None))
            n["out"] += 1
            logits(None)
            two_largest()
            link(v.tensor_tensor(lg2[:, :, :], oh[:, 0:nb, :], oh[:, nb:2 * nb, :], ALU.add))
            v.tensor_copy(gb[:, 0:nb, :], lg[:, :, :]).then_inc(gate_e, 1)
            dve.wait_ge(gate_ep, 1)
            link(v.tensor_tensor(lg2[:, :, :], lg2[:, :, :], ga[:, 0:nb, :], ALU.mult))
            link(v.tensor_reduce(gs[:, :], lg2[:, :, :], AX.X, ALU.add))
            link(v.reciprocal(gs[:, :], gs[:, :]))
            v.tensor_tensor(lg2[:, :, :], lg2[:, :, :], bc(gs[:, :], [P, nb, E], [2]), ALU.mult).then_inc(oh_ready, 1)
            dve.wait_ge(oh_ready, 2)
            dve.wait_ge(cum_mm, 2)
            kept(2, CAP2, "base2")
            for k in range(2):
                kk = slice(nb * k, nb * (k + 1))
                link(v.tensor_tensor(gb[:, kk, :], gb[:, kk, :], lg2[:, :, :], ALU.mult))
            link(v.tensor_reduce(wgt[:, :], gb[:, :, :], AX.X, ALU.add))
            evacuate("m2", 1)
            norms(x, xn, before=gather_in(2, 1))
            attend("L3")
            norms(x, xn, before=lambda t: add_out(x, t, "L3ob"))
            n["out"] += 1
            logits(None)
            two_largest()
            link(v.tensor_tensor(lg2[:, :, :], oh[:, 0:nb, :], oh[:, nb:2 * nb, :], ALU.add))
            v.tensor_copy(gb[:, 0:nb, :], lg[:, :, :]).then_inc(gate_e, 1)
            dve.wait_ge(gate_ep, 2)
            link(v.tensor_reduce(gs[:, :], ga[:, 0:nb, :], AX.X, ALU.add))
            link(v.reciprocal(gs[:, :], gs[:, :]))
            link(v.tensor_tensor(ga[:, 0:nb, :], ga[:, 0:nb, :], bc(gs[:, :], [P, nb, E], [2]), ALU.mult))
            link(v.tensor_tensor(lg2[:, :, :], lg2[:, :, :], ga[:, 0:nb, :], ALU.mult))
            link(v.tensor_reduce(gs[:, :], lg2[:, :, :], AX.X, ALU.add))
            link(v.tensor_scalar(gs[:, :], gs[:, :], 1e-9, None, ALU.add))
            link(v.reciprocal(gs[:, :], gs[:, :]))
            v.tensor_tensor(gate[:, :, :], lg2[:, :, :], bc(gs[:, :], [P, nb, E], [2]), ALU.mult).then_inc(gate_ready, 1)
            dve.wait_ge(gate_ready, 1)
            add_bias_rows()
            experts()

        @block.gpsimd
        def _(pool):
            g_ = nc.gpsimd

            def prepare(name, k, keys):
                a = ATT[name]
                PD, H, nk, RB, G, hb, dh = (a[i] for i in ("PD", "H", "nk", "RB", "G", "hb", "dh"))
                if k >= 1:
                    pool.wait_ge(v_mm, k)
                g_.tensor_copy(rep[:, :, 0:RB].rearrange("p b (h k) -> p b h k", h=hb),
                               bc(keys, [P, B, hb, nk], [2])).then_inc(kv_rep, 1)
                pool.wait_ge(k_sb, k + 1)
                for b in range(B):
                    g_.tensor_tensor(KB[name][0:PD, b, :].rearrange("p (h k) -> p h k", h=H),
                                     bc(kts[0:PD, b * nk:(b + 1) * nk], [PD, H, nk], [1]),
                                     bc(K(name + "_dim")[0:PD, :], [PD, H, nk], [2]), ALU.mult)
                pool.wait_ge(v_sb, k + 1)
                sel = K(name + "_sel")[0:RB, :].rearrange("p (g h) -> p g h", g=G)
                for b in range(B):
                    for g in range(G):
                        g_.tensor_tensor(VB[name][0:RB, b, g, 0:PD].rearrange("p (h d) -> p h d", h=H),
                                         vr[0:RB, b, 0:PD].rearrange("p (h d) -> p h d", h=H),
                                         bc(sel[:, g, :], [RB, H, dh], [2]), ALU.mult)
                i = g_.tensor_copy(VB[name][0:RB, :, :, PD:PD + H], bc(sel, [RB, B, G, H], [1]))
                i.then_inc(kv_ready, 1)

            n = dict(norm=0)

            def rstds(times=1, rows=P, tiles=B, width=C):
                for _ in range(times):
                    for t in range(tiles):
                        tt = slice(C * t, C * t + width)
                        n["norm"] += 1
                        pool.wait_ge(var_ready, n["norm"])
                        g_.tensor_scalar(rstd[0:rows, tt], mv[0:rows, tt, 1], EPS, None, ALU.add).then_inc(pool_chain, 1)
                        pool.wait_ge(pool_chain, n["norm"])
                        g_.tensor_tensor(rstd[0:rows, tt], rstd[0:rows, tt], half[0:rows, 0:width], ALU.pow).then_inc(rstd_ready, 1)

            def send(name, seen):
                a = PLACED[name]
                last_row = E * a["cap"] - 1
                pool.wait_ge(idx_ready, seen + 1)
                pool.wait_ge(cleared, 32)
                for j in range(a["ranks"] * B * C):
                    g_.indirect_dma_start(out=tok_d[name], out_offset=bass.IndirectOffsetOnAxis(ap=to_slot[:, j:j + 1], axis=0),
                                          in_=xn[:, j % (B * C), :], in_offset=None, bounds_check=last_row,
                                          oob_is_err=False).then_inc(sent, 16)

            def fetch(name, seen):
                a = PLACED[name]
                for s_ in gy_st:
                    pool.wait_ge(s_, 16 * 4 * (seen + 1))
                for t in range(B):
                    for k in range(a["ranks"]):
                        for c in range(C * t, C * t + C):
                            j = B * C * k + c
                            g_.indirect_dma_start(out=yg[:, k, c, :], out_offset=None, in_=res_d[name],
                                                  in_offset=bass.IndirectOffsetOnAxis(ap=at_slot[:, j:j + 1], axis=0),
                                                  bounds_check=E * a["cap"] - 1, oob_is_err=False).then_inc(back[t], 16)

            g_.memset(zero[:, :], 0.0).then_inc(zeroed, 1)
            g_.memset(half[:, :], -0.5).then_inc(minus_half, 1)
            pool.wait_ge(minus_half, 1)
            pool.wait_ge(ld_c, 48)
            for k, name in enumerate(CTX_ATT):
                prepare(name, k, V("ctxT", 0, B * NK).rearrange("p (b k) -> p b k", b=B))
            rstds(5)
            send("m0", 0)
            fetch("m0", 0)
            rstds(2)
            rstds(1, rows=B * SLOTS, tiles=1, width=1)
            pool.wait_ge(oT_ready, 1)
            prepare("CB", 3, oT[:, :, :])
            rstds(1)
            prepare("L3", 4, V("ctxT", 0, B * NK).rearrange("p (b k) -> p b k", b=B))
            rstds(1)
            send("m2", 1)
            fetch("m2", 1)
            rstds(2)




def kernel(**inputs):
    import concourse.bacc as _bacc
    from concourse.bass_utils import run_bass_kernel_spmd as _run

    i = {k: np.asarray(v) for k, v in inputs.items()}
    T = lambda a: a.T
    rows_of = lambda a: np.concatenate([a[j * P:(j + 1) * P] for j in range(a.shape[0] // P)], axis=1)
    qkv, inp = i["L0_xattn_qkv_w"], i["L0_xattn_in_proj_w"]
    wkv = i["L1_xattn_Wkv"]
    squares = {
        "L0v": T(qkv[256:384]), "L0so": T(i["L0_xattn_sa_out_w"]), "L0q": T(inp[0:128]), "L0k": T(inp[128:256]),
        "L0mv": T(inp[256:384]), "L0o": T(i["L0_xattn_mha_out_w"]), "L0l1": T(i["L0_xattn_lin1_w"]),
        "L0l2": rows_of(T(i["L0_xattn_lin2_w"])),
        "L1q": i["L1_xattn_Wq"], "L1k": wkv[:, 0:128], "L1v": wkv[:, 128:256], "L1o": i["L1_xattn_Wo"],
        "L2q": T(i["L2_xattn_Wq"]), "L2k": T(i["L2_xattn_Wk"]), "L2v": T(i["L2_xattn_Wv"]),
        "L3q": T(i["L3_xattn_wq"]), "L3k": T(i["L3_xattn_wk"]), "L3v": T(i["L3_xattn_wv"]), "L3o": T(i["L3_xattn_wo"]),
        "Dq": i["L1_ffn_d_Wq"], "Dk": i["L1_ffn_d_Wk"], "Dv": i["L1_ffn_d_Wv"], "Do": i["L1_ffn_d_Wo"],
        "CBq": i["L1_ffn_c_Wq"], "CBk": i["L1_ffn_c_Wk"], "CBv": i["L1_ffn_c_Wv"], "CBo": i["L1_ffn_c_Wo"],
        "wr0": i["L0_ffn_w_switch"], "wr2": i["L2_ffn_w_g"], "wr3": T(i["L3_ffn_router_w"]),
    }
    on_p = lambda a: a.reshape(-1, P).T
    ib = i["L0_xattn_in_proj_b"]
    columns = {
        "L0bv": on_p(i["L0_xattn_qkv_b"][256:384]), "L0bq": on_p(ib[0:128]), "L0bk": on_p(ib[128:256]),
        "L0bl1": on_p(i["L0_xattn_lin1_b"]), "L3bq": on_p(i["L3_xattn_bq"]), "L3bk": on_p(i["L3_xattn_bk"]),
        "Dbq": on_p(i["L1_ffn_d_bq"]), "Dbk": on_p(i["L1_ffn_d_bk"]), "Dbv": on_p(i["L1_ffn_d_bv"]),
        "CBbq": on_p(i["L1_ffn_c_bq"]), "CBbk": on_p(i["L1_ffn_c_bk"]),
        "m0b1": on_p(i["L0_ffn_b1"]), "m3b1": on_p(i["L3_ffn_b1"]),
        "eb1": on_p(i["L1_ffn_e_b1"]), "ebg": on_p(i["L1_ffn_e_bg"]), "eb2": T(i["L1_ffn_e_b2"]),
        "sqT": T(i["L1_ffn_slot_query"][0]), "ctxT": T(i["ctx_1024"].reshape(B * NK, D)),
    }
    rows = {
        "so_b": i["L0_xattn_sa_out_b"], "g1": i["L0_xattn_ln1_g"], "b1": i["L0_xattn_ln1_b"],
        "mo_b": i["L0_xattn_mha_out_b"], "g2": i["L0_xattn_ln2_g"], "b2": i["L0_xattn_ln2_b"],
        "l2_b": i["L0_xattn_lin2_b"], "g3": i["L0_xattn_ln3_g"], "b3": i["L0_xattn_ln3_b"],
        "L0mvb": ib[256:384], "L3vb": i["L3_xattn_bv"], "L3ob": i["L3_xattn_bo"],
        "CBvb": i["L1_ffn_c_bv"], "CBob": i["L1_ffn_c_bo"], "Dob": i["L1_ffn_d_bo"], "sw_b": i["L0_ffn_b_switch"],
    }
    bits = lambda a: a.view(np.uint8)
    m3 = i["mask_BxS2_ff1"]
    given = {
        "x": i["x"], "con": constants(),
        "sq": np.concatenate([squares[k] for k, _ in SQUARES], axis=1), "wout2": T(i["L2_xattn_Wout"]),
        "col": np.concatenate([columns[k] for k, _ in COLUMNS], axis=1),
        "row": np.concatenate([rows[k] for k, _ in ROWS])[None, :],
        "mask": bits(i["mask_BxSxS2_bf1"]),
        "maskT": bits(np.ascontiguousarray(i["mask_BxSxS2_bf1"].transpose(2, 0, 1).reshape(NK, B * S))),
        "mask2": bits(i["mask_BxS2_bf1"].reshape(1, B * NK)), "mask2c": bits(np.ascontiguousarray(i["mask_BxS2_bf1"].T)),
        "mask3": m3.reshape(1, B * NK), "mask3c": np.concatenate([m3.T] * 4, axis=0),
        "m0b2": i["L0_ffn_b2"], "m3b2": i["L3_ffn_b2"],
        "sqrow": i["L1_ffn_slot_query"][0], "lng": i["L1_ffn_e_ln_g"], "lnb": i["L1_ffn_e_ln_b"],
        "m0w1": i["L0_ffn_w1"], "m0w2": i["L0_ffn_w2"], "m2w1": i["L2_ffn_c_fc"], "m2w2": i["L2_ffn_c_proj"],
        "m3w1": i["L3_ffn_w1"], "m3w2": i["L3_ffn_w2"],
        "ew1": i["L1_ffn_e_W1"], "ewg": i["L1_ffn_e_Wg"], "ew2": i["L1_ffn_e_W2"],
    }
    nc = _bacc.Bacc("TRN2", target_bir_lowering=False, num_devices=1)
    arrays, ins = {}, {}
    for name, a in given.items():
        a = np.ascontiguousarray(a)
        arrays[f"in_{name}"] = a
        ins[name] = nc.dram_tensor(f"in_{name}", a.shape, mybir.dt.from_np(a.dtype), kind="ExternalInput").ap()
    out = nc.dram_tensor("out_x", (B, S, D), F32, kind="ExternalOutput").ap()
    build(nc, ins, out)
    got = _run(nc, [arrays], core_ids=[0])
    return got.results[0]["out_x"]
```

```python
from contextlib import ExitStack

import numpy as np

import concourse.bass as bass
from concourse import mybir

ALU = mybir.AluOpType
ACT = mybir.ActivationFunctionType
AX = mybir.AxisListType
F32 = mybir.dt.float32
BF16 = mybir.dt.bfloat16
F32R = mybir.dt.float32r
U8 = mybir.dt.uint8
U32 = mybir.dt.uint32

P = 128
B = 4
S = 512
D = 128
NK = 32
C = S // P
E = 8
SE = 16
SLOTS = 16
EPS = 1e-5
CAP0 = int(0.5 * B * S / E)
CAP2 = int(2 * 1.25 * B * S / E)
CAP2 += CAP2 % 2
SKIP = 1e6
BIG = 1e30

ATT = {
    "L0": dict(H=8, nk=NK, dh=16, scale=16 ** -0.5),
    "L1": dict(H=2, nk=NK, dh=64, scale=64 ** -0.5),
    "CB": dict(H=16, nk=SLOTS, dh=8, scale=8 ** -0.5),
    "L2": dict(H=1, nk=NK, dh=64, scale=64 ** -0.5),
    "L3": dict(H=16, nk=NK, dh=8, scale=8 ** -0.5),
}
for _a in ATT.values():
    _a["PD"] = _a["H"] * _a["dh"]
    _a["R"] = _a["H"] * _a["nk"]
    _a["RB"] = min(P, _a["R"])
    _a["G"] = _a["R"] // _a["RB"]
    _a["hb"] = _a["RB"] // _a["nk"]
    _a["cpu"] = min(C, 512 // _a["R"])
    _a["nu"] = C // _a["cpu"]

def attention(n):
    a = ATT[n]
    return ([("score", n, u) for u in range(a["nu"])] + [("maxima", n)] + [("prob", n, g) for g in range(a["G"])]
            + [("average", n), ("turn", "xn", a["PD"], None, None)])


SEQ0 = [("stats", None, "x"), ("scale", "xn"), ("turn", "xn", D, None, "so"), ("project", "L0v"), ("out", "L0so"),
        ("stats", "out", "r"), ("scale", "xn"), ("turn", "xn", D, "1", "mo"), ("project", "L0q"), *attention("L0"),
        ("out", "L0o"),
        ("stats", "out", "r"), ("scale", "xn"), ("turn", "xn", D, "2", "l2"), *[("up", f) for f in range(4)], ("down",),
        ("stats", "out", "r"), ("scale", "x3"), ("gain",), ("stats", "x3", "x"), ("scale", "xs"),
        ("turn", "xs", D, None, None), ("router", "wr0"),
        ("choose", "m0"), ("count", "m0"), ("place", "m0")]
SEQ1 = [("stats", "m0", "x"), ("scale", "xn"), ("turn", "xn", D, None, None), ("project", "L1q"), *attention("L1"),
        ("out", "L1o"),
        ("stats", "out", "x"), ("scale", "xn"), ("turn", "xn", D, None, "CB"), ("project", "Dk"), ("values",),
        ("dscore", 0), ("dscore", 1), ("dturn", 0), ("dturn", 1), ("daverage",)]
SEQ2 = [("project", "CBq"), *attention("CB"), ("out", "CBo"),
        ("stats", "out", "x"), ("scale", "xn"), ("turn", "xn", D, None, None), ("project", "L2q"), *attention("L2"),
        ("out", "L2o"), ("stats", "out", "x"), ("scale", "xs"), ("turn", "xs", D, None, None), ("router", "wr2"),
        ("choose", "m2"), ("count", "m2"), ("place", "m2")]
SEQ3 = [("stats", "m2", "x"), ("scale", "xn"), ("turn", "xn", D, None, "L3"), ("project", "L3q"), *attention("L3"),
        ("out", "L3o"), ("stats", "out", "x"), ("scale", "xn"), ("turn", "xn", D, None, None), ("router", "wr3")]
NORM_X3 = 4
ACT_SHARE = 2
LAST_TURN = sum(q[0] == "turn" for q in SEQ0 + SEQ1 + SEQ2 + SEQ3) - 1
TURNS_TO_SLOTS = sum(q[0] == "turn" for q in SEQ0 + SEQ1)


def wavefront(make, seq):
    stages = [make[name](*how) if name in make else None for name, *how in seq]
    for step in range(len(stages) + B - 1):
        for t in reversed(range(B)):
            if 0 <= step - t < len(stages) and stages[step - t]:
                stages[step - t](t)


SQUARES = [("L0v", 128), ("L0so", 128), ("L0q", 128), ("L0k", 128), ("L0mv", 128), ("L0o", 128),
           ("L0l1", 512), ("L0l2", 512),
           ("L1q", 128), ("L1k", 128), ("L1v", 128), ("L1o", 128),
           ("L2q", 64), ("L2k", 64), ("L2v", 64),
           ("L3q", 128), ("L3k", 128), ("L3v", 128), ("L3o", 128),
           ("Dq", 128), ("Dk", 128), ("Dv", 128), ("Do", 128),
           ("CBq", 128), ("CBk", 128), ("CBv", 128), ("CBo", 128),
           ("wr0", 8), ("wr2", 8), ("wr3", 8)]
COLUMNS = [("L0bv", 1), ("L0bq", 1), ("L0bk", 1), ("L0bl1", 4), ("L3bq", 1), ("L3bk", 1),
           ("Dbq", 1), ("Dbk", 1), ("Dbv", 1), ("CBbq", 1), ("CBbk", 1),
           ("m0b1", 32), ("m3b1", 16), ("g1", 1), ("b1", 1), ("g2", 1), ("b2", 1), ("sqT", 16),
           ("ctxT", 128)]
ROWS = [("so_b", 128), ("g1", 128), ("b1", 128), ("mo_b", 128), ("g2", 128), ("b2", 128),
        ("l2_b", 128), ("g3", 128), ("b3", 128), ("L0mvb", 128), ("L3vb", 128), ("L3ob", 128),
        ("CBvb", 128), ("CBob", 128), ("Dob", 128), ("sw_b", 8)]
CONSTS = [("ident", 128), ("tri", 128), ("ones", 128), ("first", 8), ("base0", 8), ("base2", 8), ("tokid", 16), ("pos", 5), ("chunk", C)]
for _n, _a in ATT.items():
    CONSTS += [(_n + "_dim", _a["H"]), (_n + "_sel", _a["G"] * _a["H"])]
NEGS = [(_n, _a["R"]) for _n, _a in ATT.items()]


def places(fields):
    at, out = 0, {}
    for name, n in fields:
        out[name] = (at, at + n)
        at += n
    return out, at


SQ_AT, SQ_N = places(SQUARES)
COL_AT, COL_N = places(COLUMNS)
ROW_AT, ROW_N = places(ROWS)
CON_AT, CON_N = places(CONSTS)
NEG_AT, NEG_N = places(NEGS)


def constants():
    out = np.zeros((P, CON_N), np.float32)
    p = np.arange(P)
    out[:, slice(*CON_AT["ident"])] = np.eye(P)
    out[:, slice(*CON_AT["tri"])] = p[:, None] <= p[None, :]
    out[:, slice(*CON_AT["ones"])] = 1.0
    out[:, slice(*CON_AT["first"])] = E - np.arange(E)
    out[:, slice(*CON_AT["base0"])] = CAP0 * np.arange(E) - 1 - SKIP
    out[:, slice(*CON_AT["base2"])] = CAP2 * np.arange(E) - 1 - SKIP
    out[:, slice(*CON_AT["tokid"])] = p[:, None] + P * np.arange(B * C)
    out[:, slice(*CON_AT["pos"])] = p[:, None] + P * np.arange(5)
    out[:, slice(*CON_AT["chunk"])] = (p[:, None] // E) % C == np.arange(C)
    for n, a in ATT.items():
        h = np.arange(a["H"])
        out[:, slice(*CON_AT[n + "_dim"])] = (p[:, None] // a["dh"]) == h
        sel = np.zeros((P, a["G"], a["H"]), np.float32)
        for g in range(a["G"]):
            sel[:, g, :] = (g * a["hb"] + p[:, None] // a["nk"]) == h
        sel[a["RB"]:] = 0
        out[:, slice(*CON_AT[n + "_sel"])] = sel.reshape(P, -1)
    return out


def head_signs():
    out = np.zeros((16, NEG_N), np.float32)
    for n, a in ATT.items():
        of = np.arange(a["R"])[None, :] // a["nk"] == np.arange(a["H"])[:, None]
        out[:a["H"], slice(*NEG_AT[n])] = np.where(of, -1.0, 0.0)
    return out


def build(nc, ins, out):
    ctx = ExitStack()
    with ctx:
        def sb(name, shape, dt=F32):
            return ctx.enter_context(nc.sbuf_tensor(name, shape, dt))

        def under(name, shape):
            with nc.sbuf_tensor(name, shape, F32R) as t:
                return t

        def sem(name):
            return ctx.enter_context(nc.semaphore(name))

        x = sb("x", [P, B * C, D])
        r_ = sb("r", [P, B * C * (D + 1)])
        r = r_[:, 0:B * C * D].rearrange("p (a d) -> p a d", d=D)
        xs = r_[:, :].rearrange("p (a d) -> p a d", d=D + 1)
        xnR = under("xnR", [P, B, S])
        xn = sb("xn", [P, B * C, D])
        xTR = under("xTR", [P, B, S])
        xT = sb("xT", [P, B, S])
        qTR = under("qTR", [P, B, S])
        qT = sb("qT", [P, B, S])
        bigR = under("bigR", [P, 4, B, S])
        big = sb("big", [P, 4, B, S])
        qR = bigR[:, 3, :, :]
        mT = bigR[0:16, 3, :, :]
        sq = sb("sq", [P, SQ_N])
        wout2 = sb("wout2", [64, D])
        col = sb("col", [P, COL_N])
        row = sb("row", [P, ROW_N])
        con = sb("con", [P, CON_N])
        mask_tok = sb("mask_tok", [P, B * C, NK], U8)
        mask_key = sb("mask_key", [NK, B * S], U8)
        mask2 = sb("mask2", [1, B, NK], U8)
        mask2c = sb("mask2c", [NK, B], U8)
        mask3 = sb("mask3", [1, B, NK])
        mask3c = sb("mask3c", [P, B])
        b2m0 = sb("b2m0", [E, D])
        b2m3 = sb("b2m3", [P, D])
        moe_r = under("moe_r", [P, E, 1024])
        moe_w = sb("moe_w", [P, E, 1024])
        RING = 5
        SLOT_BUFS = 10
        ring_r = under("ring_r", [P, RING, 3 * 512])
        ring = sb("ring", [P, RING, 3 * 512])
        sqrow = sb("sqrow", [B * SLOTS, D])
        lng = sb("lng", [B * SLOTS, D])
        lnb = sb("lnb", [B * SLOTS, D])
        KB, KR, VB = {}, {}, {}
        NL0, NL2 = B * ATT["L0"]["R"], B * NK
        kvR = under("kvR", [P, B, ATT["L3"]["R"]])
        kv = sb("kv", [P, NL0 + B * 2 * 144])
        kr = sb("kr", [P, NL0], F32R)
        by_b = lambda ap: ap.rearrange("p (b r) -> p b r", b=B)
        for n in ("L0", "L1", "CB"):
            a = ATT[n]
            w = P + 16 if a["G"] == 2 else a["PD"] + a["H"]
            KB[n] = by_b(kv[:, 0:B * a["R"]])
            KR[n] = by_b(kr[:, 0:B * a["R"]])
            VB[n] = kv[:, NL0:NL0 + B * a["G"] * w].rearrange("p (b g w) -> p b g w", b=B, g=a["G"])
        KR["L3"] = kvR
        KB["L2"] = sb("kb_L2", [P, B, NK])
        KR["L2"] = sb("kr_L2", [P, B, NK], F32R)
        VB["L2"] = sb("vb_L2", [P, B, 1, ATT["L2"]["PD"] + 1])
        ring_flat = ring[:, :, :].rearrange("p a b -> p (a b)")
        w3 = moe_w[:, 0:E // 2, :].rearrange("p a (c n) -> p (a c) n", c=2)
        w1_high = {"m2": ring_r[:, :, :].rearrange("p a b -> p (a b)")[:, 0:E * 512].rearrange("p (e n) -> p e n", e=E),
                   "m3": moe_r[:, E // 2:E // 2 + E // 4, :].rearrange("p a (c n) -> p (a c) n", c=4)}
        w1_low = {"m2": moe_r[:, :, 0:512],
                  "m3": moe_r[:, 0:E // 2, :].rearrange("p a (c n) -> p (a c) n", c=2)[:, :, 0:256]}
        VB["L3"] = ring_flat[:, E * 512:E * 512 + B * 4 * 144].rearrange("p (b g w) -> p b g w", b=B, g=4)
        KB["L3"] = r.rearrange("p (b c) d -> p b (c d)", b=B)
        kts = sb("kts", [P, B * NK])
        rep = sb("rep", [P, B, P])
        vr = sb("vr", [P, B, D])
        st = sb("st", [P, B * C, 6])
        mv = sb("mv", [P, B * C, 2])
        rstd = sb("rstd", [P, B * C])
        half = sb("half", [P, C])
        mx = sb("mx", [P, B * C, 16])
        rs = sb("rs", [P, B * C, 16])
        msc = sb("msc", [P, C, 2, NK])
        madd_t = sb("madd_t", [P, B * C, NK])
        madd_k = r_[0:NK, 0:B * S]
        m2c = sb("m2c", [NK, B])
        m2r = sb("m2r", [1, B, NK], F32R)
        m3c = sb("m3c", [P, B])
        m3r = sb("m3r", [1, B, NK], F32R)
        one_r = sb("one_r", [1, P], F32R)
        neg = sb("neg", [16, NEG_N], F32R)
        rep2 = sb("rep2", [NK, 2, NK])
        lg = sb("lg", [P, B * C, E])
        lg2 = sb("lg2", [P, B * C, E])
        ga = sb("ga", [P, B * C, E])
        gb = sb("gb", [P, 2 * B * C, E])
        gt = sb("gt", [P, B * C, E])
        oh = sb("oh", [P, 2 * B * C, E], BF16)
        tri = sb("tri", [P, P], BF16)
        ones = sb("ones", [P, P], BF16)
        negmean = sb("negmean", [P, B * C])
        gm = sb("gm", [P, B * C])
        gs = sb("gs", [P, B * C])
        gate = sb("gate", [P, B * C, E])
        slot = sb("slot", [P, 2 * B * C])
        have = sb("have", [P, 2 * B * C])
        wgt = sb("wgt", [P, 2 * B * C])
        to_slot = sb("to_slot", [P, 2 * B * C], U32)
        first_n = sb("first_n", [P, E])
        dest_f = sb("dest_f", [P, 2, 5])
        dest = sb("dest", [P, 2 * E * 5], U32)
        zero = sb("zero", [P, D + 1])
        drop = sb("drop", [P, B * C])
        gateT = r_[:, 0:P]
        b2_blocks = rep[:, :, :]
        qblk = sb("qblk", [P, SE, SLOTS])
        dqT = sb("dqT", [P, SLOTS])
        dm = sb("dm", [P, B, 2])
        dsum = sb("dsum", [P, B, 2])
        drs = sb("drs", [P, B, 2])
        pair = rep[:, 0:2, :].rearrange("p a (h s) -> p (a h) s", s=SLOTS)
        attT = sb("attT", [P, B * SLOTS])
        orow = sb("orow", [B * SLOTS, D])
        hrow = vr[0:B * SLOTS, 0, :]
        eb2 = sb("eb2", [B * SLOTS, D])
        oT = sb("oT", [P, B, SLOTS])
        flat = big[:, :, :, :].rearrange("p a b n -> p (a b n)")
        neg_in = flat[0:16, 0:NEG_N]
        hTm = xn[:, 0:8, :].rearrange("p a b -> p (a b)")
        uTm = flat[:, 0:4096].rearrange("p (f n) -> p f n", f=4)
        uu, gg, eu, eg, eb1, ebg = (flat[0:B * SLOTS, 4096 + 512 * j:4608 + 512 * j] for j in range(6))
        xg = flat[:, 0:1290].rearrange("p (g n) -> p g n", g=2)
        xgT = flat[:, 1290:2570].rearrange("p (g n) -> p g n", g=2)
        xg_high = bigR[:, :, :, :].rearrange("p a b n -> p (a b n)")[:, 1290:2570].rearrange("p (g n) -> p g n", g=2)
        xg_low = xTR[:, :, :].rearrange("p a b -> p (a b)")[:, 0:1280].rearrange("p (g n) -> p g n", g=2)
        hid = flat[:, 2570:7690].rearrange("p (g f n) -> p g f n", g=2, f=4)
        yg = flat[:, 0:4096].rearrange("p (k c d) -> p k c d", k=2, c=B * C)
        ysb = qT[:, :, :].rearrange("p a b -> p (a b)")[:, 0:1280].rearrange("p (g n) -> p g n", g=2)
        tok_d = {"m0": nc.dram_tensor("tok0", (E * CAP0, D + 1), F32, kind="Internal").ap(),
                 "m2": nc.dram_tensor("tok2", (E * CAP2, D + 1), F32, kind="Internal").ap()}
        res_d = {"m0": nc.dram_tensor("res0", (B * S, D), F32, kind="Internal").ap(),
                 "m2": nc.dram_tensor("res2", (2 * B * S, D), F32, kind="Internal").ap()}
        ps = [ctx.enter_context(nc.psum_tensor(f"ps{i}", [P, 512], F32)) for i in range(8)]

        ld_w = sem("ld_w")
        ld_w2 = sem("ld_w2")
        ld_c = sem("ld_c")
        ld_r = sem("ld_r")
        ld_x = sem("ld_x")
        ld_s = sem("ld_s")
        ld_m0 = sem("ld_m0")
        ld_m2 = sem("ld_m2")
        ld_m3 = sem("ld_m3")
        ld_e = [sem(f"ld_e{i}") for i in range(SLOT_BUFS)]
        zeroed, cleared = sem("zeroed"), sem("cleared")
        idx_ready, sent = sem("idx_ready"), sem("sent")
        g_ld = [sem("g_ld0"), sem("g_ld1")]
        gT_m, gT_s = sem("gT_m"), sem("gT_s")
        gy_mm, gy_sb = sem("gy_mm"), sem("gy_sb")
        gy_st = [sem("gy_st0"), sem("gy_st1")]
        def tile_sems(name):
            return [sem(f"{name}{t}") for t in range(B)]

        back = tile_sems("back")
        stored = sem("stored")
        dve_chain, pool_chain = sem("dve_chain"), sem("pool_chain")
        negs, masks, minus_half, res_ready = sem("negs"), sem("masks"), sem("minus_half"), sem("res_ready")
        var_ready, rstd_ready = tile_sems("var_ready"), tile_sems("rstd_ready")
        tok_ready, turned, xT_ready = sem("tok_ready"), sem("turned"), sem("xT_ready")
        qR_ready = sem("qR_ready")
        proj_mm, proj_ready = sem("proj_mm"), sem("proj_ready")
        out_mm = sem("out_mm")
        kv_rep, k_mm, k_sb, v_mm, v_sb, kv_ready = (sem(n) for n in ("kv_rep", "k_mm", "k_sb", "v_mm", "v_sb", "kv_ready"))
        s_mm, s_max = tile_sems("s_mm"), tile_sems("s_max")
        m_turned, mT_ready = sem("m_turned"), sem("mT_ready")
        blk_mm, blk_sb = tile_sems("blk_mm"), tile_sems("blk_sb")
        av_mm = sem("av_mm")
        h_mm, h_act, y_mm, y_used = sem("h_mm"), sem("h_act"), sem("y_mm"), sem("y_used")
        lg_mm, oh_ready, cum_mm = sem("lg_mm"), sem("oh_ready"), sem("cum_mm")
        gate_e, gate_ep, gate_ready, gT_mm, gT_sb, gb_mm = (sem(n) for n in ("gate_e", "gate_ep", "gate_ready", "gT_mm", "gT_sb", "gb_mm"))
        dq_mm, qblk_ready, dv_mm, dv_sb, da_mm, att_ready = (
            sem(n) for n in ("dq_mm", "qblk_ready", "dv_mm", "dv_sb", "da_mm", "att_ready"))
        dmax, dnorm, dp_mm, dp_sb = (tile_sems(n) for n in ("dmax", "dnorm", "dp_mm", "dp_sb"))
        nm_ready, tok_act = sem("nm_ready"), sem("tok_act")
        kb_ready, kr_ready, b3_in, split = sem("kb_ready"), sem("kr_ready"), sem("b3_in"), sem("split")
        x_high, x_low = sem("x_high"), sem("x_low")
        x3_dve, x3_gain = sem("x3_dve"), sem("x3_gain")
        o_var, o_rstd = sem("o_var"), sem("o_rstd")
        do_mm, h_rows, hT_mm, hTm_zero, hT_ready, e_mm, e_h, e_silu, e_act, uT_mm, uTm_zero, uT_ready, ey_use, oT_rows, oT_mm, oT_ready, ld_eb = (
            sem(n) for n in ("do_mm", "h_rows", "hT_mm", "hTm_zero", "hT_ready", "e_mm", "e_h", "e_silu", "e_act", "uT_mm",
                             "uTm_zero", "uT_ready", "ey_use", "oT_rows", "oT_mm", "oT_ready", "ld_eb"))

        def W(name):
            return sq[:, slice(*SQ_AT[name])]

        def V(name, i=0, n=None):
            lo, hi = COL_AT[name]
            return col[:, lo + i:lo + i + (n or 1)]

        def ROW(name):
            return row[:, slice(*ROW_AT[name])]

        def K(name):
            return con[:, slice(*CON_AT[name])]

        ident = K("ident")

        def bc(ap, shape, axes):
            for i in axes:
                ap = ap.unsqueeze(i)
            return ap.to_broadcast(shape)

        units0 = {"m0": 0, "m2": 4 * E, "m3": 4 * E + 8 * E}
        cols = lambda c: slice(P * c, P * c + P)
        KV = {"L0": 0, "L1": 1, "L2": 2, "CB": 3, "L3": 4}
        keys_in = V("ctxT", 0, B * NK)
        block = ctx.enter_context(nc.Block())

        def slot_w(q):
            i = q % SLOT_BUFS
            return ring[:, i, :] if i < RING else moe_w[:, :, :].rearrange("p a b -> p (a b)")[:, 1536 * (i - RING):1536 * (i - RING + 1)]

        PLACED = {"m0": dict(cap=CAP0, eg=4, ranks=1), "m2": dict(cap=CAP2, eg=1, ranks=2)}
        for a in PLACED.values():
            a["nb"] = a["cap"] // P
            a["groups"] = E // a["eg"]
            a["gb"] = a["nb"] * a["eg"]
            a["pieces"] = 1 if a["cap"] <= 512 else 2
            a["N"] = a["cap"] // a["pieces"]

        def probs_T(t, c):
            return big[:, 2:4, t, :].rearrange("p g (c n) -> p g c n", c=C)[:, :, c, :]

        def moe_load(sp, name, w, F, done):
            for e in range(E):
                sp.dma_start(w[:, e, 0:F], ins[name + "w1"][e]).then_inc(done, 16)
                sp.dma_start(w[:, e, F:2 * F].rearrange("p (c n) -> p c n", n=D),
                             ins[name + "w2"][e].rearrange("(c p) n -> p c n", p=P)).then_inc(done, 16)

        def stores(name, experts):
            before = 0 if name == "m0" else 16 * PLACED["m0"]["nb"] * E // 2
            return before + 16 * PLACED[name]["nb"] * experts

        @block.sync
        def _(sp):
            sp.dma_start(con[:, :], ins["con"]).then_inc(ld_c, 16)
            sp.dma_start(col[:, :], ins["col"]).then_inc(ld_c, 16)
            sp.dma_start(sq[:, 0:SQ_AT["L0o"][1]], ins["sq"][:, 0:SQ_AT["L0o"][1]]).then_inc(ld_w, 16)
            sp.dma_start(row[:, :], ins["row"].to_broadcast([P, ROW_N])).then_inc(ld_r, 16)
            sp.dma_start(neg_in, ins["neg"]).then_inc(ld_r, 16)
            sp.dma_start(x[:, :, :], ins["x"].rearrange("b (c p) d -> p (b c) d", p=P)).then_inc(ld_x, 16)
            sp.dma_start(sq[:, SQ_AT["L0o"][1]:], ins["sq"][:, SQ_AT["L0o"][1]:]).then_inc(ld_w2, 16)
            sp.dma_start(wout2[:, :], ins["wout2"]).then_inc(ld_w2, 16)
            moe_load(sp, "m0", moe_w, 512, ld_m0)
            sp.wait_ge(zeroed, 1)
            for name, a in PLACED.items():
                nb = E * a["nb"]
                sp.dma_start(tok_d[name].rearrange("(p b) d -> p b d", b=nb), bc(zero[:, :], [P, nb, D + 1], [1])).then_inc(cleared, 16)
                nb = a["ranks"] * B * C
                sp.dma_start(res_d[name].rearrange("(p b) d -> p b d", b=nb), bc(zero[:, 0:D], [P, nb, D], [1])).then_inc(cleared, 16)
            sp.dma_start(mask_tok[:, :, :], ins["mask"].rearrange("b (c p) k -> p (b c) k", p=P)).then_inc(ld_s, 16)
            sp.dma_start(mask_key[:, :], ins["maskT"]).then_inc(ld_s, 16)
            sp.dma_start(mask2[:, :, :], ins["mask2"].rearrange("p (b k) -> p b k", b=B)).then_inc(ld_s, 16)
            sp.dma_start(mask2c[:, :], ins["mask2c"]).then_inc(ld_s, 16)
            sp.dma_start(mask3[:, :, :], ins["mask3"].rearrange("p (b k) -> p b k", b=B)).then_inc(ld_s, 16)
            sp.dma_start(mask3c[:, :], ins["mask3c"]).then_inc(ld_s, 16)
            sp.dma_start(b2m0[:, :], ins["m0b2"]).then_inc(ld_s, 16)
            sp.dma_start(b2m3[:, :], ins["m3b2"]).then_inc(ld_s, 16)
            for b in range(B):
                rows = slice(b * SLOTS, (b + 1) * SLOTS)
                sp.dma_start(sqrow[rows, :], ins["sqrow"]).then_inc(ld_s, 16)
                sp.dma_start(lng[rows, :], ins["lng"]).then_inc(ld_s, 16)
                sp.dma_start(lnb[rows, :], ins["lnb"]).then_inc(ld_s, 16)
                sp.dma_start(eb2[rows, :], ins["eb2"]).then_inc(ld_s, 16)

            def slot_load(q):
                for j in range(3 * q, 3 * q + 3):
                    w = slot_w(q)[:, 512 * (j % 3):512 * (j % 3) + 512]
                    if j < 2 * SE:
                        sp.dma_start(w, ins[("ew1", "ewg")[j % 2]][j // 2]).then_inc(ld_e[q % SLOT_BUFS], 16)
                    else:
                        sp.dma_start(w.rearrange("p (c n) -> p c n", c=4),
                                     ins["ew2"][j - 2 * SE].rearrange("(c p) n -> p c n", p=P)).then_inc(ld_e[q % SLOT_BUFS], 16)

            def placed_traffic(name, k):
                a = PLACED[name]
                g0 = 0 if name == "m0" else PLACED["m0"]["groups"]
                sp.wait_ge(sent, 16 * B * C * (1 if name == "m0" else 3))
                for g in range(a["groups"]):
                    if g >= 2:
                        sp.wait_ge(gT_s, g0 + g - 1)
                    rows = slice(g * a["gb"] * P, (g + 1) * a["gb"] * P)
                    sp.dma_start(xg[:, g % 2, 0:a["gb"] * (D + 1)].rearrange("p (b d) -> p b d", d=D + 1),
                                 tok_d[name][rows, :].rearrange("(b p) d -> p b d", p=P)).then_inc(g_ld[g % 2], 16)
                for i in range(2):
                    sp.wait_ge(gy_st[i], stores(name, E // 2))
                for t in range(B):
                    for q in range(a["ranks"]):
                        rows = slice(q * B * S + t * S, q * B * S + (t + 1) * S)
                        sp.dma_start(yg[:, q, C * t:C * t + C, :], res_d[name][rows, :].rearrange("(c p) d -> p c d", p=P)).then_inc(back[t], 16)

            for q in range(RING):
                slot_load(q)
            placed_traffic("m0", 0)
            for q in range(RING, SLOT_BUFS):
                slot_load(q)
            sp.wait_ge(att_ready, B)
            for b in range(B):
                rows = slice(b * SLOTS, (b + 1) * SLOTS)
                sp.dma_start(eb1[rows, :], ins["eb1"]).then_inc(ld_eb, 16)
                sp.dma_start(ebg[rows, :], ins["ebg"]).then_inc(ld_eb, 16)
            for q in range(SLOT_BUFS, SE):
                sp.wait_ge(ey_use, q - SLOT_BUFS + 1)
                slot_load(q)
            sp.wait_ge(ey_use, SE)
            moe_load(sp, "m2", moe_w, 512, ld_m2)
            placed_traffic("m2", 1)
            moe_load(sp, "m3", w3, 256, ld_m3)
            for t in range(B):
                sp.wait_ge(y_used, E * B + t + 1)
                sp.dma_start(out[t].rearrange("(c p) d -> p c d", p=P), x[:, C * t:C * t + C, :]).then_inc(stored, 16)
            sp.wait_ge(stored, 16 * B)

        @block.tensor
        def _(pe):
            mm = nc.tensor.matmul
            n = dict(turn=0, proj=0, smax=0, att=0, blk=0, g=0, h=0, normed=0, after_average=0)
            source = {"xn": xn, "xs": xs}
            wq = {"L0v": W("L0v"), "L0q": W("L0q"), "L1q": W("L1q"), "Dk": W("Dk"), "CBq": W("CBq"), "L2q": W("L2q"), "L3q": W("L3q")}
            wout = {"L0so": W("L0so"), "L0o": W("L0o"), "L1o": W("L1o"), "CBo": W("CBo"), "L2o": wout2[:, :], "L3o": W("L3o")}
            wr = {k: W(k) for k in ("wr0", "wr2", "wr3")}

            def turn(src, width, affine, fold):
                k = n["turn"]
                n["turn"] += 1
                normed = None if n["after_average"] else n["normed"] - 1
                n["after_average"] = 0

                def stage(t):
                    pe.wait_ge(tok_ready, 4 * k + t + 1)
                    if normed is not None:
                        pe.wait_ge(tok_act, 4 * normed + t + 1)
                    for c in range(C):
                        last = nc.tensor.transpose(ps[2 * t][0:width, cols(c)], source[src][:, C * t + c, 0:width], ident)
                    last.then_inc(turned, 1)
                return stage

            def project(name):
                k = n["turn"] - 1
                n["proj"] += 1
                w = wq[name]
                width = w.shape[1]

                def stage(t):
                    pe.wait_ge(xT_ready, 4 * k + t + 1)
                    mm(ps[2 * t + 1][0:width, :], w, xT[:, t, :], start=True, stop=True).then_inc(proj_mm, 1)
                return stage

            def out_tokens(name):
                w = wout[name]
                width = w.shape[0]
                k = n["proj" if name == "L0so" else "turn"] - 1

                def stage(t):
                    if name == "L0so":
                        pe.wait_ge(proj_ready, 4 * k + t + 1)
                    else:
                        pe.wait_ge(xT_ready, 4 * k + t + 1)
                    src, bank = (qT, 0) if name == "L0so" else (xT, 1)
                    for c in range(C):
                        last = mm(ps[2 * t + bank][:, cols(c)], src[0:width, t, cols(c)], w, start=True, stop=True)
                    last.then_inc(out_mm, 1)
                return stage

            def up(f):
                k, blk = n["turn"] - 1, n["blk"]
                n["blk"] += 1

                def stage(t):
                    if f == 0:
                        pe.wait_ge(xT_ready, 4 * k + t + 1)
                        pe.wait_ge(ld_w2, 32)
                    if f >= 2:
                        pe.wait_ge(blk_sb[t], blk - 1)
                    mm(ps[2 * t + 1 - f % 2][:, :], W("L0l1")[:, cols(f)], xT[:, t, :], start=True, stop=True).then_inc(blk_mm[t], 1)
                return stage

            def down():
                blk = n["blk"]

                def stage(t):
                    pe.wait_ge(blk_sb[t], blk)
                    for c in range(C):
                        for f in range(4):
                            last = mm(ps[2 * t + 1][:, cols(c)], big[:, f, t, cols(c)], W("L0l2")[:, cols(f)], start=f == 0, stop=f == 3)
                    last.then_inc(out_mm, 1)
                return stage

            def score(name, u):
                a = ATT[name]
                R, H, cpu, PD = (a[i] for i in ("R", "H", "cpu", "PD"))
                proj, smax, n_att = n["proj"] - 1, n["smax"], n["att"]
                n["smax"] += 1

                def stage(t):
                    if u == 0:
                        pe.wait_ge(kr_ready, KV[name] + 1)
                        pe.wait_ge(proj_ready, 4 * proj + t + 1)
                        pe.wait_ge(qR_ready, 4 * n_att + t + 1)
                        if name in ("L2", "L3"):
                            pe.wait_ge(masks, 1)
                    if u >= 2:
                        pe.wait_ge(s_max[t], smax - 1)
                    for i in range(cpu):
                        o = ps[2 * t + u % 2][:, i * R:(i + 1) * R]
                        if name == "L3":
                            mm(o, one_r[:, :], bc(m3r[0:1, t, :], [1, H, NK], [1]), start=True, stop=False)
                        if name == "L2":
                            mm(o, one_r[:, :], m2r[0:1, t, :], start=True, stop=False)
                        last = mm(o, qR[0:PD, t, cols(u * cpu + i)], KR[name][0:PD, t, 0:R], start=name not in ("L2", "L3"), stop=True)
                    last.then_inc(s_mm[t], 1)
                return stage

            def maxima(name):
                H, smax = ATT[name]["H"], n["smax"]

                def stage(t):
                    pe.wait_ge(s_max[t], smax)
                    for c in range(C):
                        last = nc.tensor.transpose(ps[2 * t][0:H, cols(c)], mx[:, C * t + c, 0:H], ident)
                    last.then_inc(m_turned, 1)
                n["att"] += 1
                return stage

            def prob(name, g):
                a = ATT[name]
                RB, H, PD = (a[i] for i in ("RB", "H", "PD"))
                att, blk = n["att"] - 1, n["blk"]
                n["blk"] += 1

                def stage(t):
                    if g == 0:
                        pe.wait_ge(mT_ready, 4 * att + t + 1)
                        pe.wait_ge(negs, 1)
                        if name == "L1":
                            pe.wait_ge(masks, 2)
                    if g >= 2:
                        pe.wait_ge(blk_sb[t], blk - 1)
                    o = ps[2 * t + 1 - g % 2][0:RB, :]
                    mm(o, KB[name][0:PD, t, g * RB:(g + 1) * RB], qT[0:PD, t, :], start=True, stop=False)
                    if name == "L1":
                        mm(o, rep2[:, :, :].rearrange("p a b -> p (a b)"), madd_k[:, t * S:(t + 1) * S], start=False, stop=False)
                    mm(o, neg[0:H, NEG_AT[name][0] + g * RB:NEG_AT[name][0] + (g + 1) * RB], mT[0:H, t, :], start=False, stop=True).then_inc(blk_mm[t], 1)
                return stage

            def average(name):
                a = ATT[name]
                RB, G = a["RB"], a["G"]
                wd = a["PD"] + a["H"]
                blk = n["blk"]
                n["after_average"] = 1

                def stage(t):
                    pe.wait_ge(kv_ready, KV[name] + 1)
                    pe.wait_ge(blk_sb[t], blk)
                    for c in range(C):
                        o = ps[2 * t + c // 2][:, (c % 2) * wd:(c % 2 + 1) * wd]
                        for g in range(G):
                            last = mm(o, big[0:RB, g, t, cols(c)], VB[name][0:RB, t, g, 0:wd], start=g == 0, stop=g == G - 1)
                    last.then_inc(av_mm, 1)
                return stage

            def router(name):
                k = n["turn"] - 1

                def stage(t):
                    pe.wait_ge(xT_ready, 4 * k + t + 1)
                    for c in range(C):
                        last = mm(ps[2 * t + 1][:, c * E:(c + 1) * E], xT[:, t, cols(c)], wr[name], start=True, stop=True)
                    last.then_inc(lg_mm, 1)
                return stage

            def values():
                k = n["turn"] - 1

                def stage(t):
                    pe.wait_ge(xT_ready, 4 * k + t + 1)
                    for c in range(C):
                        last = mm(ps[2 * t][:, cols(c)], xT[:, t, cols(c)], W("Dv"), start=True, stop=True)
                    last.then_inc(dv_mm, 1)
                return stage

            def dscore(g):
                proj = n["proj"] - 1

                def stage(t):
                    if g == 0:
                        pe.wait_ge(proj_ready, 4 * proj + t + 1)
                    else:
                        pe.wait_ge(dv_sb, t + 1)
                    mm(ps[2 * t + 1 - g][:, :], qblk[:, 8 * g:8 * g + 8, :].rearrange("p h s -> p (h s)"), qT[:, t, :],
                       start=True, stop=True).then_inc(blk_mm[t], 1)
                n["blk"] += 1
                return stage

            def dturn(g):
                def stage(t):
                    pe.wait_ge(dnorm[t], g + 1)
                    for c in range(C):
                        last = nc.tensor.transpose(ps[2 * t + 1 - g][:, cols(c)], big[:, g, t, cols(c)], ident)
                    last.then_inc(dp_mm[t], 1)
                return stage

            def daverage():
                def stage(t):
                    pe.wait_ge(dp_sb[t], 2)
                    o = ps[2 * t][:, 0:2 * P]
                    for c in range(C):
                        last = mm(o, r[:, C * t + c, :], probs_T(t, c), start=c == 0, stop=c == C - 1)
                    last.then_inc(da_mm, 1)
                return stage

            def scale(where):
                n["normed"] += 1

            def count(name):
                k = 0 if name == "m0" else 1

                def stage(t):
                    pe.wait_ge(oh_ready, 4 * k + t + 1)
                    o = ps[2 * t][:, 0:C * E]
                    mm(o, tri[:, :], oh[:, C * t:C * t + C, :].rearrange("p a b -> p (a b)"), start=True, stop=False)
                    for c in range(C * t + C - 1):
                        later = min(C, C * t + C - 1 - c)
                        last = mm(o[:, (C - later) * E:], ones[:, :], bc(oh[:, c, :], [P, later, E], [1]),
                                  start=False, stop=c == C * t + C - 2)
                    last.then_inc(cum_mm, 1)
                return stage

            make = dict(turn=turn, project=project, out=out_tokens, up=up, down=down, score=score, maxima=maxima, prob=prob,
                        average=average, router=router, values=values, dscore=dscore, dturn=dturn, daverage=daverage, count=count, scale=scale)

            def prepare(name, keys):
                a = ATT[name]
                k = KV[name]
                pe.wait_ge(kv_rep, k + 1)
                mm(ps[0][0:a["PD"], 0:B * a["nk"]], W(name + "k"), keys, start=True, stop=True).then_inc(k_mm, 1)
                wv = W("L0mv") if name == "L0" else W(name + "v")
                for b in range(B):
                    last = mm(ps[1][0:a["RB"], b * a["PD"]:(b + 1) * a["PD"]], rep[:, b, 0:a["RB"]], wv,
                              start=True, stop=True)
                last.then_inc(v_mm, 1)
                pe.wait_ge(k_sb, k + 1)
                pe.wait_ge(v_sb, k + 1)

            def count_second():
                nb = B * C
                for c in range(nb):
                    mm(ps[2][:, 0:(nb + 1) * E], ones[:, :], bc(oh[:, c, :], [P, nb + 1, E], [1]), start=c == 0, stop=False)
                pe.wait_ge(oh_ready, 2 * B + 1)
                o = ps[2][:, E:(nb + 1) * E]
                mm(o, tri[:, :], oh[:, nb:2 * nb, :].rearrange("p a b -> p (a b)"), start=False, stop=False)
                for c in range(nb - 1):
                    last = mm(o[:, (c + 1) * E:], ones[:, :], bc(oh[:, nb + c, :], [P, nb - 1 - c, E], [1]),
                              start=False, stop=c == nb - 2)
                last.then_inc(cum_mm, 1)

            def product(o, high, low, x_high_, x_low_):
                mm(o, high, x_high_, start=True, stop=False)
                mm(o, high, x_low_, start=False, stop=False)
                mm(o, low, x_high_, start=False, stop=True).then_inc(h_mm, 1)

            def placed(name, k, loaded, bias, prepares):
                a = PLACED[name]
                nb, gb, eg, N = a["nb"], a["gb"], a["eg"], a["N"]
                if name == "m2":
                    pe.wait_ge(idx_ready, 2 * B)
                    count_second()
                pe.wait_ge(idx_ready, B if name == "m0" else 2 * B + 1)
                if name == "m0":
                    mm(ps[2][:, 0:SLOTS], W("Dq"), V("sqT", 0, SLOTS), start=True, stop=True).then_inc(dq_mm, 1)
                    pe.wait_ge(qblk_ready, 1)
                for att in prepares:
                    prepare(att, keys_in)
                g0, h0 = n["g"], n["h"]
                pe.wait_ge(loaded, 32 * E)
                if name == "m2":
                    pe.wait_ge(split, 8)

                def turn_group(g):
                    done = sum(1 for q in range(g + 1) if q % 2 == g % 2) + sum(1 for q in range(g0) if q % 2 == g % 2)
                    pe.wait_ge(g_ld[g % 2], 16 * done)
                    if g >= 1:
                        pe.wait_ge(gT_s, g0 + g)
                    for b in range(gb):
                        last = nc.tensor.transpose(ps[b // 4][:, cols(b % 4)], xg[:, g % 2, b * (D + 1):b * (D + 1) + D], ident)
                    last.then_inc(gT_m, 1)
                    n["g"] += 1

                def hidden(e):
                    g = e // eg
                    pe.wait_ge(gT_s, g0 + g + 1)
                    at = (e % eg) * a["cap"]
                    for f in range(4):
                        for j in range(a["pieces"]):
                            u = n["h"] - h0
                            if u >= 4:
                                pe.wait_ge(h_act, n["h"] - 3)
                            tokens = slice(at + j * N, at + (j + 1) * N)
                            if name == "m2":
                                high, low = w1_high[name][:, e, cols(f)], w1_low[name][:, e, cols(f)]
                                product(ps[2 + u % 4][:, 0:N], high, low, xg_high[:, g % 2, tokens], xg_low[:, g % 2, tokens])
                            else:
                                mm(ps[2 + u % 4][:, 0:N], moe_w[:, e, cols(f)], xgT[:, g % 2, tokens],
                                   start=True, stop=True).then_inc(h_mm, 1)
                            n["h"] += 1
                    if e % eg == eg - 1 and g + 2 < a["groups"]:
                        turn_group(g + 2)
                    return n["h"]

                def results(e, units):
                    pe.wait_ge(h_act, units)
                    if e >= 2 or (e >= 1 and nb > 4):
                        pe.wait_ge(gy_sb, k * E + e - (1 if nb <= 4 else 0))
                    for b in range(nb):
                        o = ps[6 + (b // 4 if nb > 4 else e % 2)][:, cols(b % 4)]
                        for f in range(4):
                            last = mm(o, hid[:, e % 2, f, cols(b)], moe_w[:, e, 512 + P * f:512 + P * f + P],
                                      start=f == 0, stop=f == 3 and bias is None)
                        if bias is not None:
                            last = mm(o, ident[0:E, e:e + 1].to_broadcast([E, P]), bias[:, :], start=False, stop=True)
                    last.then_inc(gy_mm, 1)

                turn_group(0)
                turn_group(1)
                units = hidden(0)
                for e in range(E):
                    nxt = hidden(e + 1) if e + 1 < E else None
                    results(e, units)
                    units = nxt

            def mixture(w, F, loaded, bias):
                FC = F // P
                pe.wait_ge(oh_ready, 2 * B + 2)
                pe.wait_ge(split, 16)

                def hidden(i):
                    e, t = divmod(i, B)
                    if e == 0:
                        pe.wait_ge(x_low, t + 1)
                    for f in range(FC):
                        if i * FC + f >= 6:
                            pe.wait_ge(h_act, n["h"] - 5)
                        product(ps[(i * FC + f) % 6][:, :], w1_high["m3"][:, e, cols(f)], w1_low["m3"][:, e, cols(f)],
                                qTR[:, t, :], xnR[:, t, :])
                        n["h"] += 1
                    return n["h"]

                def outputs(i, units):
                    pe.wait_ge(h_act, units)
                    pe.wait_ge(y_used, B + i - 1)
                    e = i // B
                    for c in range(C):
                        for f in range(FC):
                            last = mm(ps[7 - i % 2][:, cols(c)], big[:, f, i % B, cols(c)],
                                      w[:, e, F + P * f:F + P * f + P], start=f == 0, stop=f == FC - 1)
                    last.then_inc(y_mm, 1)

                units = [hidden(i) for i in range(B)]
                pe.wait_ge(gate_ready, 1)
                nc.tensor.transpose(ps[6][:, 0:P], gate[:, :, :].rearrange("p a b -> p (a b)"), ident).then_inc(gT_mm, 1)
                pe.wait_ge(loaded, 32 * E)
                pe.wait_ge(gT_sb, 1)
                for t in range(B):
                    if t >= 2:
                        pe.wait_ge(y_used, t - 1)
                    mine = slice(C * E * t, C * E * (t + 1))
                    mm(ps[7 - t % 2][:, :], gateT[mine, :], bias[mine, :, :].rearrange("p c d -> p (c d)"),
                       start=True, stop=True).then_inc(gb_mm, 1)
                for i in range(E * B):
                    outputs(i, units[i])
                    if i + B < E * B:
                        units.append(hidden(i + B))

            def slot_experts():
                rows = B * SLOTS
                pe.wait_ge(att_ready, B)
                mm(ps[0][0:rows, 0:D], attT[:, :], W("Do"), start=True, stop=True).then_inc(do_mm, 1)
                pe.wait_ge(h_rows, 1)
                nc.tensor.transpose(ps[1][:, 0:rows], hrow, ident[0:rows, 0:rows]).then_inc(hT_mm, 1)
                pe.wait_ge(hT_ready, 1)

                def unit(j):
                    q = j // 3
                    if j % 3 == 0:
                        pe.wait_ge(ld_e[q % SLOT_BUFS], 48 * (q // SLOT_BUFS + 1))
                    return slot_w(q)[:, 512 * (j % 3):512 * (j % 3) + 512]

                for j in range(2 * SE):
                    e = j // 2
                    last = mm(ps[3 + j % 2][0:rows, :], hTm[:, rows * e:rows * (e + 1)], unit(j), start=e == 0, stop=e == SE - 1)
                    if j == 2 * SE - 1:
                        last.then_inc(e_mm, 1)
                    elif j % 3 == 2:
                        last.then_inc(ey_use, 1)
                pe.wait_ge(e_act, 1)
                for f in range(4):
                    last = nc.tensor.transpose(ps[6][:, rows * f:rows * (f + 1)], uu[:, cols(f)], ident[0:rows, 0:rows])
                last.then_inc(uT_mm, 1)
                pe.wait_ge(uT_ready, 1)
                for e in range(SE):
                    j = 2 * SE + e
                    w = unit(j)
                    for f in range(4):
                        last = mm(ps[5][0:rows, 0:D], uTm[:, f, rows * e:rows * (e + 1)], w[:, cols(f)],
                                  start=e == 0 and f == 0, stop=e == SE - 1 and f == 3)
                    if e == 0:
                        last.then_inc(ey_use, 1)
                    elif j % 3 == 2:
                        last.then_inc(ey_use, 1)
                pe.wait_ge(oT_rows, 1)
                nc.tensor.transpose(ps[7][:, 0:rows], orow[:, :], ident[0:rows, 0:rows]).then_inc(oT_mm, 1)
                pe.wait_ge(oT_ready, 1)
                prepare("CB", oT[:, :, :].rearrange("p b s -> p (b s)"))

            pe.wait_ge(ld_w, 16)
            pe.wait_ge(ld_c, 32)
            prepare("L0", keys_in)
            wavefront(make, SEQ0)
            placed("m0", 0, ld_m0, b2m0, ["L1", "L2"])
            wavefront(make, SEQ1)
            slot_experts()
            wavefront(make, SEQ2)
            placed("m2", 1, ld_m2, None, ["L3"])
            wavefront(make, SEQ3)
            mixture(w3, 256, ld_m3, b2_blocks)

        @block.scalar
        def _(act):
            A = nc.scalar.activation
            n = dict(turn=0, proj=0, blk=0, h=0, moe=0, norm=0, scale=0)

            def turn(src, width, affine, fold):
                k = n["turn"]
                n["turn"] += 1

                def stage(t):
                    act.wait_ge(turned, 4 * k + t + 1)
                    if affine:
                        A(xT[:, t, :], ps[2 * t][:, :], ACT.Identity, bias=V("b" + affine), scale=V("g" + affine)).then_inc(xT_ready, 1)
                    else:
                        A(xT[0:width, t, :], ps[2 * t][0:width, :], ACT.Identity).then_inc(xT_ready, 1)
                        if k == LAST_TURN:
                            A(qTR[:, t, :], ps[2 * t][:, :], ACT.Identity).then_inc(x_high, 1)
                return stage

            def project(name):
                k = n["proj"]
                n["proj"] += 1
                bias = {"L0v": "L0bv", "L0q": "L0bq", "Dk": "Dbk", "CBq": "CBbq", "L3q": "L3bq"}.get(name)
                width = 64 if name == "L2q" else D

                def stage(t):
                    act.wait_ge(proj_mm, 4 * k + t + 1)
                    A(qT[0:width, t, :], ps[2 * t + 1][0:width, :], ACT.Identity, bias=V(bias) if bias else 0.0).then_inc(proj_ready, 1)
                    if name in ("L0q", "L1q", "CBq", "L2q", "L3q"):
                        A(qR[0:width, t, :], ps[2 * t + 1][0:width, :], ACT.Identity,
                          bias=V(bias) if bias else 0.0).then_inc(qR_ready, 1)
                return stage

            def prob(name, g):
                a = ATT[name]
                RB = a["RB"]
                blk = n["blk"]
                n["blk"] += 1

                def stage(t):
                    act.wait_ge(blk_mm[t], blk + 1)
                    if name in ("L2", "L3"):
                        act.wait_ge(masks, 1)
                    bias = m2c[:, t:t + 1] if name == "L2" else m3c[:, t:t + 1] if name == "L3" else 0.0
                    A(big[0:RB, g, t, :], ps[2 * t + 1 - g % 2][0:RB, :], ACT.Exp, bias=bias, scale=a["scale"]).then_inc(blk_sb[t], 1)
                return stage

            def up(f):
                blk = n["blk"]
                n["blk"] += 1

                def stage(t):
                    act.wait_ge(blk_mm[t], blk + 1)
                    A(big[:, f, t, :], ps[2 * t + 1 - f % 2][:, :], ACT.Relu, bias=V("L0bl1", f)).then_inc(blk_sb[t], 1)
                return stage

            def dscore(g):
                blk = n["blk"]
                n["blk"] += 1

                def stage(t):
                    act.wait_ge(dmax[t], g + 1)
                    A(big[:, g, t, :], ps[2 * t + 1 - g][:, :], ACT.Exp, bias=dm[:, t, g:g + 1],
                      scale=ATT["CB"]["scale"], accum_out=dsum[:, t, g:g + 1]).then_inc(blk_sb[t], 1)
                return stage

            def dturn(g):
                def stage(t):
                    act.wait_ge(dp_mm[t], g + 1)
                    A(big[:, 2 + g, t, :], ps[2 * t + 1 - g][:, :], ACT.Identity).then_inc(dp_sb[t], 1)
                return stage

            def stats(added, dst):
                n["norm"] += 1
                return None

            def scale(where):
                k, norm = n["scale"], n["norm"]
                n["scale"] += 1
                src = r if norm in (2, 3, NORM_X3) else x
                dst = {"xn": xn, "xs": xs, "x3": xn}[where]

                def stage(t):
                    act.wait_ge(nm_ready, 4 * k + t + 1)
                    if norm == NORM_X3 + 1 and t < B - 1:
                        act.wait_ge(var_ready[t + 1], norm)
                    for c in range(C * t + C - ACT_SHARE, C * t + C):
                        last = A(dst[:, c, 0:D], src[:, c, :], ACT.Identity, bias=negmean[:, c:c + 1], scale=rstd[:, c:c + 1])
                    last.then_inc(tok_act, 1)
                return stage

            make = dict(stats=stats, scale=scale, turn=turn, project=project, prob=prob, up=up, dscore=dscore, dturn=dturn)

            def round_keys(name):
                a = ATT[name]
                act.wait_ge(kb_ready, KV[name] + 1)
                A(KR[name][0:a["PD"], :, :], KB[name][0:a["PD"], :, :], ACT.Identity).then_inc(kr_ready, 1)

            def chances():
                act.wait_ge(gate_e, n["moe"] + 1)
                A(ga[:, :, :], ga[:, :, :], ACT.Exp).then_inc(gate_ep, 1)
                n["moe"] += 1

            def placed(name, k, fn, bias):
                a = PLACED[name]
                for e in range(E):
                    if e >= 2:
                        act.wait_ge(gy_mm, k * E + e - 1)
                    if name == "m2" and e == 1:
                        round_keys("L3")
                    for f in range(4):
                        for j in range(a["pieces"]):
                            u = n["h"] - units0[name]
                            act.wait_ge(h_mm, n["h"] + 1)
                            A(hid[:, e % 2, f, j * a["N"]:(j + 1) * a["N"]], ps[2 + u % 4][:, 0:a["N"]], fn,
                              bias=V(bias, e * 4 + f) if bias else 0.0).then_inc(h_act, 1)
                            n["h"] += 1

            def mixture(F, fn, bias):
                FC = F // P
                for i in range(E * B):
                    e, t = divmod(i, B)
                    if i == B:
                        act.wait_ge(gT_mm, 1)
                        A(gateT, ps[6][:, 0:P], ACT.Identity).then_inc(gT_sb, 1)
                    for f in range(FC):
                        act.wait_ge(h_mm, n["h"] + 1)
                        if i >= B and f == 0:
                            act.wait_ge(y_mm, i - B + 1)
                        A(big[:, f, i % B, :], ps[(i * FC + f) % 6][:, :], fn,
                          bias=V(bias, e * FC + f)).then_inc(h_act, 1)
                        n["h"] += 1

            act.wait_ge(ld_c, 32)
            round_keys("L0")
            wavefront(make, SEQ0)
            round_keys("L1")
            round_keys("L2")
            placed("m0", 0, ACT.Relu, "m0b1")
            wavefront(make, SEQ1)
            act.wait_ge(e_h, 1)
            A(eu, uu, ACT.Silu).then_inc(e_silu, 1)
            act.wait_ge(e_h, 2)
            A(eg, gg, ACT.Silu).then_inc(e_silu, 1)
            round_keys("CB")
            wavefront(make, SEQ2)
            chances()
            placed("m2", 1, ACT.Gelu, None)
            wavefront(make, SEQ3)
            chances()
            mixture(256, ACT.Gelu, "m3b1")

        @block.vector
        def _(dve):
            v = nc.vector
            n = dict(chain=0, out=0, smax=0, att=0, lg=0, norm=0, fold=0, two=0)
            nb = B * C

            def link(i):
                n["chain"] += 1
                i.then_inc(dve_chain, 1)
                dve.wait_ge(dve_chain, n["chain"])

            def chunks(t):
                return slice(C * t, C * t + C)

            def stats(added, dst):
                n["norm"] += 1
                fold, out_k = n["fold"], n["out"]
                if added == "out":
                    n["out"] += 1
                d = r if dst == "r" else x

                def stage(t):
                    tt = chunks(t)
                    if fold:
                        dve.wait_ge(res_ready, 4 * (fold - 1) + t + 1)
                    if added == "out":
                        dve.wait_ge(out_mm, 4 * out_k + t + 1)
                        bank = ps[2 * t + (0 if out_k == 0 else 1)]
                        link(v.tensor_tensor(d[:, tt, :], d[:, tt, :], bank[:, :].rearrange("p (c d) -> p c d", c=C), ALU.add))
                    elif added == "x3":
                        dve.wait_ge(x3_gain, t + 1)
                        dve.wait_ge(b3_in, t + 1)
                        link(v.tensor_tensor(x[:, tt, :], x[:, tt, :], xn[:, tt, :], ALU.add))
                    elif added:
                        fetched(added, t)
                    for c in range(C):
                        i = v.bn_stats(st[:, C * t + c, :], d[:, C * t + c, :])
                    link(i)
                    for c in range(C):
                        i = v.bn_aggr(mv[:, C * t + c, :], st[:, C * t + c, :])
                    i.then_inc(var_ready[t], 1)
                return stage

            def scale(where):
                k = n["norm"]
                src = r if (where == "xn" and k in (2, 3)) or where == "x3" else x
                dst = {"xn": xn, "xs": xs, "x3": xn}[where]

                def stage(t):
                    dve.wait_ge(rstd_ready[t], k)
                    for c in range(C - ACT_SHARE):
                        i = v.tensor_scalar(dst[:, C * t + c, 0:D], src[:, C * t + c, :], mv[:, C * t + c, 0:1],
                                            rstd[:, C * t + c:C * t + c + 1], ALU.subtract, ALU.mult)
                    if where == "x3":
                        i.then_inc(x3_dve, 1)
                        return
                    if where == "xs":
                        i = v.tensor_copy(xs[:, chunks(t), D], K("tokid")[:, chunks(t)])
                    i.then_inc(tok_ready, 1)
                return stage

            def turn(src, width, affine, fold):
                if fold:
                    n["fold"] += 1
                return None

            def score(name, u):
                a = ATT[name]
                R, H, cpu = (a[i] for i in ("R", "H", "cpu"))
                n["smax"] += 1
                smax = n["smax"]

                def stage(t):
                    dve.wait_ge(s_mm[t], smax)
                    c0 = C * t + u * cpu
                    src = ps[2 * t + u % 2][:, 0:cpu * R].rearrange("p (c h k) -> p c h k", c=cpu, h=H)
                    if name == "L1":
                        if t:
                            dve.wait_ge(s_max[t - 1], smax)
                        link(v.tensor_tensor(msc[:, :, :, :], src, bc(madd_t[:, c0:c0 + C, :], [P, C, H, NK], [2]), ALU.add))
                        src = msc[:, :, :, :]
                    v.tensor_reduce(mx[:, c0:c0 + cpu, 0:H], src, AX.X, ALU.max).then_inc(s_max[t], 1)
                return stage

            def maxima(name):
                H, att = ATT[name]["H"], n["att"]
                n["att"] += 1

                def stage(t):
                    dve.wait_ge(m_turned, 4 * att + t + 1)
                    v.tensor_copy(mT[0:H, t, :], ps[2 * t][0:H, :]).then_inc(mT_ready, 1)
                return stage

            def average(name):
                a = ATT[name]
                H, PD, dh = (a[i] for i in ("H", "PD", "dh"))
                wd = PD + H
                att, fold = n["att"] - 1, n["fold"]

                def stage(t):
                    if fold:
                        dve.wait_ge(res_ready, 4 * (fold - 1) + t + 1)
                    dve.wait_ge(av_mm, 4 * att + t + 1)
                    part = lambda j: ps[2 * t + j][:, 0:2 * wd].rearrange("p (c w) -> p c w", c=2)
                    pair_ = lambda j: slice(C * t + 2 * j, C * t + 2 * j + 2)
                    for j in range(2):
                        i = v.reciprocal(rs[:, pair_(j), 0:H], part(j)[:, :, PD:wd])
                    link(i)
                    for j in range(2):
                        i = v.tensor_tensor(xn[:, pair_(j), 0:PD].rearrange("p c (h d) -> p c h d", h=H),
                                            part(j)[:, :, 0:PD].rearrange("p c (h d) -> p c h d", h=H),
                                            bc(rs[:, pair_(j), 0:H], [P, 2, H, dh], [3]), ALU.mult)
                    i.then_inc(tok_ready, 1)
                return stage

            def router(name):
                k = n["lg"]
                n["lg"] += 1

                def stage(t):
                    dve.wait_ge(lg_mm, 4 * k + t + 1)
                    s_ = ps[2 * t + 1][:, 0:C * E].rearrange("p (c e) -> p c e", e=E)
                    if name == "wr0":
                        link(v.tensor_tensor(lg[:, chunks(t), :], s_, bc(ROW("sw_b"), [P, C, E], [1]), ALU.add))
                    else:
                        link(v.tensor_copy(lg[:, chunks(t), :], s_))
                return stage

            def values():
                def stage(t):
                    dve.wait_ge(dv_mm, t + 1)
                    v.tensor_copy(r[:, chunks(t), :], ps[2 * t][:, :].rearrange("p (c d) -> p c d", c=C)).then_inc(dv_sb, 1)
                return stage

            def dscore(g):
                blk = dblk0 + g

                def stage(t):
                    dve.wait_ge(blk_mm[t], blk + 1)
                    link(v.tensor_reduce(dm[:, t, g:g + 1], ps[2 * t + 1 - g][:, :], AX.X, ALU.max))
                    v.tensor_scalar(dm[:, t, g:g + 1], dm[:, t, g:g + 1], -ATT["CB"]["scale"], None, ALU.mult).then_inc(dmax[t], 1)
                return stage

            dblk0 = sum(q[0] in ("prob", "up") for q in SEQ0 + SEQ1)

            def dturn(g):
                def stage(t):
                    dve.wait_ge(blk_sb[t], dblk0 + g + 1)
                    link(v.reciprocal(drs[:, t, g:g + 1], dsum[:, t, g:g + 1]))
                    v.tensor_scalar(big[:, g, t, :], big[:, g, t, :], drs[:, t, g:g + 1], None, ALU.mult).then_inc(dnorm[t], 1)
                return stage

            def daverage():
                def stage(t):
                    dve.wait_ge(da_mm, t + 1)
                    link(v.tensor_tensor(pair[:, :, :], ps[2 * t][:, 0:2 * P].rearrange("p (h s) -> p h s", h=SE),
                                         bc(K("CB_dim"), [P, SE, SLOTS], [2]), ALU.mult))
                    a_ = attT[:, SLOTS * t:SLOTS * (t + 1)]
                    link(v.tensor_reduce(a_, pair[:, :, :].rearrange("p h s -> p s h"), AX.X, ALU.add))
                    v.tensor_scalar(a_, a_, V("Dbv"), None, ALU.add).then_inc(att_ready, 1)
                return stage

            def first_largest(src, dst, kk):
                m = kk.stop - kk.start
                link(v.tensor_reduce(gm[:, kk], src, AX.X, ALU.max))
                link(v.tensor_tensor(gt[:, kk, :], src, bc(gm[:, kk], [P, m, E], [2]), ALU.is_equal))
                link(v.tensor_tensor(gt[:, kk, :], gt[:, kk, :], bc(K("first"), [P, m, E], [1]), ALU.mult))
                link(v.tensor_reduce(gs[:, kk], gt[:, kk, :], AX.X, ALU.max))
                v.tensor_tensor(dst, gt[:, kk, :], bc(gs[:, kk], [P, m, E], [2]), ALU.is_equal).then_inc(oh_ready, 1)

            def places(counted, kk, capacity, base):
                m = kk.stop - kk.start
                v.scalar_tensor_tensor(out=gb[:, kk, :], in0=counted, scalar=float(capacity), in1=oh[:, kk, :],
                                       op0=ALU.is_le, op1=ALU.mult)
                g = gt[:, kk.start % nb:kk.start % nb + m, :]
                link(v.tensor_tensor(g, counted, bc(K(base), [P, m, E], [1]), ALU.add))
                link(v.tensor_tensor(g, g, gb[:, kk, :], ALU.mult))
                link(v.tensor_reduce(slot[:, kk], g, AX.X, ALU.add))
                v.tensor_scalar(to_slot[:, kk], slot[:, kk], SKIP, None, ALU.add).then_inc(idx_ready, 1)

            def choose(name):
                def stage(t):
                    first_largest(lg[:, chunks(t), :], oh[:, chunks(t), :], chunks(t))
                return stage

            def place(name):
                k = 0 if name == "m0" else 1

                def stage(t):
                    dve.wait_ge(cum_mm, 4 * k + t + 1)
                    places(ps[2 * t][:, 0:C * E].rearrange("p (c e) -> p c e", e=E), chunks(t), PLACED[name]["cap"],
                           "base0" if name == "m0" else "base2")
                return stage

            make = dict(choose=choose, place=place, stats=stats, scale=scale, turn=turn, score=score, maxima=maxima, average=average, router=router,
                        values=values, dscore=dscore, dturn=dturn, daverage=daverage)

            def prepared(name):
                a = ATT[name]
                k = KV[name]
                dve.wait_ge(k_mm, k + 1)
                if k >= 1:
                    dve.wait_ge(kv_ready, k)
                o, i_ = kts[0:a["PD"], 0:B * a["nk"]], ps[0][0:a["PD"], 0:B * a["nk"]]
                b = {"L0": "L0bk", "L3": "L3bk", "CB": "CBbk"}.get(name)
                if b:
                    v.tensor_scalar(o, i_, V(b), None, ALU.add).then_inc(k_sb, 1)
                else:
                    v.tensor_copy(o, i_).then_inc(k_sb, 1)
                dve.wait_ge(v_mm, k + 1)
                RB, PD = a["RB"], a["PD"]
                o = vr[0:RB, :, 0:PD]
                i_ = ps[1][0:RB, 0:B * PD].rearrange("p (b d) -> p b d", b=B)
                b = {"L0": "L0mvb", "L3": "L3vb", "CB": "CBvb"}.get(name)
                if b:
                    v.tensor_tensor(o, i_, bc(ROW(b)[0:RB, :], [RB, B, PD], [1]), ALU.add).then_inc(v_sb, 1)
                else:
                    v.tensor_copy(o, i_).then_inc(v_sb, 1)

            def second_largest():
                v.scalar_tensor_tensor(out=lg2[:, :, :], in0=oh[:, 0:nb, :], scalar=-BIG, in1=lg[:, :, :],
                                       op0=ALU.mult, op1=ALU.add)
                v.tensor_tensor(ga[:, :, :], lg[:, :, :], bc(gm[:, :], [P, nb, E], [2]), ALU.subtract).then_inc(gate_e, 1)
                n["two"] += 1

            def evacuate(name, k):
                a = PLACED[name]
                nb_, gb_, eg = a["nb"], a["gb"], a["eg"]
                g0 = 0 if name == "m0" else PLACED["m0"]["groups"]

                def group(g):
                    dve.wait_ge(gT_m, g0 + g + 1)
                    if g >= 2:
                        dve.wait_ge(h_mm, units0[name] + 4 * a["pieces"] * eg * (g - 1))
                    for j in range(0, gb_, 4):
                        m = min(4, gb_ - j)
                        piece = slice(j * P, (j + m) * P)
                        if name == "m2":
                            link(v.tensor_copy(xg_high[:, g % 2, piece], ps[j // 4][:, 0:m * P]))
                            v.tensor_tensor(xg_low[:, g % 2, piece], ps[j // 4][:, 0:m * P], xg_high[:, g % 2, piece].bitcast(F32),
                                            ALU.subtract)
                        else:
                            v.tensor_copy(xgT[:, g % 2, piece], ps[j // 4][:, 0:m * P])
                    number = xg[:, g % 2, 0:gb_ * (D + 1)].rearrange("p (b d) -> p b d", d=D + 1)[:, :, D]
                    at = (40 if k else 0) + g * gb_
                    if a["ranks"] == 1:
                        i = v.tensor_copy(dest[:, at:at + gb_], number)
                    else:
                        link(v.tensor_scalar(dest_f[:, g % 2, :], K("pos"), first_n[:, g:g + 1], float(B * S), ALU.is_ge, ALU.mult))
                        i = v.tensor_tensor(dest[:, at:at + gb_], dest_f[:, g % 2, :], number, ALU.add)
                    i.then_inc(gT_s, 1)

                group(0)
                group(1)
                for e in range(E):
                    g = e // eg
                    if e % eg == eg - 1 and g + 2 < a["groups"]:
                        group(g + 2)
                    dve.wait_ge(gy_mm, k * E + e + 1)
                    if e >= 2 or k:
                        dve.wait_ge(gy_st[e % 2], stores(name, e // 2))
                    for j in range(0, nb_, 4):
                        m = min(4, nb_ - j)
                        i = v.tensor_copy(ysb[:, e % 2, j * P:(j + m) * P], ps[6 + (j // 4 if nb_ > 4 else e % 2)][:, 0:m * P])
                    i.then_inc(gy_sb, 1)

            def fetched(name, t):
                ranks = PLACED[name]["ranks"]
                dve.wait_ge(back[t], 16 * (1 if name == "m0" else 3))
                for q in range(ranks):
                    for c in range(C * t, C * t + C):
                        i = v.scalar_tensor_tensor(out=x[:, c, :], in0=yg[:, q, c, :], scalar=wgt[:, nb * q + c:nb * q + c + 1],
                                                   in1=x[:, c, :], op0=ALU.mult, op1=ALU.add)
                    link(i)

            def add_bias_rows():
                for t in range(B):
                    dve.wait_ge(gb_mm, t + 1)
                    v.tensor_tensor(x[:, chunks(t), :], x[:, chunks(t), :],
                                    ps[7 - t % 2][:, :].rearrange("p (c d) -> p c d", c=C), ALU.add).then_inc(y_used, 1)

            def experts():
                for i in range(E * B):
                    e, t = divmod(i, B)
                    dve.wait_ge(y_mm, i + 1)
                    dve.wait_ge(y_used, i + 1)
                    for c in range(C):
                        last = v.scalar_tensor_tensor(out=x[:, C * t + c, :], in0=ps[7 - i % 2][:, cols(c)],
                                                      scalar=gate[:, C * t + c, e:e + 1], in1=x[:, C * t + c, :],
                                                      op0=ALU.mult, op1=ALU.add)
                    last.then_inc(y_used, 1)

            dve.wait_ge(ld_c, 32)
            dve.wait_ge(ld_r, 32)
            v.tensor_copy(neg[:, :], neg_in).then_inc(negs, 1)
            v.tensor_copy(tri[:, :], K("tri"))
            v.tensor_copy(ones[:, :], K("ones"))
            prepared("L0")
            dve.wait_ge(ld_x, 16)
            wavefront(make, SEQ0)
            link(v.tensor_reduce(have[:, 0:nb], gb[:, 0:nb, :], AX.X, ALU.add))
            link(v.tensor_scalar(drop[:, :], have[:, 0:nb], -1.0, 1.0, ALU.mult, ALU.add))
            link(v.tensor_copy(wgt[:, 0:nb], have[:, 0:nb]))
            for c in range(nb):
                i = v.scalar_tensor_tensor(out=x[:, c, :], in0=xs[:, c, 0:D], scalar=drop[:, c:c + 1], in1=x[:, c, :],
                                           op0=ALU.mult, op1=ALU.add)
            link(i)
            dve.wait_ge(dq_mm, 1)
            link(v.tensor_scalar(dqT[:, :], ps[2][:, 0:SLOTS], V("Dbq"), None, ALU.add))
            v.tensor_tensor(qblk[:, :, :], bc(dqT[:, :], [P, SE, SLOTS], [1]), bc(K("CB_dim"), [P, SE, SLOTS], [2]),
                            ALU.mult).then_inc(qblk_ready, 1)
            dve.wait_ge(ld_s, 16 * (8 + 4 * B))
            v.tensor_scalar(madd_t[:, :, :], mask_tok[:, :, :], -1.0, BIG, ALU.add, ALU.mult)
            v.tensor_scalar(m2c[:, :], mask2c[:, :], -1.0, BIG, ALU.add, ALU.mult)
            v.tensor_scalar(m2r[:, :, :], mask2[:, :, :], -1.0, BIG, ALU.add, ALU.mult)
            v.tensor_scalar(m3c[:, :], mask3c[:, :], -1.0, 1e4, ALU.add, ALU.mult)
            v.tensor_scalar(m3r[:, :, :], mask3[:, :, :], -1.0, 1e4 / ATT["L3"]["scale"], ALU.add, ALU.mult)
            v.tensor_copy(one_r[:, :], K("ones")[0:1, :])
            for h in range(2):
                i = v.tensor_copy(rep2[:, h, :], ident[0:NK, 0:NK])
            i.then_inc(masks, 1)
            prepared("L1")
            prepared("L2")
            evacuate("m0", 0)
            dve.wait_ge(sent, 16 * nb)
            v.tensor_scalar(madd_k, mask_key[:, :], -1.0, BIG, ALU.add, ALU.mult).then_inc(masks, 1)
            wavefront(make, SEQ1)
            nr = B * SLOTS
            dve.wait_ge(do_mm, 1)
            link(v.tensor_tensor(orow[:, :], ps[0][0:nr, 0:D], ROW("Dob")[0:nr, :], ALU.add))
            link(v.tensor_tensor(orow[:, :], orow[:, :], sqrow[:, :], ALU.add))
            link(v.bn_stats(st[0:nr, 0, :], orow[:, :]))
            v.bn_aggr(mv[0:nr, 0, :], st[0:nr, 0, :]).then_inc(o_var, 1)
            dve.wait_ge(o_rstd, 1)
            link(v.tensor_scalar(hrow, orow[:, :], mv[0:nr, 0, 0:1], rstd[0:nr, 0:1], ALU.subtract, ALU.mult))
            link(v.tensor_tensor(hrow, hrow, lng[:, :], ALU.mult))
            v.tensor_tensor(hrow, hrow, lnb[:, :], ALU.add).then_inc(h_rows, 1)
            dve.wait_ge(hT_mm, 1)
            dve.wait_ge(hTm_zero, 1)
            for b in range(B):
                i = v.tensor_copy(hTm[:, SLOTS * b:nr * SE:nr + 1][:, 0:SE], ps[1][:, SLOTS * b:SLOTS * (b + 1)])
            i.then_inc(hT_ready, 1)
            dve.wait_ge(e_mm, 1)
            dve.wait_ge(ld_eb, 16 * 2 * B)
            v.tensor_tensor(uu, ps[3][0:nr, :], eb1, ALU.add).then_inc(e_h, 1)
            v.tensor_tensor(gg, ps[4][0:nr, :], ebg, ALU.add).then_inc(e_h, 1)
            dve.wait_ge(e_silu, 2)
            v.tensor_tensor(uu, eu, eg, ALU.mult).then_inc(e_act, 1)
            dve.wait_ge(uT_mm, 1)
            dve.wait_ge(uTm_zero, 1)
            for b in range(B):
                i = v.tensor_copy(uTm[:, :, SLOTS * b:nr * SE:nr + 1][:, :, 0:SE],
                                  ps[6][:, 0:4 * nr].rearrange("p (f n) -> p f n", f=4)[:, :, SLOTS * b:SLOTS * (b + 1)])
            i.then_inc(uT_ready, 1)
            dve.wait_ge(ey_use, SE)
            link(v.tensor_tensor(orow[:, :], orow[:, :], ps[5][0:nr, 0:D], ALU.add))
            v.tensor_tensor(orow[:, :], orow[:, :], eb2[:, :], ALU.add).then_inc(oT_rows, 1)
            dve.wait_ge(oT_mm, 1)
            v.tensor_copy(oT[:, :, :], ps[7][:, 0:nr].rearrange("p (b s) -> p b s", b=B)).then_inc(oT_ready, 1)
            prepared("CB")
            wavefront(make, SEQ2)
            second_largest()
            dve.wait_ge(gate_e, n["two"])
            first_largest(lg2[:, :, :], oh[:, nb:2 * nb, :], slice(0, nb))
            dve.wait_ge(oh_ready, 2 * B + 1)
            link(v.tensor_tensor(lg2[:, :, :], oh[:, 0:nb, :], oh[:, nb:2 * nb, :], ALU.add))
            dve.wait_ge(gate_ep, 1)
            dve.wait_ge(cum_mm, 2 * B + 1)
            v.tensor_copy(first_n[:, :], ps[2][:, 0:E])
            places(ps[2][:, E:(nb + 1) * E].rearrange("p (c e) -> p c e", e=E), slice(nb, 2 * nb), CAP2, "base2")
            link(v.tensor_tensor(lg2[:, :, :], lg2[:, :, :], ga[:, :, :], ALU.mult))
            link(v.tensor_reduce(gs[:, :], lg2[:, :, :], AX.X, ALU.add))
            link(v.reciprocal(gs[:, :], gs[:, :]))
            link(v.tensor_tensor(lg2[:, :, :], lg2[:, :, :], bc(gs[:, :], [P, nb, E], [2]), ALU.mult))
            for k in range(2):
                kk = slice(nb * k, nb * (k + 1))
                link(v.tensor_tensor(gb[:, kk, :], gb[:, kk, :], lg2[:, :, :], ALU.mult))
            link(v.tensor_reduce(wgt[:, :], gb[:, :, :], AX.X, ALU.add))
            prepared("L3")
            evacuate("m2", 1)
            v.tensor_tensor(b2_blocks, bc(b2m3[:, :], [P, C, D], [1]), bc(K("chunk"), [P, C, D], [2]), ALU.mult)
            wavefront(make, SEQ3)
            first_largest(lg[:, :, :], oh[:, 0:nb, :], slice(0, nb))
            dve.wait_ge(oh_ready, 2 * B + 2)
            second_largest()
            dve.wait_ge(gate_e, n["two"])
            first_largest(lg2[:, :, :], oh[:, nb:2 * nb, :], slice(0, nb))
            dve.wait_ge(oh_ready, 2 * B + 3)
            link(v.tensor_tensor(lg2[:, :, :], oh[:, 0:nb, :], oh[:, nb:2 * nb, :], ALU.add))
            dve.wait_ge(gate_ep, 2)
            link(v.tensor_reduce(gs[:, :], ga[:, :, :], AX.X, ALU.add))
            link(v.reciprocal(gs[:, :], gs[:, :]))
            link(v.tensor_tensor(ga[:, :, :], ga[:, :, :], bc(gs[:, :], [P, nb, E], [2]), ALU.mult))
            link(v.tensor_tensor(lg2[:, :, :], lg2[:, :, :], ga[:, :, :], ALU.mult))
            link(v.tensor_reduce(gs[:, :], lg2[:, :, :], AX.X, ALU.add))
            link(v.tensor_scalar(gs[:, :], gs[:, :], 1e-9, None, ALU.add))
            link(v.reciprocal(gs[:, :], gs[:, :]))
            v.tensor_tensor(gate[:, :, :], lg2[:, :, :], bc(gs[:, :], [P, nb, E], [2]), ALU.mult).then_inc(gate_ready, 1)
            dve.wait_ge(gate_ready, 1)
            add_bias_rows()
            experts()

        @block.gpsimd
        def _(pool):
            g_ = nc.gpsimd
            heads_in = keys_in.rearrange("p (b k) -> p b k", b=B)
            n = dict(norm=0, chain=0, turn=0, scale=0)

            def link(i):
                n["chain"] += 1
                i.then_inc(pool_chain, 1)
                pool.wait_ge(pool_chain, n["chain"])

            def rstd_of(rows, t, width, done):
                tt = slice(C * t, C * t + width)
                link(g_.tensor_scalar(rstd[0:rows, tt], mv[0:rows, tt, 1], EPS, None, ALU.add))
                g_.tensor_tensor(rstd[0:rows, tt], rstd[0:rows, tt], half[0:rows, 0:width], ALU.pow).then_inc(done, 1)

            def stats(added, dst):
                n["norm"] += 1
                k = n["norm"]

                def stage(t):
                    pool.wait_ge(var_ready[t], k)
                    tt = slice(C * t, C * t + C)
                    g_.tensor_scalar(negmean[:, tt], mv[:, tt, 0], -1.0, None, ALU.mult)
                    rstd_of(P, t, C, rstd_ready[t])
                    pool.wait_ge(rstd_ready[t], k)
                    g_.tensor_tensor(negmean[:, tt], negmean[:, tt], rstd[:, tt], ALU.mult).then_inc(nm_ready, 1)
                return stage

            def turn(src, width, affine, fold):
                k = n["turn"]
                n["turn"] += 1
                normed = n["scale"] - 1
                if not fold:
                    return None

                def stage(t):
                    pool.wait_ge(tok_ready, 4 * k + t + 1)
                    pool.wait_ge(tok_act, 4 * normed + t + 1)
                    tt = slice(C * t, C * t + C)
                    over = lambda ap: bc(ap, [P, C, D], [1])
                    if fold == "so":
                        i = g_.tensor_tensor(r[:, tt, :], xn[:, tt, :], over(ROW("so_b")), ALU.add)
                    elif fold in ("mo", "l2"):
                        link(g_.tensor_tensor(r[:, tt, :], xn[:, tt, :], over(ROW("g" + affine)), ALU.mult))
                        i = g_.tensor_tensor(r[:, tt, :], r[:, tt, :], over(ROW("b" + affine)), ALU.add)
                    else:
                        i = g_.tensor_tensor(x[:, tt, :], x[:, tt, :], over(ROW(fold + "ob")), ALU.add)
                    i.then_inc(res_ready, 1)
                return stage

            def scale(where):
                n["scale"] += 1

            def gain():
                k = n["scale"] - 1

                def stage(t):
                    pool.wait_ge(x3_dve, t + 1)
                    pool.wait_ge(tok_act, 4 * k + t + 1)
                    tt = slice(C * t, C * t + C)
                    g_.tensor_tensor(xn[:, tt, :], xn[:, tt, :], bc(ROW("g3"), [P, C, D], [1]), ALU.mult).then_inc(x3_gain, 1)
                return stage

            def up(f):
                if f != 1:
                    return None

                def stage(t):
                    tt = slice(C * t, C * t + C)
                    g_.tensor_tensor(x[:, tt, :], x[:, tt, :], bc(ROW("b3"), [P, C, D], [1]), ALU.add).then_inc(b3_in, 1)
                return stage

            def maxima(name):
                if name not in ("CB", "L3"):
                    return None
                mix, w, width, loaded = ("m2", moe_w, 512, ld_m2) if name == "CB" else ("m3", w3, 256, ld_m3)

                def stage(t):
                    if t == 0:
                        pool.wait_ge(loaded, 32 * E)
                    for e in (2 * t, 2 * t + 1):
                        link(g_.tensor_copy(w1_high[mix][:, e, :], w[:, e, 0:width]))
                        g_.tensor_tensor(w1_low[mix][:, e, :], w[:, e, 0:width], w1_high[mix][:, e, :].bitcast(F32),
                                         ALU.subtract).then_inc(split, 1)
                return stage

            def router(name):
                if name != "wr3":
                    return None

                def stage(t):
                    pool.wait_ge(x_high, t + 1)
                    g_.tensor_tensor(xnR[:, t, :], xT[:, t, :], qTR[:, t, :].bitcast(F32), ALU.subtract).then_inc(x_low, 1)
                return stage

            def send(name, j):
                g_.indirect_dma_start(out=tok_d[name], out_offset=bass.IndirectOffsetOnAxis(ap=to_slot[:, j:j + 1], axis=0),
                                      in_=xs[:, j % (B * C), :], in_offset=None, bounds_check=E * PLACED[name]["cap"] - 1,
                                      oob_is_err=False).then_inc(sent, 16)

            def place(name):
                k = 0 if name == "m0" else 1

                def stage(t):
                    if t == 0:
                        pool.wait_ge(cleared, 64)
                    pool.wait_ge(idx_ready, 4 * k + t + 1)
                    for c in range(C * t, C * t + C):
                        send(name, c)
                return stage

            def repeat(name, keys):
                a = ATT[name]
                k = KV[name]
                if k >= 1:
                    pool.wait_ge(v_mm, k)
                g_.tensor_copy(rep[:, :, 0:a["RB"]].rearrange("p b (h k) -> p b h k", h=a["hb"]),
                               bc(keys, [P, B, a["hb"], a["nk"]], [2])).then_inc(kv_rep, 1)

            def keys_by_heads(name):
                a = ATT[name]
                k = KV[name]
                PD, H, nk = (a[i] for i in ("PD", "H", "nk"))
                pool.wait_ge(k_sb, k + 1)
                for b in range(B):
                    i = g_.tensor_tensor(KB[name][0:PD, b, :].rearrange("p (h k) -> p h k", h=H),
                                     bc(kts[0:PD, b * nk:(b + 1) * nk], [PD, H, nk], [1]),
                                     bc(K(name + "_dim")[0:PD, :], [PD, H, nk], [2]), ALU.mult)
                i.then_inc(kb_ready, 1)

            def values_by_heads(name):
                a = ATT[name]
                k = KV[name]
                PD, H, RB, G, dh = (a[i] for i in ("PD", "H", "RB", "G", "dh"))
                pool.wait_ge(v_sb, k + 1)
                sel = K(name + "_sel")[0:RB, :].rearrange("p (g h) -> p g h", g=G)
                for b in range(B):
                    for g in range(G):
                        g_.tensor_tensor(VB[name][0:RB, b, g, 0:PD].rearrange("p (h d) -> p h d", h=H),
                                         vr[0:RB, b, 0:PD].rearrange("p (h d) -> p h d", h=H),
                                         bc(sel[:, g, :], [RB, H, dh], [2]), ALU.mult)
                i = g_.tensor_copy(VB[name][0:RB, :, :, PD:PD + H], bc(sel, [RB, B, G, H], [1]))
                i.then_inc(kv_ready, 1)

            def by_heads(name):
                keys_by_heads(name)
                values_by_heads(name)

            def prob(name, g):
                def stage(t):
                    if t == 0:
                        values_by_heads("L0")
                        repeat("L1", heads_in)
                return stage if name == "L0" and g == 0 else None

            make = dict(prob=prob, gain=gain, place=place, stats=stats, scale=scale, turn=turn, up=up, maxima=maxima, router=router)

            def deliver(name, seen):
                a = PLACED[name]
                for e in range(E):
                    pool.wait_ge(gy_sb, seen * E + e + 1)
                    for b in range(a["nb"]):
                        at = (40 if seen else 0) + e * a["nb"] + b
                        g_.indirect_dma_start(out=res_d[name], out_offset=bass.IndirectOffsetOnAxis(ap=dest[:, at:at + 1], axis=0),
                                              in_=ysb[:, e % 2, cols(b)], in_offset=None, bounds_check=a["ranks"] * B * S - 1,
                                              oob_is_err=False).then_inc(gy_st[e % 2], 16)

            g_.memset(zero[:, 0:D], 0.0)
            g_.memset(zero[:, D:D + 1], SKIP).then_inc(zeroed, 1)
            g_.memset(half[:, :], -0.5).then_inc(minus_half, 1)
            pool.wait_ge(minus_half, 1)
            pool.wait_ge(ld_c, 32)
            repeat("L0", heads_in)
            pool.wait_ge(ld_r, 32)
            g_.tensor_tensor(ROW("b1"), ROW("b1"), ROW("mo_b"), ALU.add)
            link(g_.tensor_tensor(ROW("b2"), ROW("b2"), ROW("l2_b"), ALU.add))
            keys_by_heads("L0")
            wavefront(make, SEQ0)
            by_heads("L1")
            repeat("L2", heads_in)
            by_heads("L2")
            deliver("m0", 0)
            wavefront(make, SEQ1)
            pool.wait_ge(turned, 4 * TURNS_TO_SLOTS)
            g_.memset(hTm[:, :], 0.0).then_inc(hTm_zero, 1)
            pool.wait_ge(o_var, 1)
            rstd_of(B * SLOTS, 0, 1, o_rstd)
            pool.wait_ge(att_ready, B)
            g_.memset(uTm[:, :, :], 0.0).then_inc(uTm_zero, 1)
            pool.wait_ge(oT_ready, 1)
            repeat("CB", oT[:, :, :])
            by_heads("CB")
            repeat("L3", heads_in)
            wavefront(make, SEQ2)
            pool.wait_ge(idx_ready, 2 * B + 1)
            for j in range(B * C, 2 * B * C):
                send("m2", j)
            pool.wait_ge(sent, 16 * 3 * B * C)
            by_heads("L3")
            deliver("m2", 1)
            wavefront(make, SEQ3)


def kernel(**inputs):
    import concourse.bacc as _bacc
    from concourse.bass_utils import run_bass_kernel_spmd as _run

    i = {k: np.asarray(v) for k, v in inputs.items()}
    T = lambda a: a.T
    rows_of = lambda a: np.concatenate([a[j * P:(j + 1) * P] for j in range(a.shape[0] // P)], axis=1)
    qkv, inp = i["L0_xattn_qkv_w"], i["L0_xattn_in_proj_w"]
    wkv = i["L1_xattn_Wkv"]
    squares = {
        "L0v": T(qkv[256:384]), "L0so": T(i["L0_xattn_sa_out_w"]), "L0q": T(inp[0:128]), "L0k": T(inp[128:256]),
        "L0mv": T(inp[256:384]), "L0o": T(i["L0_xattn_mha_out_w"]), "L0l1": T(i["L0_xattn_lin1_w"]),
        "L0l2": rows_of(T(i["L0_xattn_lin2_w"])),
        "L1q": i["L1_xattn_Wq"], "L1k": wkv[:, 0:128], "L1v": wkv[:, 128:256], "L1o": i["L1_xattn_Wo"],
        "L2q": T(i["L2_xattn_Wq"]), "L2k": T(i["L2_xattn_Wk"]), "L2v": T(i["L2_xattn_Wv"]),
        "L3q": T(i["L3_xattn_wq"]), "L3k": T(i["L3_xattn_wk"]), "L3v": T(i["L3_xattn_wv"]), "L3o": T(i["L3_xattn_wo"]),
        "Dq": i["L1_ffn_d_Wq"], "Dk": i["L1_ffn_d_Wk"], "Dv": i["L1_ffn_d_Wv"], "Do": i["L1_ffn_d_Wo"],
        "CBq": i["L1_ffn_c_Wq"], "CBk": i["L1_ffn_c_Wk"], "CBv": i["L1_ffn_c_Wv"], "CBo": i["L1_ffn_c_Wo"],
        "wr0": i["L0_ffn_w_switch"], "wr2": i["L2_ffn_w_g"], "wr3": T(i["L3_ffn_router_w"]),
    }
    on_p = lambda a: a.reshape(-1, P).T
    ib = i["L0_xattn_in_proj_b"]
    columns = {
        "L0bv": on_p(i["L0_xattn_qkv_b"][256:384]), "L0bq": on_p(ib[0:128]), "L0bk": on_p(ib[128:256]),
        "L0bl1": on_p(i["L0_xattn_lin1_b"]), "L3bq": on_p(i["L3_xattn_bq"]), "L3bk": on_p(i["L3_xattn_bk"]),
        "Dbq": on_p(i["L1_ffn_d_bq"]), "Dbk": on_p(i["L1_ffn_d_bk"]), "Dbv": on_p(i["L1_ffn_d_bv"]),
        "CBbq": on_p(i["L1_ffn_c_bq"]), "CBbk": on_p(i["L1_ffn_c_bk"]),
        "m0b1": on_p(i["L0_ffn_b1"]), "m3b1": on_p(i["L3_ffn_b1"]),
        "g1": on_p(i["L0_xattn_ln1_g"]), "b1": on_p(i["L0_xattn_ln1_b"]),
        "g2": on_p(i["L0_xattn_ln2_g"]), "b2": on_p(i["L0_xattn_ln2_b"]),
        "sqT": T(i["L1_ffn_slot_query"][0]), "ctxT": T(i["ctx_1024"].reshape(B * NK, D)),
    }
    rows = {
        "so_b": i["L0_xattn_sa_out_b"], "g1": i["L0_xattn_ln1_g"], "b1": i["L0_xattn_ln1_b"],
        "mo_b": i["L0_xattn_mha_out_b"], "g2": i["L0_xattn_ln2_g"], "b2": i["L0_xattn_ln2_b"],
        "l2_b": i["L0_xattn_lin2_b"], "g3": i["L0_xattn_ln3_g"], "b3": i["L0_xattn_ln3_b"],
        "L0mvb": ib[256:384], "L3vb": i["L3_xattn_bv"], "L3ob": i["L3_xattn_bo"],
        "CBvb": i["L1_ffn_c_bv"], "CBob": i["L1_ffn_c_bo"], "Dob": i["L1_ffn_d_bo"], "sw_b": i["L0_ffn_b_switch"],
    }
    bits = lambda a: a.view(np.uint8)
    m3 = i["mask_BxS2_ff1"]
    given = {
        "x": i["x"], "con": constants(), "neg": head_signs(),
        "sq": np.concatenate([squares[k] for k, _ in SQUARES], axis=1), "wout2": T(i["L2_xattn_Wout"]),
        "col": np.concatenate([columns[k] for k, _ in COLUMNS], axis=1),
        "row": np.concatenate([rows[k] for k, _ in ROWS])[None, :],
        "mask": bits(i["mask_BxSxS2_bf1"]),
        "maskT": bits(np.ascontiguousarray(i["mask_BxSxS2_bf1"].transpose(2, 0, 1).reshape(NK, B * S))),
        "mask2": bits(i["mask_BxS2_bf1"].reshape(1, B * NK)), "mask2c": bits(np.ascontiguousarray(i["mask_BxS2_bf1"].T)),
        "mask3": m3.reshape(1, B * NK), "mask3c": np.concatenate([m3.T] * 4, axis=0),
        "m0b2": i["L0_ffn_b2"], "m3b2": np.concatenate([i["L3_ffn_b2"]] * (B * C), axis=0),
        "eb1": i["L1_ffn_e_b1"], "ebg": i["L1_ffn_e_bg"], "eb2": i["L1_ffn_e_b2"],
        "sqrow": i["L1_ffn_slot_query"][0], "lng": i["L1_ffn_e_ln_g"], "lnb": i["L1_ffn_e_ln_b"],
        "m0w1": i["L0_ffn_w1"], "m0w2": i["L0_ffn_w2"], "m2w1": i["L2_ffn_c_fc"], "m2w2": i["L2_ffn_c_proj"],
        "m3w1": i["L3_ffn_w1"], "m3w2": i["L3_ffn_w2"],
        "ew1": i["L1_ffn_e_W1"], "ewg": i["L1_ffn_e_Wg"], "ew2": i["L1_ffn_e_W2"],
    }
    nc = _bacc.Bacc("TRN2", target_bir_lowering=False, num_devices=1)
    arrays, ins = {}, {}
    for name, a in given.items():
        a = np.ascontiguousarray(a)
        arrays[f"in_{name}"] = a
        ins[name] = nc.dram_tensor(f"in_{name}", a.shape, mybir.dt.from_np(a.dtype), kind="ExternalInput").ap()
    out = nc.dram_tensor("out_x", (B, S, D), F32, kind="ExternalOutput").ap()
    build(nc, ins, out)
    got = _run(nc, [arrays], core_ids=[0])
    return got.results[0]["out_x"]
```
